# Optimizing a Trainium2 kernel written in Bass

```python
import numpy as np
import jax
import jax.numpy as jnp

def _softmax(x, axis=-1):
    return jax.nn.softmax(x, axis=axis)

def _gelu(x):
    return jax.nn.gelu(x, approximate=True)

def _silu(x):
    return jax.nn.silu(x)

def _sigmoid(x):
    return jax.nn.sigmoid(x)

def _layernorm(x, axis=-1, eps=1e-05):
    m = jnp.mean(x, axis=axis, keepdims=True)
    v = jnp.var(x, axis=axis, keepdims=True)
    return (x - m) / jnp.sqrt(v + eps)

def _scatter_add(tgt, idx, src, axis=0):
    return tgt.at[idx].add(src)

def _segment_sum(src, seg, n):
    return jax.ops.segment_sum(src, seg, n)
kernel_name = 'mk_cond_seq_d4_seqx_r4_4bb0a9'

def setup_inputs(seed: int=0):
    np.random.seed(seed)
    _w = jnp.asarray

    def _rec_inputs():
        import jax
        import jax.numpy as jnp
        _rk = jax.random.key(seed)
        x = -0.0003929 + 0.9999 * jax.random.normal(jax.random.fold_in(_rk, 1), (128, 64, 256), jnp.float32)
        _lenS = 64 - jax.random.randint(jax.random.fold_in(_rk, 7), (128,), 0, max(1, 64 // 4) + 1, jnp.int32)
        _lenS2 = 64 - jax.random.randint(jax.random.fold_in(_rk, 8), (128,), 0, max(1, 64 // 4) + 1, jnp.int32)
        cond_1024 = 0.00782532 + 1.00527 * jax.random.normal(jax.random.fold_in(_rk, 11), (128, 256), jnp.float32)
        _validS = jnp.arange(64)[None, :] < _lenS[:, None]
        _validS2 = jnp.arange(64)[None, :] < _lenS2[:, None]
        _causal = jnp.tril(jnp.ones((64, 64), dtype=bool))
        mask_BxSxSx11_ik0 = jnp.where(jnp.ones((128, 64, 64, 11), dtype=bool), 0, 1).astype(jnp.int32)
        return (x, cond_1024, mask_BxSxSx11_ik0)
    x, cond_1024, mask_BxSxSx11_ik0 = _rec_inputs()

    def _L0_cond_setup():
        import jax, jax.numpy as jnp
        import numpy as np
        B, L, D, P = (8, 512, 256, 64)

        def _ln(x):
            m = x.mean(-1, keepdims=True)
            v = x.var(-1, keepdims=True)
            return (x - m) * jax.lax.rsqrt(v + 1e-05)

        def _s5(u, Lam_re, Lam_im, B_re, B_im, C_re, C_im, D_diag, log_step):
            Lam = Lam_re + 1j * Lam_im
            dt = jnp.exp(log_step)
            Lam_bar = jnp.exp(Lam * dt)
            Bc = B_re + 1j * B_im
            B_bar = ((Lam_bar - 1.0) / Lam)[:, None] * Bc
            Bu = jnp.einsum('bld,pd->blp', u.astype(B_bar.dtype), B_bar)
            A = jnp.broadcast_to(Lam_bar, Bu.shape)

            def binop(e1, e2):
                a1, b1 = e1
                a2, b2 = e2
                return (a1 * a2, a2 * b1 + b2)
            _, xs = jax.lax.associative_scan(binop, (A, Bu), axis=1)
            Cc = C_re + 1j * C_im
            return 2.0 * jnp.einsum('blp,dp->bld', xs, Cc).real + D_diag * u
        key = jax.random.key(seed)
        ks = jax.random.split(key, 16)
        inp = {'y': jax.random.normal(ks[0], (B, L, D), jnp.float32), 't': jax.random.normal(ks[1], (B, D), jnp.float32), 'Wm': jax.random.normal(ks[2], (D, 6 * D), jnp.float32) * 0.02, 'bm': jax.random.normal(ks[3], (6 * D,), jnp.float32) * 0.02, 'Lam_re': -0.5 * jnp.ones((P,), jnp.float32), 'Lam_im': jnp.pi * jnp.arange(P, dtype=jnp.float32), 'B_re': jax.random.normal(ks[4], (P, D), jnp.float32) / np.sqrt(D), 'B_im': jax.random.normal(ks[5], (P, D), jnp.float32) / np.sqrt(D), 'C_re': jax.random.normal(ks[6], (D, P), jnp.float32) / np.sqrt(P), 'C_im': jax.random.normal(ks[7], (D, P), jnp.float32) / np.sqrt(P), 'D_diag': jax.random.normal(ks[8], (D,), jnp.float32), 'log_step': jax.random.uniform(ks[9], (P,), jnp.float32, np.log(0.001), np.log(0.1)), 'Wc': jax.random.normal(ks[10], (D, 2 * D), jnp.float32) * 0.02, 'bc': jax.random.normal(ks[11], (2 * D,), jnp.float32) * 0.02, 'W1': jax.random.normal(ks[12], (D, 4 * D), jnp.float32) / np.sqrt(D), 'b1': jnp.zeros((4 * D,), jnp.float32), 'W2': jax.random.normal(ks[13], (4 * D, D), jnp.float32) / np.sqrt(4 * D) * 0.1, 'b2': jnp.zeros((D,), jnp.float32)}
        return inp
    _L0_cond_all = _L0_cond_setup()
    _L0_cond_in = {k: v for k, v in _L0_cond_all.items() if k in ('Wm', 'bm', 'Lam_re', 'Lam_im', 'B_re', 'B_im', 'C_re', 'C_im', 'D_diag', 'log_step', 'Wc', 'bc', 'W1', 'b1', 'W2', 'b2')}
    del _L0_cond_all

    def _L1_cond_setup():
        import jax, jax.numpy as jnp
        import numpy as np
        DIM = 256
        MLP_RATIO = 4
        EPS = 1e-06

        def rmsnorm(x, w):
            return x * jax.lax.rsqrt(jnp.mean(x * x, axis=-1, keepdims=True) + EPS) * w

        def film(x, cond, w, b):
            ss = cond @ w + b
            scale, shift = jnp.split(ss, 2, axis=-1)
            return x * (1.0 + scale[:, None, :]) + shift[:, None, :]
        key = jax.random.key(seed)
        ks = jax.random.split(key, 16)
        B, N, D = (4, 512, DIM)
        H = D * MLP_RATIO
        s = lambda fan_in: 1.0 / np.sqrt(fan_in)
        return {'x': jax.random.normal(ks[0], (B, N, D), jnp.float32), 'cond': jax.random.normal(ks[1], (B, D), jnp.float32), 'norm1_w': jnp.ones((D,), jnp.float32), 'film1_w': jax.random.normal(ks[2], (D, 2 * D), jnp.float32) * s(D), 'film1_b': jnp.zeros((2 * D,), jnp.float32), 'q_w': jax.random.normal(ks[3], (D, D), jnp.float32) * s(D), 'q_b': jnp.zeros((D,), jnp.float32), 'k_w': jax.random.normal(ks[4], (D, D), jnp.float32) * s(D), 'k_b': jnp.zeros((D,), jnp.float32), 'v_w': jax.random.normal(ks[5], (D, D), jnp.float32) * s(D), 'v_b': jnp.zeros((D,), jnp.float32), 'proj_w': jax.random.normal(ks[6], (D, D), jnp.float32) * s(D), 'proj_b': jnp.zeros((D,), jnp.float32), 'norm2_w': jnp.ones((D,), jnp.float32), 'film2_w': jax.random.normal(ks[7], (D, 2 * D), jnp.float32) * s(D), 'film2_b': jnp.zeros((2 * D,), jnp.float32), 'mlp_w1': jax.random.normal(ks[8], (D, H), jnp.float32) * s(D), 'mlp_b1': jnp.zeros((H,), jnp.float32), 'mlp_w2': jax.random.normal(ks[9], (H, D), jnp.float32) * s(H), 'mlp_b2': jnp.zeros((D,), jnp.float32)}
    _L1_cond_all = _L1_cond_setup()
    _L1_cond_in = {k: v for k, v in _L1_cond_all.items() if k in ('norm1_w', 'film1_w', 'film1_b', 'q_w', 'q_b', 'k_w', 'k_b', 'v_w', 'v_b', 'proj_w', 'proj_b', 'norm2_w', 'film2_w', 'film2_b', 'mlp_w1', 'mlp_b1', 'mlp_w2', 'mlp_b2')}
    del _L1_cond_all

    def _L2_cond_setup():
        import jax, jax.numpy as jnp
        import numpy as np
        NONGT = 20
        H = 16
        NEG = -9000000000000000.0

        def _gat_attention(self_feat, cond_adj, label_bias, Wq, bq, Wk, bk, Wout, bout):
            B, N, F = self_feat.shape
            ng = min(NONGT, N)
            dh = F // H
            kv = self_feat[:, :ng]
            qh = (self_feat @ Wq.T + bq).reshape(B, N, H, dh)
            kh = (kv @ Wk.T + bk).reshape(B, ng, H, dh)
            aff = jnp.einsum('bnhd,bmhd->bnhm', qh, kh) * (1.0 / np.sqrt(dh))
            mask = cond_adj[:, :, None, :] > 0
            aff = jnp.where(mask, aff, NEG) + label_bias[:, :, None, :]
            w = jax.nn.softmax(aff, axis=-1)
            out_t = jnp.einsum('bnhm,bmf->bnhf', w, kv)
            out = jnp.einsum('bnhf,hgf->bnhg', out_t, Wout) + bout.reshape(H, F // H)
            return out.reshape(B, N, F)

        def _forward(v, q, adj, W_self, b_self, w_bias, b_bias, Wq, bq, Wk, bk, Wout, bout):
            adj_f = adj.astype(jnp.float32)
            exp_v = v
            row_zero = exp_v.sum(-1) == 0
            q_exp = jnp.where(row_zero[..., None], 0.0, q[:, None, :])
            vcq = jnp.concatenate([exp_v, q_exp], axis=-1)
            self_feat = vcq @ W_self.T + b_self
            output = self_feat
            for d in range(2):
                A = adj_f if d == 0 else jnp.swapaxes(adj_f, 1, 2)
                A = A[:, :, :NONGT, :]
                cond = A.sum(-1)
                vb = A @ w_bias + b_bias
                output = output + _gat_attention(self_feat, cond, vb, Wq[d], bq[d], Wk[d], bk[d], Wout[d], bout[d])
            rel = jax.nn.relu(output)
            return exp_v + rel
        key = jax.random.key(seed)
        ks = jax.random.split(key, 8)
        B, N, L, F, Q = (64, 36, 11, 256, 256)
        IN = F + Q
        s = 0.02
        return {'v': jax.random.normal(ks[0], (B, N, F), jnp.float32), 'q': jax.random.normal(ks[1], (B, Q), jnp.float32), 'adj': jax.random.randint(ks[2], (B, N, N, L), 0, 2, jnp.int32), 'W_self': jax.random.normal(ks[3], (F, IN), jnp.float32) * s, 'b_self': jnp.zeros((F,), jnp.float32), 'w_bias': jax.random.normal(ks[4], (L,), jnp.float32) * s, 'b_bias': jnp.zeros((), jnp.float32), 'Wq': jax.random.normal(ks[5], (2, F, F), jnp.float32) * s, 'bq': jnp.zeros((2, F), jnp.float32), 'Wk': jax.random.normal(ks[6], (2, F, F), jnp.float32) * s, 'bk': jnp.zeros((2, F), jnp.float32), 'Wout': jax.random.normal(ks[7], (2, H, F // H, F), jnp.float32) * s, 'bout': jnp.zeros((2, F), jnp.float32)}
    _L2_cond_all = _L2_cond_setup()
    _L2_cond_in = {k: v for k, v in _L2_cond_all.items() if k in ('W_self', 'b_self', 'w_bias', 'b_bias', 'Wq', 'bq', 'Wk', 'bk', 'Wout', 'bout')}
    del _L2_cond_all

    def _L3_cond_setup():
        import jax, jax.numpy as jnp
        import numpy as np
        EPS = float(np.finfo(np.float32).eps)

        def _rmsnorm(x, g):
            return x * jax.lax.rsqrt(jnp.mean(x * x, axis=-1, keepdims=True) + EPS) * g

        def _silu(x):
            return x * jax.nn.sigmoid(x)

        def _swiglu(x):
            a, gate = jnp.split(x, 2, axis=-1)
            return a * _silu(gate)

        def _rope(x):
            T, hd = (x.shape[1], x.shape[-1])
            inv_freq = 1.0 / 10000.0 ** (jnp.arange(0, hd, 2, dtype=jnp.float32) / hd)
            ang = jnp.arange(T, dtype=jnp.float32)[:, None] * inv_freq[None, :]
            cos = jnp.cos(ang)[None, :, None, :]
            sin = jnp.sin(ang)[None, :, None, :]
            x0, x1 = (x[..., 0::2], x[..., 1::2])
            o0 = x0 * cos - x1 * sin
            o1 = x1 * cos + x0 * sin
            return jnp.stack([o0, o1], axis=-1).reshape(x.shape)

        def _mha(x, w_qkv, b_qkv, w_ao, b_ao, n_head):
            B, T, C = x.shape
            hd = C // n_head
            qkv = x @ w_qkv + b_qkv
            q, k, v = jnp.split(qkv, 3, axis=-1)
            q = _rope(q.reshape(B, T, n_head, hd)).transpose(0, 2, 1, 3)
            k = _rope(k.reshape(B, T, n_head, hd)).transpose(0, 2, 1, 3)
            v = v.reshape(B, T, n_head, hd).transpose(0, 2, 1, 3)
            attn = jnp.einsum('bhqd,bhkd->bhqk', q, k) * (1.0 / np.sqrt(hd))
            attn = jax.nn.softmax(attn, axis=-1)
            out = jnp.einsum('bhqk,bhkd->bhqd', attn, v)
            out = out.transpose(0, 2, 1, 3).reshape(B, T, C)
            return out @ w_ao + b_ao

        def _ffn(x, w_fc, b_fc, w_fo, b_fo):
            return _swiglu(x @ w_fc + b_fc) @ w_fo + b_fo
        key = jax.random.key(seed)
        ks = jax.random.split(key, 10)
        B, T, D, H = (2, 512, 256, 16)
        s = 0.02
        return {'x': jax.random.normal(ks[0], (B, T, D), jnp.float32), 'time_emb': jax.random.normal(ks[1], (B, D), jnp.float32), 'g1': jnp.ones((D,), jnp.float32), 'g2': jnp.ones((D,), jnp.float32), 'w_qkv': jax.random.normal(ks[2], (D, 3 * D), jnp.float32) * s, 'b_qkv': jnp.zeros((3 * D,), jnp.float32), 'w_ao': jax.random.normal(ks[3], (D, D), jnp.float32) * s, 'b_ao': jnp.zeros((D,), jnp.float32), 'w_fc': jax.random.normal(ks[4], (D, 8 * D), jnp.float32) * s, 'b_fc': jnp.zeros((8 * D,), jnp.float32), 'w_fo': jax.random.normal(ks[5], (4 * D, D), jnp.float32) * s, 'b_fo': jnp.zeros((D,), jnp.float32), 'w_t1': jax.random.normal(ks[6], (D, 2 * D), jnp.float32) * s, 'b_t1': jnp.zeros((2 * D,), jnp.float32), 'w_t2': jax.random.normal(ks[7], (D, 4 * D), jnp.float32) * s, 'b_t2': jnp.zeros((4 * D,), jnp.float32)}
    _L3_cond_all = _L3_cond_setup()
    _L3_cond_in = {k: v for k, v in _L3_cond_all.items() if k in ('g1', 'g2', 'w_qkv', 'b_qkv', 'w_ao', 'b_ao', 'w_fc', 'b_fc', 'w_fo', 'b_fo', 'w_t1', 'b_t1', 'w_t2', 'b_t2')}
    del _L3_cond_all
    return {'x': x, 'cond_1024': cond_1024, 'mask_BxSxSx11_ik0': mask_BxSxSx11_ik0, 'L0_cond_Wm': _L0_cond_in['Wm'], 'L0_cond_bm': _L0_cond_in['bm'], 'L0_cond_Lam_re': _L0_cond_in['Lam_re'], 'L0_cond_Lam_im': _L0_cond_in['Lam_im'], 'L0_cond_B_re': _L0_cond_in['B_re'], 'L0_cond_B_im': _L0_cond_in['B_im'], 'L0_cond_C_re': _L0_cond_in['C_re'], 'L0_cond_C_im': _L0_cond_in['C_im'], 'L0_cond_D_diag': _L0_cond_in['D_diag'], 'L0_cond_log_step': _L0_cond_in['log_step'], 'L0_cond_Wc': _L0_cond_in['Wc'], 'L0_cond_bc': _L0_cond_in['bc'], 'L0_cond_W1': _L0_cond_in['W1'], 'L0_cond_b1': _L0_cond_in['b1'], 'L0_cond_W2': _L0_cond_in['W2'], 'L0_cond_b2': _L0_cond_in['b2'], 'L1_cond_norm1_w': _L1_cond_in['norm1_w'], 'L1_cond_film1_w': _L1_cond_in['film1_w'], 'L1_cond_film1_b': _L1_cond_in['film1_b'], 'L1_cond_q_w': _L1_cond_in['q_w'], 'L1_cond_q_b': _L1_cond_in['q_b'], 'L1_cond_k_w': _L1_cond_in['k_w'], 'L1_cond_k_b': _L1_cond_in['k_b'], 'L1_cond_v_w': _L1_cond_in['v_w'], 'L1_cond_v_b': _L1_cond_in['v_b'], 'L1_cond_proj_w': _L1_cond_in['proj_w'], 'L1_cond_proj_b': _L1_cond_in['proj_b'], 'L1_cond_norm2_w': _L1_cond_in['norm2_w'], 'L1_cond_film2_w': _L1_cond_in['film2_w'], 'L1_cond_film2_b': _L1_cond_in['film2_b'], 'L1_cond_mlp_w1': _L1_cond_in['mlp_w1'], 'L1_cond_mlp_b1': _L1_cond_in['mlp_b1'], 'L1_cond_mlp_w2': _L1_cond_in['mlp_w2'], 'L1_cond_mlp_b2': _L1_cond_in['mlp_b2'], 'L2_cond_W_self': _L2_cond_in['W_self'], 'L2_cond_b_self': _L2_cond_in['b_self'], 'L2_cond_w_bias': _L2_cond_in['w_bias'], 'L2_cond_b_bias': _L2_cond_in['b_bias'], 'L2_cond_Wq': _L2_cond_in['Wq'], 'L2_cond_bq': _L2_cond_in['bq'], 'L2_cond_Wk': _L2_cond_in['Wk'], 'L2_cond_bk': _L2_cond_in['bk'], 'L2_cond_Wout': _L2_cond_in['Wout'], 'L2_cond_bout': _L2_cond_in['bout'], 'L3_cond_g1': _L3_cond_in['g1'], 'L3_cond_g2': _L3_cond_in['g2'], 'L3_cond_w_qkv': _L3_cond_in['w_qkv'], 'L3_cond_b_qkv': _L3_cond_in['b_qkv'], 'L3_cond_w_ao': _L3_cond_in['w_ao'], 'L3_cond_b_ao': _L3_cond_in['b_ao'], 'L3_cond_w_fc': _L3_cond_in['w_fc'], 'L3_cond_b_fc': _L3_cond_in['b_fc'], 'L3_cond_w_fo': _L3_cond_in['w_fo'], 'L3_cond_b_fo': _L3_cond_in['b_fo'], 'L3_cond_w_t1': _L3_cond_in['w_t1'], 'L3_cond_b_t1': _L3_cond_in['b_t1'], 'L3_cond_w_t2': _L3_cond_in['w_t2'], 'L3_cond_b_t2': _L3_cond_in['b_t2']}

def reference(x, cond_1024, mask_BxSxSx11_ik0, L0_cond_Wm, L0_cond_bm, L0_cond_Lam_re, L0_cond_Lam_im, L0_cond_B_re, L0_cond_B_im, L0_cond_C_re, L0_cond_C_im, L0_cond_D_diag, L0_cond_log_step, L0_cond_Wc, L0_cond_bc, L0_cond_W1, L0_cond_b1, L0_cond_W2, L0_cond_b2, L1_cond_norm1_w, L1_cond_film1_w, L1_cond_film1_b, L1_cond_q_w, L1_cond_q_b, L1_cond_k_w, L1_cond_k_b, L1_cond_v_w, L1_cond_v_b, L1_cond_proj_w, L1_cond_proj_b, L1_cond_norm2_w, L1_cond_film2_w, L1_cond_film2_b, L1_cond_mlp_w1, L1_cond_mlp_b1, L1_cond_mlp_w2, L1_cond_mlp_b2, L2_cond_W_self, L2_cond_b_self, L2_cond_w_bias, L2_cond_b_bias, L2_cond_Wq, L2_cond_bq, L2_cond_Wk, L2_cond_bk, L2_cond_Wout, L2_cond_bout, L3_cond_g1, L3_cond_g2, L3_cond_w_qkv, L3_cond_b_qkv, L3_cond_w_ao, L3_cond_b_ao, L3_cond_w_fc, L3_cond_b_fc, L3_cond_w_fo, L3_cond_b_fo, L3_cond_w_t1, L3_cond_b_t1, L3_cond_w_t2, L3_cond_b_t2):
    import jax
    import jax.numpy as jnp

    def _L0_cond_ref(y, t, Wm, bm, Lam_re, Lam_im, B_re, B_im, C_re, C_im, D_diag, log_step, Wc, bc, W1, b1, W2, b2):
        import jax, jax.numpy as jnp
        import numpy as np
        B, L, D, P = (8, 512, 256, 64)

        def _ln(x):
            m = x.mean(-1, keepdims=True)
            v = x.var(-1, keepdims=True)
            return (x - m) * jax.lax.rsqrt(v + 1e-05)

        def _s5(u, Lam_re, Lam_im, B_re, B_im, C_re, C_im, D_diag, log_step):
            Lam = Lam_re + 1j * Lam_im
            dt = jnp.exp(log_step)
            Lam_bar = jnp.exp(Lam * dt)
            Bc = B_re + 1j * B_im
            B_bar = ((Lam_bar - 1.0) / Lam)[:, None] * Bc
            Bu = jnp.einsum('bld,pd->blp', u.astype(B_bar.dtype), B_bar)
            A = jnp.broadcast_to(Lam_bar, Bu.shape)

            def binop(e1, e2):
                a1, b1 = e1
                a2, b2 = e2
                return (a1 * a2, a2 * b1 + b2)
            _, xs = jax.lax.associative_scan(binop, (A, Bu), axis=1)
            Cc = C_re + 1j * C_im
            return 2.0 * jnp.einsum('blp,dp->bld', xs, Cc).real + D_diag * u
        mod = t @ Wm + bm
        shift_a, scale_a, gate_a, shift_ff, scale_ff, gate_ff = jnp.split(mod, 6, axis=-1)
        y_mod = _ln(y) * (1 + scale_a[:, None]) + shift_a[:, None]
        a_y = _s5(y_mod, Lam_re, Lam_im, B_re, B_im, C_re, C_im, D_diag, log_step)
        y = y + gate_a[:, None] * a_y
        cond = t @ Wc + bc
        scale_c, shift_c = jnp.split(cond, 2, axis=-1)
        y_norm = _ln(y) * (1 + scale_c[:, None]) + shift_c[:, None]
        y_mod = y_norm * (1 + scale_ff[:, None]) + shift_ff[:, None]
        h = jax.nn.gelu(y_mod @ W1 + b1)
        ff_y = h @ W2 + b2
        return y + gate_ff[:, None] * ff_y

    def _L1_cond_ref(x, cond, norm1_w, film1_w, film1_b, q_w, q_b, k_w, k_b, v_w, v_b, proj_w, proj_b, norm2_w, film2_w, film2_b, mlp_w1, mlp_b1, mlp_w2, mlp_b2):
        import jax, jax.numpy as jnp
        import numpy as np
        DIM = 256
        MLP_RATIO = 4
        EPS = 1e-06

        def rmsnorm(x, w):
            return x * jax.lax.rsqrt(jnp.mean(x * x, axis=-1, keepdims=True) + EPS) * w

        def film(x, cond, w, b):
            ss = cond @ w + b
            scale, shift = jnp.split(ss, 2, axis=-1)
            return x * (1.0 + scale[:, None, :]) + shift[:, None, :]
        B, N, D = x.shape
        x_in = x
        h = film(rmsnorm(x, norm1_w), cond, film1_w, film1_b)
        Q = h @ q_w + q_b
        K = h @ k_w + k_b
        V = h @ v_w + v_b
        scores = jnp.einsum('bnd,bmd->bnm', Q, K) * D ** (-0.5)
        attn = jax.nn.softmax(scores, axis=-1)
        out = jnp.einsum('bnm,bmd->bnd', attn, V)
        x = x_in + (out @ proj_w + proj_b)
        x_in = x
        h = film(rmsnorm(x, norm2_w), cond, film2_w, film2_b)
        h = jax.nn.gelu(h @ mlp_w1 + mlp_b1, approximate=False) @ mlp_w2 + mlp_b2
        return x_in + h

    def _L2_cond_ref(v, q, adj, W_self, b_self, w_bias, b_bias, Wq, bq, Wk, bk, Wout, bout):
        import jax, jax.numpy as jnp
        import numpy as np
        NONGT = 20
        H = 16
        NEG = -9000000000000000.0

        def _gat_attention(self_feat, cond_adj, label_bias, Wq, bq, Wk, bk, Wout, bout):
            B, N, F = self_feat.shape
            ng = min(NONGT, N)
            dh = F // H
            kv = self_feat[:, :ng]
            qh = (self_feat @ Wq.T + bq).reshape(B, N, H, dh)
            kh = (kv @ Wk.T + bk).reshape(B, ng, H, dh)
            aff = jnp.einsum('bnhd,bmhd->bnhm', qh, kh) * (1.0 / np.sqrt(dh))
            mask = cond_adj[:, :, None, :] > 0
            aff = jnp.where(mask, aff, NEG) + label_bias[:, :, None, :]
            w = jax.nn.softmax(aff, axis=-1)
            out_t = jnp.einsum('bnhm,bmf->bnhf', w, kv)
            out = jnp.einsum('bnhf,hgf->bnhg', out_t, Wout) + bout.reshape(H, F // H)
            return out.reshape(B, N, F)

        def _forward(v, q, adj, W_self, b_self, w_bias, b_bias, Wq, bq, Wk, bk, Wout, bout):
            adj_f = adj.astype(jnp.float32)
            exp_v = v
            row_zero = exp_v.sum(-1) == 0
            q_exp = jnp.where(row_zero[..., None], 0.0, q[:, None, :])
            vcq = jnp.concatenate([exp_v, q_exp], axis=-1)
            self_feat = vcq @ W_self.T + b_self
            output = self_feat
            for d in range(2):
                A = adj_f if d == 0 else jnp.swapaxes(adj_f, 1, 2)
                A = A[:, :, :NONGT, :]
                cond = A.sum(-1)
                vb = A @ w_bias + b_bias
                output = output + _gat_attention(self_feat, cond, vb, Wq[d], bq[d], Wk[d], bk[d], Wout[d], bout[d])
            rel = jax.nn.relu(output)
            return exp_v + rel
        return _forward(v, q, adj, W_self, b_self, w_bias, b_bias, Wq, bq, Wk, bk, Wout, bout)

    def _L3_cond_ref(x, time_emb, g1, g2, w_qkv, b_qkv, w_ao, b_ao, w_fc, b_fc, w_fo, b_fo, w_t1, b_t1, w_t2, b_t2):
        import jax, jax.numpy as jnp
        import numpy as np
        EPS = float(np.finfo(np.float32).eps)

        def _rmsnorm(x, g):
            return x * jax.lax.rsqrt(jnp.mean(x * x, axis=-1, keepdims=True) + EPS) * g

        def _silu(x):
            return x * jax.nn.sigmoid(x)

        def _swiglu(x):
            a, gate = jnp.split(x, 2, axis=-1)
            return a * _silu(gate)

        def _rope(x):
            T, hd = (x.shape[1], x.shape[-1])
            inv_freq = 1.0 / 10000.0 ** (jnp.arange(0, hd, 2, dtype=jnp.float32) / hd)
            ang = jnp.arange(T, dtype=jnp.float32)[:, None] * inv_freq[None, :]
            cos = jnp.cos(ang)[None, :, None, :]
            sin = jnp.sin(ang)[None, :, None, :]
            x0, x1 = (x[..., 0::2], x[..., 1::2])
            o0 = x0 * cos - x1 * sin
            o1 = x1 * cos + x0 * sin
            return jnp.stack([o0, o1], axis=-1).reshape(x.shape)

        def _mha(x, w_qkv, b_qkv, w_ao, b_ao, n_head):
            B, T, C = x.shape
            hd = C // n_head
            qkv = x @ w_qkv + b_qkv
            q, k, v = jnp.split(qkv, 3, axis=-1)
            q = _rope(q.reshape(B, T, n_head, hd)).transpose(0, 2, 1, 3)
            k = _rope(k.reshape(B, T, n_head, hd)).transpose(0, 2, 1, 3)
            v = v.reshape(B, T, n_head, hd).transpose(0, 2, 1, 3)
            attn = jnp.einsum('bhqd,bhkd->bhqk', q, k) * (1.0 / np.sqrt(hd))
            attn = jax.nn.softmax(attn, axis=-1)
            out = jnp.einsum('bhqk,bhkd->bhqd', attn, v)
            out = out.transpose(0, 2, 1, 3).reshape(B, T, C)
            return out @ w_ao + b_ao

        def _ffn(x, w_fc, b_fc, w_fo, b_fo):
            return _swiglu(x @ w_fc + b_fc) @ w_fo + b_fo
        n_head = 16
        tp = _swiglu(time_emb @ w_t1 + b_t1) @ w_t2 + b_t2
        shift1, scale1, shift2, scale2 = jnp.split(tp, 4, axis=-1)
        h = _rmsnorm(x, g1) * (1.0 + scale1[:, None, :]) + shift1[:, None, :]
        x = x + _mha(h, w_qkv, b_qkv, w_ao, b_ao, n_head)
        h = _rmsnorm(x, g2) * (1.0 + scale2[:, None, :]) + shift2[:, None, :]
        x = x + _ffn(h, w_fc, b_fc, w_fo, b_fo)
        return x
    x = _L0_cond_ref(x, cond_1024, L0_cond_Wm, L0_cond_bm, L0_cond_Lam_re, L0_cond_Lam_im, L0_cond_B_re, L0_cond_B_im, L0_cond_C_re, L0_cond_C_im, L0_cond_D_diag, L0_cond_log_step, L0_cond_Wc, L0_cond_bc, L0_cond_W1, L0_cond_b1, L0_cond_W2, L0_cond_b2)
    x = _L1_cond_ref(x, cond_1024, L1_cond_norm1_w, L1_cond_film1_w, L1_cond_film1_b, L1_cond_q_w, L1_cond_q_b, L1_cond_k_w, L1_cond_k_b, L1_cond_v_w, L1_cond_v_b, L1_cond_proj_w, L1_cond_proj_b, L1_cond_norm2_w, L1_cond_film2_w, L1_cond_film2_b, L1_cond_mlp_w1, L1_cond_mlp_b1, L1_cond_mlp_w2, L1_cond_mlp_b2)
    x = _L2_cond_ref(x, cond_1024, mask_BxSxSx11_ik0, L2_cond_W_self, L2_cond_b_self, L2_cond_w_bias, L2_cond_b_bias, L2_cond_Wq, L2_cond_bq, L2_cond_Wk, L2_cond_bk, L2_cond_Wout, L2_cond_bout)
    x = _L3_cond_ref(x, cond_1024, L3_cond_g1, L3_cond_g2, L3_cond_w_qkv, L3_cond_b_qkv, L3_cond_w_ao, L3_cond_b_ao, L3_cond_w_fc, L3_cond_b_fc, L3_cond_w_fo, L3_cond_b_fo, L3_cond_w_t1, L3_cond_b_t1, L3_cond_w_t2, L3_cond_b_t2)
    return x

_drawn_inputs = setup_inputs


def setup_inputs(seed=0):
    import zlib

    import numpy as np

    out = dict(_drawn_inputs(seed))
    spreads = {'L0_cond_Lam_re': (-0.5, 0.6),
     'L0_cond_b1': (0.0, 0.8),
     'L0_cond_b2': (0.0, 0.1),
     'L1_cond_norm1_w': (1.0, 0.2),
     'L1_cond_film1_b': (0.0, 0.1),
     'L1_cond_q_b': (0.0, 0.1),
     'L1_cond_k_b': (0.0, 0.8),
     'L1_cond_v_b': (0.0, 0.1),
     'L1_cond_proj_b': (0.0, 0.1),
     'L1_cond_norm2_w': (1.0, 0.2),
     'L1_cond_film2_b': (0.0, 0.1),
     'L1_cond_mlp_b1': (0.0, 0.1),
     'L1_cond_mlp_b2': (0.0, 0.1),
     'L2_cond_b_self': (0.0, 0.1),
     'L2_cond_bq': (0.0, 0.1),
     'L2_cond_bk': (0.0, 0.1),
     'L2_cond_bout': (0.0, 0.1),
     'L3_cond_g1': (1.0, 0.6),
     'L3_cond_g2': (1.0, 0.6),
     'L3_cond_b_qkv': (0.0, 0.493),
     'L3_cond_b_ao': (0.0, 0.1),
     'L3_cond_b_fc': (0.0, 0.8),
     'L3_cond_b_fo': (0.0, 0.1),
     'L3_cond_b_t1': (0.0, 0.8),
     'L3_cond_b_t2': (0.0, 0.8)}
    factors = {'L0_cond_Wc': 5.191,
     'L0_cond_bc': 8.0,
     'L3_cond_w_fc': 3.04,
     'L3_cond_w_fo': 3.031,
     'L3_cond_w_t1': 8.0,
     'L3_cond_w_t2': 8.0}
    for name, (base, spread) in spreads.items():
        noise = np.random.default_rng([zlib.crc32(name.encode()), seed]).standard_normal(out[name].shape)
        drawn = base * np.exp(spread * noise) if base else spread * noise
        out[name] = jnp.asarray(drawn.astype(out[name].dtype))
    for name, factor in factors.items():
        out[name] = (out[name] * factor).astype(out[name].dtype)
    return out
```

```python
import concourse.bass as bass
from concourse import mybir
from contextlib import ExitStack
import numpy as np

F32 = mybir.dt.float32
I32 = mybir.dt.int32
ALU = mybir.AluOpType
ACT = mybir.ActivationFunctionType
AX = mybir.AxisListType

P = 128
B, S, D = 128, 64, 256
KT = D // P
GB = 8
GT = GB * S
NG = B // GB
NP = GB // 2
FF = 4 * D
HJ = FF // P
NS = 64
LAYERS = 4


class Mem:

    def __init__(self, nc, ctx):
        self.nc, self.ctx = nc, ctx

    def sb(self, name, shape, dt=F32):
        return self.ctx.enter_context(self.nc.sbuf_tensor(name, shape, dt))

    def sem(self, name):
        return self.ctx.enter_context(self.nc.semaphore(name))


def per_batch(table, batches):
    return table[:, :, batches].unsqueeze(3).broadcast_to([P, KT, GB, S])


def tokens(t):
    return t.rearrange("p k (b s) -> p k b s", s=S)


class Signal:

    def __init__(self, sem, base, per_group):
        self.sem, self.base, self.k = sem, base, per_group

    def after(self, n, j=None):
        return self.base + n * self.k + (self.k if j is None else j + 1)

    def wait(self, engine, n, j=None):
        value = self.after(n, j)
        if not isinstance(value, int) or value > 0:
            engine.wait_ge(self.sem, value)

    def wait_before(self, engine, n):
        value = self.base + n * self.k
        if not isinstance(value, int) or value > 0:
            engine.wait_ge(self.sem, value)


class Signals:

    def __init__(self, mem):
        self.mem, self.sems, self.base, self.open = mem, {}, {}, {}

    def get(self, name, per_group=1):
        if name not in self.sems:
            self.sems[name], self.base[name] = self.mem.sem(name), 0
        self.open[name] = per_group
        return Signal(self.sems[name], self.base[name], per_group)

    def close_layer(self, groups):
        for name, k in self.open.items():
            self.base[name] += groups * k
        self.open = {}



class Chain:

    def __init__(self, engine, signals, name):
        if name not in signals.sems:
            signals.sems[name], signals.base[name] = signals.mem.sem(name), 0
        self.engine, self.signals, self.name = engine, signals, name

    def __call__(self, instruction):
        instruction.then_inc(self.signals.sems[self.name], 1)
        self.signals.base[self.name] += 1
        self.engine.wait_ge(self.signals.sems[self.name], self.signals.base[self.name])

    def value(self):
        return self.signals.base[self.name]


def conditioning(nc, mem, sg, T, K):
    x_all = K["x"]
    stage = x_all.rearrange("p g k t -> p (g k t)")
    at = [6 * KT * GT]

    def staged(cols):
        a = stage[:, at[0]:at[0] + cols]
        at[0] += cols
        return a

    w_mod = staged(KT * 6 * D).rearrange("p (k n) -> p k n", k=KT)
    w_c = staged(KT * 2 * D).rearrange("p (k n) -> p k n", k=KT)
    w_f1 = staged(KT * 2 * D).rearrange("p (k n) -> p k n", k=KT)
    w_f2 = staged(KT * 2 * D).rearrange("p (k n) -> p k n", k=KT)
    w_sq = staged(KT * D).rearrange("p (k n) -> p k n", k=KT)
    w_t1 = staged(KT * 2 * D).rearrange("p (k n) -> p k n", k=KT)
    w_t2 = staged(KT * 4 * D).rearrange("p (k n) -> p k n", k=KT)
    loads = [(w_mod, "L0_cond_Wm"), (w_c, "L0_cond_Wc"), (w_f1, "L1_cond_film1_w"), (w_f2, "L1_cond_film2_w"),
             (w_sq, "WselfT_q"), (w_t1, "L3_cond_w_t1"), (w_t2, "L3_cond_w_t2")]

    with ExitStack() as ctx:
        m = Mem(nc, ctx)
        cond = m.sb("condT", [P, KT, B])
        raw = m.sb("raw_mod", [P, 12, B])
        cvec = m.sb("cvec", [P, 12])
        q = m.sb("svec", [P, 24])
        cs = m.sb("cs_tab", [P, S])
        sn = m.sb("sn_tab", [P, S])
        tmp = m.sb("tmp_tab", [P, 2, S])
        tp = m.sb("tp_act", [P, KT, B])
        tg = m.sb("tp_gate", [P, KT, B])
        ps = ctx.enter_context(nc.psum_tensor("ps_mod", [P, 4, 4, B], F32))
        d_load = sg.get("cond_loads", 0)
        n_loads = len(loads) + 4
        s_mm, s_ev = mem.sem("mod_products"), mem.sem("mod_evacuated")
        s_tp, s_swi = mem.sem("swiglu_input"), mem.sem("swiglu_gate")
        sn_ready, sn_done = mem.sem("angle_ready"), mem.sem("sine_done")
        bias = K["bias"]

        jobs = [(w_mod, 0, 4), (w_mod, 4, 4), (w_mod, 8, 4), (w_c, 0, 4), (w_f1, 0, 4), (w_f2, 0, 4), (w_sq, 0, 2),
                (w_t1, 0, 4), (w_t2, 0, 4), (w_t2, 4, 4)]

        block = ctx.enter_context(nc.Block())

        @block.sync
        def _(sp):
            for dst, src in ((cond, T["condT"]), (K["bias"], T["vectors"]), (K["consts"], T["consts"]),
                             (cvec[:, 0:3], T["lam"])):
                sp.dma_start(dst[:], src[:]).then_inc(d_load.sem, 16)
            for dst, name in loads:
                sp.dma_start(dst, T[name].rearrange("(k p) n -> p k n", p=P)).then_inc(d_load.sem, 16)
            for g in range(6):
                sp.dma_start(x_all[:, g], T["x"][:, g]).then_inc(K["x_loaded"], 16)
            for dst, src in K["weights_first"]:
                sp.dma_start(dst, src).then_inc(K["w_loaded"], 16)
            sp.wait_ge(K["x_loaded"], 6 * 16)
            sp.wait_ge(K["w_loaded"], 16 * len(K["weights_first"]))

        @block.tensor
        def _(pe):
            pe.wait_ge(d_load.sem, 16 * n_loads)
            for i, (w, first, tiles) in enumerate(jobs):
                if i >= 4:
                    pe.wait_ge(s_ev, i - 3)
                if i == 8:
                    pe.wait_ge(s_swi, 1)
                rhs = tp if i >= 8 else cond
                for t in range(tiles):
                    for k in range(KT):
                        c = (first + t) * P
                        last = nc.tensor.matmul(ps[:, i % 4, t], w[:, k, c:c + P], rhs[:, k], start=(k == 0), stop=(k == KT - 1))
                last.then_inc(s_mm, 1)

        @block.scalar
        def _(act):
            act.wait_ge(d_load.sem, 16 * n_loads)
            act.wait_ge(s_tp, 1)
            nc.scalar.activation(tg[:], tg[:], ACT.Silu).then_inc(s_tp, 1)
            act.wait_ge(sn_ready, 1)
            nc.scalar.activation(q[:, 0:1], cvec[:, 2:3], ACT.Exp).then_inc(sn_done, 1)
            act.wait_ge(sn_ready, 2)
            nc.scalar.activation(q[:, 2:3], q[:, 1:2], ACT.Exp).then_inc(sn_done, 1)
            act.wait_ge(sn_ready, 3)
            nc.scalar.activation(q[:, 6:8], q[:, 4:6], ACT.Sin).then_inc(sn_done, 1)

        @block.vector
        def _(v):
            ch = Chain(v, sg, "vector_chain")
            v.wait_ge(d_load.sem, 16 * n_loads)
            nc.vector.memset(K["eps"][:, 0:1], 1e-5)
            nc.vector.memset(K["eps"][:, 1:2], 1e-6)
            ch(nc.vector.memset(K["eps"][:, 2:3], float(np.finfo(np.float32).eps)))
            ch(nc.vector.memset(K["ones"][:], 1.0))
            ch(nc.vector.memset(K["mean"][:], 1.0 / D))

            def bias_of(col, tiles):
                return bias[:, col:col + tiles].unsqueeze(2).broadcast_to([P, tiles, B])

            def add_bias(i, dst, col, tiles=4, step=1):
                v.wait_ge(s_mm, i + 1)
                nc.vector.tensor_tensor(dst, ps[:, i % 4, 0:tiles], bias_of(col, tiles), ALU.add).then_inc(s_ev, 1)
                v.wait_ge(s_ev, i + 1)

            V = K["vec_at"]
            add_bias(0, raw[:, 0:4], V["L0_cond_bm"])
            add_bias(1, raw[:, 4:8], V["L0_cond_bm"] + 4)
            add_bias(2, raw[:, 8:12], V["L0_cond_bm"] + 8)
            ch(nc.vector.tensor_copy(K["l0_shift"][:], raw[:, 0:2]))
            ch(nc.vector.tensor_scalar_add(K["l0_scale"][:], raw[:, 2:4], 1.0))
            ch(nc.vector.tensor_copy(K["l0_gate"][:], raw[:, 4:6]))
            ch(nc.vector.tensor_copy(K["l0_gate_ff"][:], raw[:, 10:12]))
            add_bias(3, raw[:, 0:4], V["L0_cond_bc"])
            ch(nc.vector.tensor_scalar_add(raw[:, 0:2], raw[:, 0:2], 1.0))
            ch(nc.vector.tensor_scalar_add(raw[:, 8:10], raw[:, 8:10], 1.0))
            ch(nc.vector.tensor_tensor(K["l0_scale_ff"][:], raw[:, 0:2], raw[:, 8:10], ALU.mult))
            ch(nc.vector.tensor_tensor(raw[:, 2:4], raw[:, 2:4], raw[:, 8:10], ALU.mult))
            ch(nc.vector.tensor_tensor(K["l0_shift_ff"][:], raw[:, 2:4], raw[:, 6:8], ALU.add))
            for i, name, norm, film in ((4, "l1a", "L1_cond_norm1_w", "L1_cond_film1_b"), (5, "l1b", "L1_cond_norm2_w", "L1_cond_film2_b")):
                add_bias(i, raw[:, 0:4], V[film])
                ch(nc.vector.tensor_scalar_add(raw[:, 0:2], raw[:, 0:2], 1.0))
                ch(nc.vector.tensor_tensor(K[name + "_scale"][:], raw[:, 0:2], bias_of(V[norm], 2), ALU.mult))
                ch(nc.vector.tensor_copy(K[name + "_shift"][:], raw[:, 2:4]))
            v.wait_ge(s_mm, 7)
            nc.vector.tensor_copy(K["l2_q"][:], ps[:, 6 % 4, 0:2]).then_inc(s_ev, 1)
            v.wait_ge(s_ev, 7)
            add_bias(7, raw[:, 0:4], V["L3_cond_b_t1"])
            ch(nc.vector.tensor_copy(tp[:], raw[:, 0:2]))
            nc.vector.tensor_copy(tg[:], raw[:, 2:4]).then_inc(s_tp, 1)
            v.wait_ge(s_tp, 2)
            nc.vector.tensor_tensor(tp[:], tp[:], tg[:], ALU.mult).then_inc(s_swi, 1)
            for i, name, norm in ((8, "l3a", "L3_cond_g1"), (9, "l3b", "L3_cond_g2")):
                add_bias(i, raw[:, 0:4], V["L3_cond_b_t2"] + 4 * (i - 8))
                ch(nc.vector.tensor_copy(K[name + "_shift"][:], raw[:, 0:2]))
                ch(nc.vector.tensor_scalar_add(raw[:, 2:4], raw[:, 2:4], 1.0))
                ch(nc.vector.tensor_tensor(K[name + "_scale"][:], raw[:, 2:4], bias_of(V[norm], 2), ALU.mult))

            lr, li, sgn = cvec[:, 0:1], cvec[:, 1:2], K["sign"]
            TT, TS = nc.vector.tensor_tensor, nc.vector.tensor_scalar
            nc.vector.memset(q[:, 3:4], 0.0).then_inc(sn_ready, 1)
            v.wait_ge(sn_done, 1)
            TT(q[:, 1:2], lr, q[:, 0:1], ALU.mult).then_inc(sn_ready, 1)
            ch(TT(q[:, 3:4], li, q[:, 0:1], ALU.mult))
            ROUND = 12582912.0
            ch(TS(q[:, 8:9], q[:, 3:4], 1.0 / (2 * np.pi), ROUND, ALU.mult, ALU.add))
            ch(TS(q[:, 8:9], q[:, 8:9], -ROUND, None, ALU.add))
            c1 = 6.28125
            c2 = 0.0019350051879882812
            c3 = 2 * np.pi - c1 - c2
            for c in (c1, c2, c3):
                ch(TS(q[:, 9:10], q[:, 8:9], -c, None, ALU.mult))
                ch(TT(q[:, 3:4], q[:, 3:4], q[:, 9:10], ALU.add))
            ch(TS(q[:, 3:4], q[:, 3:4], float(-np.pi), float(np.pi), ALU.max, ALU.min))
            PI = 3.1415925
            ch(TS(q[:, 4:5], q[:, 3:4], 0.5, None, ALU.mult))
            ch(TS(q[:, 5:6], q[:, 4:5], float(np.pi / 2), PI, ALU.add, ALU.min))
            v.wait_ge(sn_done, 2)
            nc.vector.tensor_scalar_max(q[:, 5:6], q[:, 5:6], 0.0).then_inc(sn_ready, 1)
            v.wait_ge(sn_done, 3)
            s, c = q[:, 10:11], q[:, 11:12]
            ch(TT(s, q[:, 6:7], q[:, 7:8], ALU.mult))
            ch(TS(s, s, 2.0, None, ALU.mult))
            ch(TT(c, q[:, 6:7], q[:, 6:7], ALU.mult))
            ch(TS(c, c, -2.0, 1.0, ALU.mult, ALU.add))
            nr, ni, den, cr, ci = (q[:, k:k + 1] for k in range(12, 17))
            u0, u1 = q[:, 17:18], q[:, 18:19]
            ch(TT(nr, c, q[:, 2:3], ALU.mult))
            ch(TS(nr, nr, -1.0, None, ALU.add))
            ch(TT(ni, s, q[:, 2:3], ALU.mult))
            ch(TT(den, lr, lr, ALU.mult))
            ch(TT(u0, li, li, ALU.mult))
            ch(TT(den, den, u0, ALU.add))
            ch(nc.vector.reciprocal(den, den))
            ch(TT(u0, nr, lr, ALU.mult))
            ch(TT(u1, ni, li, ALU.mult))
            ch(TT(cr, u0, u1, ALU.add))
            ch(TT(cr, cr, den, ALU.mult))
            ch(TT(u0, ni, lr, ALU.mult))
            ch(TT(u1, nr, li, ALU.mult))
            ch(TT(ci, u0, u1, ALU.subtract))
            ch(TT(ci, ci, den, ALU.mult))
            ch(nc.vector.memset(cs[:, 0:1], 1.0))
            ch(nc.vector.memset(sn[:, 0:1], 0.0))
            h = 1
            while h < S:
                ch(TS(cs[:, h:2 * h], cs[:, 0:h], c, None, ALU.mult))
                ch(TS(tmp[:, 0, 0:h], sn[:, 0:h], s, None, ALU.mult))
                ch(TS(sn[:, h:2 * h], sn[:, 0:h], c, None, ALU.mult))
                ch(TS(tmp[:, 1, 0:h], cs[:, 0:h], s, None, ALU.mult))
                ch(TT(cs[:, h:2 * h], cs[:, h:2 * h], tmp[:, 0, 0:h], ALU.subtract))
                ch(TT(sn[:, h:2 * h], sn[:, h:2 * h], tmp[:, 1, 0:h], ALU.add))
                ch(TT(u0, c, s, ALU.mult))
                ch(TT(u1, s, s, ALU.mult))
                ch(TT(c, c, c, ALU.mult))
                ch(TT(c, c, u1, ALU.subtract))
                ch(TS(s, u0, 2.0, None, ALU.mult))
                h *= 2
            ch(TS(K["turn_in"][:, 0], cs[:], cr, None, ALU.mult))
            ch(TS(tmp[:, 0], sn[:], ci, None, ALU.mult))
            ch(TT(K["turn_in"][:, 0], K["turn_in"][:, 0], tmp[:, 0], ALU.add))
            ch(TS(K["turn_in"][:, 1], cs[:], ci, None, ALU.mult))
            ch(TS(tmp[:, 0], sn[:], cr, None, ALU.mult))
            ch(TT(K["turn_in"][:, 1], K["turn_in"][:, 1], tmp[:, 0], ALU.subtract))
            ch(TS(K["turn_in"][:, 1], K["turn_in"][:, 1], sgn, None, ALU.mult))
            ch(TS(K["turn_out"][:, 0], cs[:], sgn, -2.0, ALU.mult, ALU.mult))
            ch(TS(K["turn_out"][:, 1], sn[:], -2.0, None, ALU.mult))
            dec = K["decay"].rearrange("p (b s) -> p b s", s=S)
            ch(nc.vector.memset(K["decay"][:], 1.0))
            ch(TS(K["decay"][:], K["decay"][:], q[:, 2:3], None, ALU.mult))
            ch(nc.vector.memset(dec[:, :, 0:1], 0.0))


class Norm:

    def __init__(self, nc, m, sg, K, name, src, src_ready, out, out_read, center, eps, scale, shift, ps, shared):
        self.nc, self.K, self.src, self.src_ready, self.out, self.out_read = nc, K, src, src_ready, out, out_read
        self.center, self.eps, self.scale, self.shift, self.ps = center, eps, scale, shift, ps
        self.sum, self.xc, self.sq, self.rstd = shared
        if center:
            self.summed = sg.get(name + "_summed")
            self.meaned = sg.get(name + "_meaned")
            self.centered = sg.get(name + "_centered")
        self.squared = sg.get(name + "_squared")
        self.squares_summed = sg.get(name + "_squares_summed")
        self.varied = sg.get(name + "_varied")
        self.rooted = sg.get(name + "_rooted")
        self.inverted = sg.get(name + "_inverted")
        self.normed = sg.get(name + "_normed")
        self.scaled = sg.get(name + "_scaled")
        self.done = sg.get(name + "_done")

    def vector_sum(self, v, n):
        self.src_ready(v, n)
        x = self.src(n)
        self.nc.vector.tensor_tensor(self.sum[:], x[:, 0], x[:, 1], ALU.add).then_inc(self.summed.sem, 1)

    def tensor_mean(self, pe, n):
        pe.wait_ge(self.summed.sem, self.summed.after(n))
        self.nc.tensor.matmul(self.ps[:, 0], self.K["mean"][:], self.sum[:], start=True, stop=True).then_inc(self.meaned.sem, 1)

    def vector_center(self, v, n):
        v.wait_ge(self.meaned.sem, self.meaned.after(n))
        mean = self.ps[:, 0:1].broadcast_to([P, KT, GT])
        self.nc.vector.tensor_tensor(self.xc[:], self.src(n), mean, ALU.subtract).then_inc(self.centered.sem, 1)

    def scalar_square(self, act, n):
        if self.center:
            act.wait_ge(self.centered.sem, self.centered.after(n))
            x = self.xc[:]
        else:
            self.src_ready(act, n)
            x = self.src(n)
        self.nc.scalar.activation(self.sq[:], x, ACT.Square).then_inc(self.squared.sem, 1)

    def pool_sum(self, pool, n):
        pool.wait_ge(self.squared.sem, self.squared.after(n))
        self.nc.gpsimd.tensor_tensor(self.sum[:], self.sq[:, 0], self.sq[:, 1], ALU.add).then_inc(self.squares_summed.sem, 1)

    def tensor_variance(self, pe, n):
        pe.wait_ge(self.squares_summed.sem, self.squares_summed.after(n))
        self.nc.tensor.matmul(self.ps[:, 1], self.K["mean"][:], self.sum[:], start=True, stop=True).then_inc(self.varied.sem, 1)

    def scalar_root(self, act, n):
        act.wait_ge(self.varied.sem, self.varied.after(n))
        self.nc.scalar.activation(self.rstd[:], self.ps[:, 1], ACT.Sqrt, bias=self.K["eps"][:, self.eps:self.eps + 1]).then_inc(self.rooted.sem, 1)

    def vector_apply(self, v, n):
        v.wait_ge(self.rooted.sem, self.rooted.after(n))
        self.nc.vector.reciprocal(self.rstd[:], self.rstd[:]).then_inc(self.inverted.sem, 1)
        v.wait_ge(self.inverted.sem, self.inverted.after(n))
        rstd = self.rstd[:].unsqueeze(1).broadcast_to([P, KT, GT])
        x = self.xc[:] if self.center else self.src(n)
        self.nc.vector.tensor_tensor(self.xc[:], x, rstd, ALU.mult).then_inc(self.normed.sem, 1)
        v.wait_ge(self.normed.sem, self.normed.after(n))
        bs = bass.ds(n * GB, GB)
        self.nc.vector.tensor_tensor(tokens(self.xc[:]), tokens(self.xc[:]), per_batch(self.scale, bs), ALU.mult).then_inc(self.scaled.sem, 1)
        v.wait_ge(self.scaled.sem, self.scaled.after(n))
        self.out_read(v, n)
        self.nc.vector.tensor_tensor(tokens(self.out(n)), tokens(self.xc[:]), per_batch(self.shift, bs), ALU.add).then_inc(self.done.sem, 1)


class FeedForward:

    def __init__(self, nc, sg, w1, w2, b1, func, m, m_ready, ps_h, ps_o, hidden, out_read):
        self.nc, self.w1, self.w2, self.b1, self.func, self.m, self.m_ready = nc, w1, w2, b1, func, m, m_ready
        self.ps_h, self.ps_o, self.h, self.out_read = ps_h, ps_o, hidden, out_read
        self.up = sg.get("ff_up", HJ)
        self.act = sg.get("ff_activated", HJ)
        self.down = sg.get("ff_down", HJ)

    def tensor_up(self, pe, n, j, u):
        if j == 0:
            self.m_ready(pe, n)
        if j >= 2:
            pe.wait_ge(self.act.sem, self.act.after(n, j - 2))
        else:
            self.act.wait_before(pe, n)
        for k in range(KT):
            last = self.nc.tensor.matmul(self.ps_h[:, j % 2], self.w1[:, k, j * P:(j + 1) * P], self.m(u)[:, k], start=(k == 0), stop=(k == KT - 1))
        last.then_inc(self.up.sem, 1)

    def scalar_activate(self, act, n, j):
        act.wait_ge(self.up.sem, self.up.after(n, j))
        if j >= 2:
            act.wait_ge(self.down.sem, self.down.after(n, j - 2))
        else:
            self.down.wait_before(act, n)
        self.nc.scalar.activation(self.h[:, j % 2], self.ps_h[:, j % 2], self.func, bias=self.b1[:, j:j + 1]).then_inc(self.act.sem, 1)

    def tensor_down(self, pe, n, j):
        pe.wait_ge(self.act.sem, self.act.after(n, j))
        if j == 0:
            self.out_read(pe, n)
        for t in range(KT):
            last = self.nc.tensor.matmul(self.ps_o[:, t], self.w2[:, j, t * P:(t + 1) * P], self.h[:, j % 2], start=(j == 0), stop=(j == HJ - 1))
        last.then_inc(self.down.sem, 1)


def two_stage(engine, front, both, back):
    front(0)
    both(0, 1, 0)
    with engine.Fori(1, NG - 2, 2) as i:
        both(i, i + 1, 1)
        both(i + 1, i + 2, 0)
    back(NG - 1)


def layer0(nc, mem, sg, T, K):
    x_all = K["x"]
    V, bias = K["vec_at"], K["bias"]
    with ExitStack() as ctx:
        m = Mem(nc, ctx)
        psum = lambda name, n: ctx.enter_context(nc.psum_tensor(name, [P, n, GT], F32))
        x1 = m.sb("l0_x1", [P, 2, KT, GT])
        min_ = m.sb("l0_m", [P, 2, KT, GT])
        u_in = m.sb("l0_u", [P, KT, GT])
        xc = m.sb("l0_xc", [P, KT, GT])
        sq = m.sb("l0_sq", [P, KT, GT])
        sm = m.sb("l0_sum", [P, GT])
        rstd = m.sb("l0_rstd", [P, GT])
        bz = m.sb("l0_bz", [P, 2, GT])
        z = m.sb("l0_z", [P, GT])
        zt = m.sb("l0_zt", [P, 2, GT])
        ay = m.sb("l0_ay", [P, KT, GT])
        ot = sq
        hidden = m.sb("l0_h", [P, 2, GT])
        ps_h, ps_o, ps_n, ps_f = psum("l0_psh", 2), psum("l0_pso", 2), psum("l0_psn", 2), psum("l0_psf", 2)

        s_u = sg.get("s5_inputs")
        s_turn = sg.get("s5_turned", 2)
        s_tsum = sg.get("s5_turned_summed")
        s_scan = sg.get("s5_scanned")
        s_cos = sg.get("s5_cosine_part")
        s_sin = sg.get("s5_sine_part")
        s_y = sg.get("s5_outputs")
        s_ay = sg.get("s5_skip", 2)
        s_g = sg.get("s5_gated")
        s_x1 = sg.get("x1_ready")
        s_ffo = sg.get("ff_out_read")
        s_xo = sg.get("x_updated")

        def x_loaded(e, n):
            e.wait_ge(K["x_loaded"], (n + 1) * 16)

        def x1_ready(e, n):
            e.wait_ge(s_x1.sem, s_x1.after(n))

        def no_wait(e, n):
            pass

        par = {}
        xs = lambda n: x_all[:, n]
        n1 = Norm(nc, m, sg, K, "norm1", xs, x_loaded, lambda n: u_in[:], no_wait, True, 0, K["l0_scale"], K["l0_shift"], ps_n, (sm, xc, sq, rstd))
        n2 = Norm(nc, m, sg, K, "norm2", lambda n: x1[:, par["w"]], x1_ready, lambda n: min_[:, par["w"]], no_wait, True, 0,
                  K["l0_scale_ff"], K["l0_shift_ff"], ps_n, (sm, xc, sq, rstd))

        def m_ready(pe, n):
            pe.wait_ge(n2.done.sem, n2.done.after(n))

        def out_read(pe, n):
            s_ffo.wait_before(pe, n)

        ff = FeedForward(nc, sg, K["l0_w1"], K["l0_w2"], bias[:, V["L0_cond_b1"]:], ACT.Gelu_apprx_tanh,
                         lambda u: min_[:, u], m_ready, ps_h, ps_o, hidden, out_read)

        def bcast_turn(t, k):
            return t[:, k:k + 1].broadcast_to([P, GB, S])

        bs3 = lambda a: a.rearrange("p (b s) -> p b s", s=S)
        block = ctx.enter_context(nc.Block())

        @block.sync
        def _(sp):
            for g in range(6, NG):
                sp.dma_start(x_all[:, g], T["x"][:, g]).then_inc(K["x_loaded"], 16)
                sp.wait_ge(K["x_loaded"], (g + 1) * 16)

        @block.tensor
        def _(pe):
            def b_products(n):
                pe.wait_ge(n1.done.sem, n1.done.after(n))
                for c in range(2):
                    for k in range(KT):
                        last = nc.tensor.matmul(ps_f[:, c], K["s5_b"][:, c, k], u_in[:, k], start=(k == 0), stop=(k == KT - 1))
                last.then_inc(s_u.sem, 1)

            def c_products(n):
                pe.wait_ge(s_cos.sem, s_cos.after(n))
                pe.wait_ge(s_sin.sem, s_sin.after(n))
                for t in range(KT):
                    for c in range(2):
                        last = nc.tensor.matmul(ps_f[:, t], K["s5_c"][:, c, t * P:(t + 1) * P], zt[:, c], start=(c == 0), stop=(c == 1))
                last.then_inc(s_y.sem, 1)

            steps = [n1.tensor_mean, n1.tensor_variance, None, b_products, None, c_products, n2.tensor_mean, n2.tensor_variance]
            front_steps = [(lambda pe, n: b_products(n)) if s is b_products else (lambda pe, n: c_products(n)) if s is c_products else s for s in steps]

            def front(n):
                for s in front_steps:
                    if s:
                        s(pe, n)

            def both(n, f, u):
                for j in range(HJ):
                    ff.tensor_up(pe, n, j, u)
                    if j >= 1:
                        ff.tensor_down(pe, n, j - 1)
                    if f is not None and front_steps[j]:
                        front_steps[j](pe, f)
                ff.tensor_down(pe, n, HJ - 1)

            two_stage(pe, front, both, lambda n: both(n, None, 1))

        @block.scalar
        def _(act):
            steps = [n1.scalar_square, n1.scalar_root, None, None, None, None, n2.scalar_square, n2.scalar_root]

            def front(n):
                par["w"] = 0
                for s in steps:
                    if s:
                        s(act, n)

            def both(n, f, u):
                par["w"] = 1 - u
                for j in range(HJ):
                    ff.scalar_activate(act, n, j)
                    if f is not None and steps[j]:
                        steps[j](act, f)

            two_stage(act, front, both, lambda n: both(n, None, 1))

        @block.gpsimd
        def _(pool):
            def front(n):
                n1.pool_sum(pool, n)
                pool.wait_ge(s_turn.sem, s_turn.after(n))
                nc.gpsimd.tensor_tensor(bz[:, 0], bz[:, 0], bz[:, 1], ALU.add).then_inc(s_tsum.sem, 1)
                pool.wait_ge(s_scan.sem, s_scan.after(n))
                nc.gpsimd.tensor_tensor(bs3(zt[:, 1]), bs3(z[:]), bcast_turn(K["turn_out"], 1), ALU.mult).then_inc(s_sin.sem, 1)
                n2.pool_sum(pool, n)

            front(0)
            with pool.Fori(1, NG) as i:
                front(i)

        @block.vector
        def _(v):
            def front(n, w):
                par["w"] = w
                n1.vector_sum(v, n)
                n1.vector_center(v, n)
                n1.vector_apply(v, n)
                v.wait_ge(s_u.sem, s_u.after(n))
                for c in range(2):
                    nc.vector.tensor_tensor(bs3(bz[:, c]), bs3(ps_f[:, c]), bcast_turn(K["turn_in"], c), ALU.mult).then_inc(s_turn.sem, 1)
                v.wait_ge(s_tsum.sem, s_tsum.after(n))
                nc.vector.tensor_tensor_scan(z[:], K["decay"][:], bz[:, 0], 0.0, ALU.mult, ALU.add).then_inc(s_scan.sem, 1)
                v.wait_ge(s_scan.sem, s_scan.after(n))
                nc.vector.tensor_tensor(bs3(zt[:, 0]), bs3(z[:]), bcast_turn(K["turn_out"], 0), ALU.mult).then_inc(s_cos.sem, 1)
                v.wait_ge(s_y.sem, s_y.after(n))
                d0 = V["L0_cond_D_diag"]
                for t in range(KT):
                    nc.vector.scalar_tensor_tensor(ay[:, t], u_in[:, t], bias[:, d0 + t:d0 + t + 1], ps_f[:, t], ALU.mult, ALU.add).then_inc(s_ay.sem, 1)
                v.wait_ge(s_ay.sem, s_ay.after(n))
                nc.vector.tensor_tensor(tokens(ay[:]), tokens(ay[:]), per_batch(K["l0_gate"], bass.ds(n * GB, GB)), ALU.mult).then_inc(s_g.sem, 1)
                v.wait_ge(s_g.sem, s_g.after(n))
                nc.vector.tensor_tensor(x1[:, w], ay[:], x_all[:, n], ALU.add).then_inc(s_x1.sem, 1)
                n2.vector_sum(v, n)
                n2.vector_center(v, n)
                n2.vector_apply(v, n)

            def back(n, u):
                s_xo.wait_before(v, n)
                v.wait_ge(ff.down.sem, ff.down.after(n))
                b0 = V["L0_cond_b2"]
                gate = K["l0_gate_ff"]
                for t in range(KT):
                    g = gate[:, t, bass.ds(n * GB, GB)].unsqueeze(2).broadcast_to([P, GB, S])
                    last = nc.vector.scalar_tensor_tensor(bs3(ot[:, t]), bs3(ps_o[:, t]), bias[:, b0 + t:b0 + t + 1], g, ALU.add, ALU.mult)
                last.then_inc(s_ffo.sem, 1)
                v.wait_ge(s_ffo.sem, s_ffo.after(n))
                nc.vector.tensor_tensor(x_all[:, n], ot[:], x1[:, u], ALU.add).then_inc(s_xo.sem, 1)

            def both(n, f, u):
                front(f, 1 - u)
                back(n, u)

            two_stage(v, lambda n: front(n, 0), both, lambda n: back(n, 1))
            v.wait_ge(s_xo.sem, s_xo.after(NG - 1))
    sg.close_layer(NG)


def layer1(nc, mem, sg, T, K):
    x_all = K["x"]
    V, bias = K["vec_at"], K["bias"]
    SCALE = float(D) ** -0.5
    with ExitStack() as ctx:
        m = Mem(nc, ctx)
        psum = lambda name, n: ctx.enter_context(nc.psum_tensor(name, [P, n, GT], F32))
        x1 = m.sb("l1_x1", [P, 2, KT, GT])
        min_ = m.sb("l1_m", [P, 2, KT, GT])
        h_in = m.sb("l1_in", [P, KT, GT])
        xc = m.sb("l1_xc", [P, KT, GT])
        q = m.sb("l1_q", [P, KT, GT])
        k_ = m.sb("l1_k", [P, KT, GT])
        vt = m.sb("l1_v", [P, NP, D])
        sm = m.sb("l1_sum", [P, GT])
        rstd = m.sb("l1_rstd", [P, GT])
        sc = m.sb("l1_scores", [P, NP, P])
        pt = m.sb("l1_probs_t", [P, NP, P])
        mx = m.sb("l1_max", [P, NP])
        rs = m.sb("l1_sums", [P, NP])
        hidden = m.sb("l1_h", [P, 2, GT])
        sq = q
        o = h_in
        ps_h, ps_o, ps_n, ps_f = psum("l1_psh", 2), psum("l1_pso", 2), psum("l1_psn", 2), psum("l1_psf", 2)

        s_x1, s_ffo = sg.get("x1_ready"), sg.get("ff_out_read")
        s_qm, s_km, s_vm = sg.get("q_products"), sg.get("k_products"), sg.get("v_products")
        s_q, s_k, s_v = sg.get("q_ready"), sg.get("k_ready"), sg.get("v_ready")
        s_sm = sg.get("score_products")
        s_sc, s_mx, s_sub, s_exp = sg.get("scores_masked"), sg.get("scores_max"), sg.get("scores_minus_max"), sg.get("probs_exp")
        s_rs, s_rr, s_pn = sg.get("probs_summed"), sg.get("probs_inverted"), sg.get("probs_ready")
        s_tm, s_pt = sg.get("probs_transposed"), sg.get("probs_t_ready")
        s_om, s_o = sg.get("attn_products"), sg.get("attn_ready")
        s_pm = sg.get("proj_products")

        def no_wait(e, n):
            pass

        def x1_ready(e, n):
            e.wait_ge(s_x1.sem, s_x1.after(n))

        par = {}
        n1 = Norm(nc, m, sg, K, "norm1", lambda n: x_all[:, n], no_wait, lambda n: h_in[:], no_wait, False, 1,
                  K["l1a_scale"], K["l1a_shift"], ps_n, (sm, xc, sq, rstd))
        n2 = Norm(nc, m, sg, K, "norm2", lambda n: x1[:, par["w"]], x1_ready, lambda n: min_[:, par["w"]], no_wait, False, 1,
                  K["l1b_scale"], K["l1b_shift"], ps_n, (sm, xc, sq, rstd))

        def m_ready(pe, n):
            pe.wait_ge(n2.done.sem, n2.done.after(n))

        def out_read(pe, n):
            s_ffo.wait_before(pe, n)

        ff = FeedForward(nc, sg, K["l1_w1"], K["l1_w2"], bias[:, V["L1_cond_mlp_b1"]:], ACT.Gelu,
                         lambda u: min_[:, u], m_ready, ps_h, ps_o, hidden, out_read)
        block = ctx.enter_context(nc.Block())

        @block.sync
        def _(sp):
            for dst, src in K["weights_l2"] + K["weights_l3"]:
                sp.dma_start(dst, src).then_inc(K["w_loaded"], 16)
            sp.wait_ge(K["w_loaded"], 16 * len(K["weights_first"] + K["weights_l2"] + K["weights_l3"]))

        @block.tensor
        def _(pe):
            def project(ps, w, rhs):
                for t in range(KT):
                    for k in range(KT):
                        last = nc.tensor.matmul(ps[:, t], w[:, k, t * P:(t + 1) * P], rhs[:, k], start=(k == 0), stop=(k == KT - 1))
                return last

            def queries_keys(pe, n):
                pe.wait_ge(n1.done.sem, n1.done.after(n))
                project(ps_f, K["l1_wq"], h_in).then_inc(s_qm.sem, 1)
                project(ps_n, K["l1_wk"], h_in).then_inc(s_km.sem, 1)

            def values(pe, n):
                pe.wait_ge(s_q.sem, s_q.after(n))
                for p in range(NP):
                    dst = ps_f[:, p // 2, (p % 2) * D:(p % 2 + 1) * D]
                    for k in range(KT):
                        last = nc.tensor.matmul(dst, h_in[:, k, p * P:(p + 1) * P], K["l1_wv"][:, k], start=(k == 0), stop=(k == KT - 1))
                last.then_inc(s_vm.sem, 1)

            def scores(pe, n):
                pe.wait_ge(s_k.sem, s_k.after(n))
                for p in range(NP):
                    c = slice(p * P, (p + 1) * P)
                    for k in range(KT):
                        last = nc.tensor.matmul(ps_n[:, 0, c], q[:, k, c], k_[:, k, c], start=(k == 0), stop=(k == KT - 1))
                last.then_inc(s_sm.sem, 1)

            def transposes(pe, n):
                pe.wait_ge(s_pn.sem, s_pn.after(n))
                for p in range(NP):
                    last = nc.tensor.transpose(ps_n[:, 1, p * P:(p + 1) * P], sc[:, p], K["ident"])
                last.then_inc(s_tm.sem, 1)

            def attend(pe, n):
                pe.wait_ge(s_pt.sem, s_pt.after(n))
                pe.wait_ge(s_v.sem, s_v.after(n))
                for p in range(NP):
                    for t in range(KT):
                        last = nc.tensor.matmul(ps_f[:, t, p * P:(p + 1) * P], vt[:, p, t * P:(t + 1) * P], pt[:, p], start=True, stop=True)
                last.then_inc(s_om.sem, 1)

            def out_project(pe, n):
                pe.wait_ge(s_o.sem, s_o.after(n))
                project(ps_n, K["l1_wo"], o).then_inc(s_pm.sem, 1)

            steps = [n1.tensor_variance, queries_keys, values, scores, transposes, attend, out_project, n2.tensor_variance]

            def front(n):
                for s in steps:
                    s(pe, n)

            def both(n, f, u):
                for j in range(HJ):
                    ff.tensor_up(pe, n, j, u)
                    if j >= 1:
                        ff.tensor_down(pe, n, j - 1)
                    if f is not None:
                        steps[j](pe, f)
                ff.tensor_down(pe, n, HJ - 1)

            two_stage(pe, front, both, lambda n: both(n, None, 1))

        @block.scalar
        def _(act):
            def keys(act, n):
                act.wait_ge(s_km.sem, s_km.after(n))
                b0 = V["L1_cond_k_b"]
                for t in range(KT):
                    last = nc.scalar.activation(k_[:, t], ps_n[:, t], ACT.Identity, bias=bias[:, b0 + t:b0 + t + 1])
                last.then_inc(s_k.sem, 1)

            def values(act, n):
                act.wait_ge(s_vm.sem, s_vm.after(n))
                nc.scalar.copy(vt[:].rearrange("p a n -> p (a n)"), ps_f[:].rearrange("p a n -> p (a n)")).then_inc(s_v.sem, 1)

            def exps(act, n):
                act.wait_ge(s_sub.sem, s_sub.after(n))
                nc.scalar.activation(sc[:], sc[:], ACT.Exp).then_inc(s_exp.sem, 1)

            def probs_t(act, n):
                act.wait_ge(s_tm.sem, s_tm.after(n))
                nc.scalar.copy(pt[:].rearrange("p a n -> p (a n)"), ps_n[:, 1]).then_inc(s_pt.sem, 1)

            def first_norm(act, n):
                n1.scalar_square(act, n)
                n1.scalar_root(act, n)

            steps = [first_norm, keys, values, exps, probs_t, None, n2.scalar_square, n2.scalar_root]

            def front(n):
                par["w"] = 0
                for s in steps:
                    if s:
                        s(act, n)

            def both(n, f, u):
                par["w"] = 1 - u
                for j in range(HJ):
                    ff.scalar_activate(act, n, j)
                    if f is not None and steps[j]:
                        steps[j](act, f)

            two_stage(act, front, both, lambda n: both(n, None, 1))

        @block.gpsimd
        def _(pool):
            def front(n):
                n1.pool_sum(pool, n)
                n2.pool_sum(pool, n)

            front(0)
            with pool.Fori(1, NG) as i:
                front(i)

        @block.vector
        def _(v):
            def front(n, w):
                par["w"] = w
                n1.vector_apply(v, n)
                v.wait_ge(s_qm.sem, s_qm.after(n))
                b0 = V["L1_cond_q_b"]
                for t in range(KT):
                    last = nc.vector.tensor_scalar(q[:, t], ps_f[:, t], bias[:, b0 + t:b0 + t + 1], None, ALU.add)
                last.then_inc(s_q.sem, 1)
                v.wait_ge(s_sm.sem, s_sm.after(n))
                mask = K["block_mask"].unsqueeze(1).broadcast_to([P, NP, P])
                ps = ps_n[:, 0].rearrange("p (a n) -> p a n", n=P)
                nc.vector.scalar_tensor_tensor(sc[:], ps, SCALE, mask, ALU.mult, ALU.add).then_inc(s_sc.sem, 1)
                v.wait_ge(s_sc.sem, s_sc.after(n))
                nc.vector.reduce_max(mx[:], sc[:], AX.X).then_inc(s_mx.sem, 1)
                v.wait_ge(s_mx.sem, s_mx.after(n))
                nc.vector.tensor_tensor(sc[:], sc[:], mx[:].unsqueeze(2).broadcast_to([P, NP, P]), ALU.subtract).then_inc(s_sub.sem, 1)
                v.wait_ge(s_exp.sem, s_exp.after(n))
                nc.vector.reduce_sum(rs[:], sc[:], AX.X).then_inc(s_rs.sem, 1)
                v.wait_ge(s_rs.sem, s_rs.after(n))
                nc.vector.reciprocal(rs[:], rs[:]).then_inc(s_rr.sem, 1)
                v.wait_ge(s_rr.sem, s_rr.after(n))
                nc.vector.tensor_tensor(sc[:], sc[:], rs[:].unsqueeze(2).broadcast_to([P, NP, P]), ALU.mult).then_inc(s_pn.sem, 1)
                v.wait_ge(s_om.sem, s_om.after(n))
                b0 = V["L1_cond_v_b"]
                for t in range(KT):
                    last = nc.vector.tensor_scalar(o[:, t], ps_f[:, t], bias[:, b0 + t:b0 + t + 1], None, ALU.add)
                last.then_inc(s_o.sem, 1)
                v.wait_ge(s_pm.sem, s_pm.after(n))
                b0 = V["L1_cond_proj_b"]
                for t in range(KT):
                    last = nc.vector.scalar_tensor_tensor(x1[:, w, t], ps_n[:, t], bias[:, b0 + t:b0 + t + 1], x_all[:, n, t], ALU.add, ALU.add)
                last.then_inc(s_x1.sem, 1)
                n2.vector_apply(v, n)

            def back(n, u):
                v.wait_ge(ff.down.sem, ff.down.after(n))
                b0 = V["L1_cond_mlp_b2"]
                for t in range(KT):
                    last = nc.vector.scalar_tensor_tensor(x_all[:, n, t], ps_o[:, t], bias[:, b0 + t:b0 + t + 1], x1[:, u, t], ALU.add, ALU.add)
                last.then_inc(s_ffo.sem, 1)

            def both(n, f, u):
                front(f, 1 - u)
                back(n, u)

            two_stage(v, lambda n: front(n, 0), both, lambda n: back(n, 1))
    sg.close_layer(NG)


def layer2(nc, mem, sg, T, K):
    x_all = K["x"]
    V, bias = K["vec_at"], K["bias"]
    NGT, H, L, DIRS = 20, 16, 11, 2
    DH = D // H
    HT = H // KT
    CH = 4
    R = CH * NGT
    NC = H // CH
    KC = HT * NGT
    NEG = 9000000000000000.0
    with ExitStack() as ctx:
        m = Mem(nc, ctx)
        psum = lambda name, n: ctx.enter_context(nc.psum_tensor(name, [P, n, GT], F32))
        sf = m.sb("l2_self", [P, 2, KT, GT])
        sfk = m.sb("l2_self_plain", [P, KT, GT])
        q = m.sb("l2_queries", [P, 2, DIRS * KT, GT])
        kt = m.sb("l2_k", [P, DIRS * KT, GB * NGT])
        vt = m.sb("l2_v", [P, DIRS * KT, GB * NGT])
        key_blocks = m.sb("l2_key_blocks", [P, 2, 2, DIRS * KT, KC])
        value_cols = m.sb("l2_value_columns", [P, 2, DIRS * KT, KC])
        value_blocks = m.sb("l2_value_blocks", [P, 4, NC, CH * DH])
        sc = m.sb("l2_scores", [P, 2, DIRS, H * NGT])
        pt = m.sb("l2_probs_t", [P, DIRS, NC, P])
        adj_i = m.sb("l2_adj", [P, NP * DIRS * NGT * L], I32)
        adj = adj_i[:].bitcast(F32)
        keep = m.sb("l2_keep", [P, 2, NP, DIRS * NGT])
        lbias = m.sb("l2_label_bias", [P, 2, NP, DIRS * NGT])
        nz = m.sb("l2_nonzero", [P, GT])
        mx = m.sb("l2_max", [P, 2, DIRS * H])
        rs = m.sb("l2_sums", [P, 2, DIRS * H])
        ot = m.sb("l2_out", [P, KT, P])
        adj_neg = m.sb("l2_neg", [P, NP * DIRS * NGT])
        kb = m.sb("l2_scaled_key_bias", [P, DIRS * KT])
        ob = m.sb("l2_out_bias", [P, KT])
        ps_s, ps_r, ps_o, ps_f = psum("l2_pss", 2), psum("l2_psr", 3), psum("l2_pso", 1), psum("l2_psf", 2)

        g_bias = sg.get("l2_biases")
        g_adj_in, g_adj_f = sg.get("adj_loaded", 16), sg.get("adj_converted")
        g_cnt, g_keep, g_neg = sg.get("adj_counted"), sg.get("keep_ready"), sg.get("neg_ready")
        g_lab, g_labs, g_lbias = sg.get("adj_weighted"), sg.get("adj_labels_summed"), sg.get("label_bias_ready")
        g_negs = sg.get("neg_made")
        g_xs, g_rm, g_nz, g_tq = sg.get("row_summed"), sg.get("row_sum_products"), sg.get("row_nonzero"), sg.get("cond_part_ready")
        g_sm, g_sf, g_sfb = sg.get("self_products"), sg.get("self_ready"), sg.get("self_biased")
        g_fm, g_fe = sg.get("front_products", 8), sg.get("front_evacuated", 8)
        g_kb, g_vc = sg.get("key_blocks_ready", NP), sg.get("value_columns_ready", NP)
        g_s, g_a0, g_a1, g_mx = (sg.get(x, NP) for x in ("score_products", "scores_masked", "scores_biased", "scores_max"))
        g_sub, g_exp, g_rs, g_rr, g_pn = (sg.get(x, NP) for x in ("scores_minus_max", "probs_exp", "probs_summed", "probs_inverted", "probs_ready"))
        g_t, g_pt = sg.get("probs_transposed", 2 * NP), sg.get("probs_t_ready", 2 * NP)
        g_v, g_vb = sg.get("values_transposed", 4 * NP), sg.get("value_blocks_ready", 4 * NP)
        g_o, g_or, g_x = sg.get("attn_products", NP), sg.get("attn_ready", NP), sg.get("x_updated", NP)

        w_at = lambda name, d, k: K[name][:, d * KT + k]
        block = ctx.enter_context(nc.Block())

        @block.sync
        def _(sp):
            def load_adj(n):
                g_adj_in.wait(sp, n, -1)
                g_labs.wait(sp, n, -1)
                sp.dma_start(adj_i[:], T["adj"][n]).then_inc(g_adj_in.sem, 16)

            for n in range(NG):
                load_adj(n)

        FRONT = ([("q", d, t) for d in range(DIRS) for t in range(KT)] + [("k", d, None) for d in range(DIRS)]
                 + [("v", d, None) for d in range(DIRS)])
        SLOTS = [["row"], ["self", 0], [1], [2], [3, 4], [5, 6, 7]]

        def first_tokens(a):
            return a.rearrange("p (b s) -> p b s", s=S)[:, :, 0:NGT]

        @block.tensor
        def _(pe):
            def front_step(n, w, step):
                if step == "row":
                    g_xs.wait(pe, n)
                    g_fe.wait(pe, n, -1)
                    nc.tensor.matmul(ps_f[:, 0], K["ones"][:], nz[:], start=True, stop=True).then_inc(g_rm.sem, 1)
                elif step == "self":
                    g_nz.wait(pe, n)
                    for t in range(KT):
                        for k in range(KT):
                            last = nc.tensor.matmul(ps_f[:, t], K["l2_ws"][:, k, t * P:(t + 1) * P], x_all[:, n, k], start=(k == 0), stop=(k == KT - 1))
                    last.then_inc(g_sm.sem, 1)
                else:
                    kind, d, t = FRONT[step]
                    g_sf.wait(pe, n)
                    if step >= 2:
                        g_fe.wait(pe, n, step - 2)
                    ps = ps_f[:, step % 2]
                    if kind == "q":
                        for k in range(KT):
                            last = nc.tensor.matmul(ps, w_at("l2_wq", d, k)[:, t * P:(t + 1) * P], sfk[:, k], start=(k == 0), stop=(k == KT - 1))
                    else:
                        for t in range(KT):
                            dst = ps[:, t * GB * NGT:(t + 1) * GB * NGT]
                            for k in range(KT):
                                last = nc.tensor.matmul(dst, w_at("l2_w" + kind, d, k)[:, t * P:(t + 1) * P], first_tokens(sfk[:, k]), start=(k == 0), stop=(k == KT - 1))
                    last.then_inc(g_fm.sem, 1)

            def scores(n, u, p):
                g_kb.wait(pe, n, p)
                g_fe.wait(pe, n, 3)
                g_a0.wait(pe, n, p - 1)
                for d in range(DIRS):
                    for b in range(2):
                        for t in range(KT):
                            tok = (2 * p + b) * S
                            last = nc.tensor.matmul(ps_s[b * S:(b + 1) * S, d, t * KC:(t + 1) * KC], q[:, u, d * KT + t, tok:tok + S],
                                                    key_blocks[:, p % 2, b, d * KT + t], start=True, stop=True)
                last.then_inc(g_s.sem, 1)

            def probs_t(n, p):
                g_pn.wait(pe, n, p)
                for d in range(DIRS):
                    g_vb.wait(pe, n, 4 * (p - 1) + 1 + d)
                    for i in range(NC):
                        last = nc.tensor.transpose(ps_r[0:R, d, i * P:(i + 1) * P], sc[:, p % 2, d, i * R:(i + 1) * R], K["ident"])
                    last.then_inc(g_t.sem, 1)

            def values_t(n, p):
                g_vc.wait(pe, n, p)
                for i in range(4):
                    b, d = i // 2, i % 2
                    if i == 0:
                        g_vb.wait(pe, n, 4 * (p - 1) + 3)
                    elif i == 3:
                        g_vb.wait(pe, n, 4 * p)
                    else:
                        g_pt.wait(pe, n, 2 * p + i - 1)
                    for c in range(NC):
                        a = value_cols[:, b, d * KT + c // 2, (c % 2) * R:(c % 2 + 1) * R]
                        last = nc.tensor.transpose(ps_r[0:R, (i + 2) % 3, c * P:(c + 1) * P], a, K["ident"])
                    last.then_inc(g_v.sem, 1)

            def attend(n, p):
                g_vb.wait(pe, n, 4 * p + 3)
                g_pt.wait(pe, n, 2 * p + 1)
                g_or.wait(pe, n, p - 1)
                for b in range(2):
                    for c in range(NC):
                        for d in range(DIRS):
                            half = (c % 2) * CH * DH
                            last = nc.tensor.matmul(ps_o[half:half + CH * DH, 0, c // 2 * P + b * S:c // 2 * P + (b + 1) * S], value_blocks[0:R, 2 * b + d, c],
                                                    pt[0:R, d, c, b * S:(b + 1) * S], start=(d == 0), stop=(d == DIRS - 1))
                last.then_inc(g_o.sem, 1)

            def both(n, f, u):
                for s in range(NP + 2):
                    if s < NP:
                        scores(n, u, s)
                    if s >= 2:
                        probs_t(n, s - 2)
                        values_t(n, s - 2)
                        attend(n, s - 2)
                    if f is not None:
                        for step in SLOTS[s]:
                            front_step(f, 1 - u, step)

            def front(n):
                for slot in SLOTS:
                    for step in slot:
                        front_step(n, 0, step)

            two_stage(pe, front, both, lambda n: both(n, None, 1))

        @block.scalar
        def _(act):
            def front_step(n, w, step):
                if step == "row":
                    g_adj_in.wait(act, n)
                    nc.scalar.copy(adj, adj_i[:]).then_inc(g_adj_f.sem, 1)
                elif step != "self":
                    kind, d, t = FRONT[step]
                    g_fm.wait(act, n, step)
                    ps = ps_f[:, step % 2]
                    if kind == "q":
                        if step == 0:
                            g_s.wait(act, n, -NP - 1)
                        b0 = V["L2_cond_bq"] + d * KT + t
                        last = nc.scalar.activation(q[:, w, d * KT + t], ps, ACT.Identity, bias=bias[:, b0:b0 + 1])
                    elif kind == "k":
                        if d == 0:
                            g_kb.wait(act, n, -1)
                        for t in range(KT):
                            j = d * KT + t
                            last = nc.scalar.activation(kt[:, j], ps[:, t * GB * NGT:(t + 1) * GB * NGT], ACT.Identity,
                                                        bias=kb[:, j:j + 1], scale=1.0 / np.sqrt(DH))
                    else:
                        if d == 0:
                            g_vc.wait(act, n, -1)
                        last = nc.scalar.copy(vt[:, d * KT:(d + 1) * KT].rearrange("p a n -> p (a n)"), ps[:, 0:KT * GB * NGT])
                    last.then_inc(g_fe.sem, 1)

            def probs_t(n, p):
                g_o.wait(act, n, p - 1)
                for d in range(DIRS):
                    g_t.wait(act, n, 2 * p + d)
                    nc.scalar.copy(pt[0:R, d].rearrange("p a n -> p (a n)"), ps_r[0:R, d]).then_inc(g_pt.sem, 1)

            def exps(n, p):
                g_sub.wait(act, n, p)
                nc.scalar.activation(sc[:, p % 2], sc[:, p % 2], ACT.Exp).then_inc(g_exp.sem, 1)

            def both(n, f, u):
                for s in range(NP + 2):
                    if s >= 2:
                        probs_t(n, s - 2)
                    if s < NP:
                        exps(n, s)
                    if f is not None:
                        for step in SLOTS[s]:
                            front_step(f, 1 - u, step)

            def front(n):
                for slot in SLOTS:
                    for step in slot:
                        front_step(n, 0, step)

            g_bias.wait(act, 0)
            two_stage(act, front, both, lambda n: both(n, None, 1))

        @block.gpsimd
        def _(pool):
            def front_step(n, step):
                if step == "row":
                    g_adj_f.wait(pool, n)
                    g_cnt.wait(pool, n)
                    a = adj.rearrange("p (a l) -> p a l", l=L)
                    w = K["label_w"].unsqueeze(1).broadcast_to([P, NP * DIRS * NGT, L])
                    nc.gpsimd.tensor_tensor(a, a, w, ALU.mult).then_inc(g_lab.sem, 1)

            def blocks(n, p):
                g_fe.wait(pool, n, 5)
                g_s.wait(pool, n, p - 2)
                mask = K["head_mask"].unsqueeze(1).unsqueeze(3).broadcast_to([P, DIRS * KT, HT, NGT])
                for b in range(2):
                    at = (2 * p + b) * NGT
                    a = kt[:, :, at:at + NGT].unsqueeze(2).broadcast_to([P, DIRS * KT, HT, NGT])
                    last = nc.gpsimd.tensor_tensor(key_blocks[:, p % 2, b].rearrange("p j (h m) -> p j h m", m=NGT), a, mask, ALU.mult)
                last.then_inc(g_kb.sem, 1)

            def value_columns(n, p):
                g_fe.wait(pool, n, 7)
                g_v.wait(pool, n, 4 * (p - 1) + 3)
                mask = K["head_mask"].unsqueeze(1).unsqueeze(3).broadcast_to([P, DIRS * KT, HT, NGT])
                for b in range(2):
                    at = (2 * p + b) * NGT
                    a = vt[:, :, at:at + NGT].unsqueeze(2).broadcast_to([P, DIRS * KT, HT, NGT])
                    last = nc.gpsimd.tensor_tensor(value_cols[:, b].rearrange("p j (h m) -> p j h m", m=NGT), a, mask, ALU.mult)
                last.then_inc(g_vc.sem, 1)

            def normalise(n, p):
                g_rr.wait(pool, n, p)
                r = rs[:, p % 2].unsqueeze(2).broadcast_to([P, DIRS * H, NGT])
                a = sc[:, p % 2].rearrange("p d (h m) -> p (d h) m", m=NGT)
                nc.gpsimd.tensor_tensor(a, a, r, ALU.mult).then_inc(g_pn.sem, 1)

            def both(n, f, u):
                blocks(n, 0)
                for s in range(NP + 1):
                    if s + 1 < NP:
                        blocks(n, s + 1)
                    if s >= 1:
                        normalise(n, s - 1)
                        value_columns(n, s - 1)
                    if f is not None and s == 0:
                        front_step(f, "row")

            two_stage(pool, lambda n: front_step(n, "row"), both, lambda n: both(n, None, 1))

        @block.vector
        def _(v):
            b0 = V["L2_cond_bk"]
            nc.vector.tensor_scalar(kb[:], bias[:, b0:b0 + DIRS * KT], 1.0 / np.sqrt(DH), None, ALU.mult)
            b0 = V["L2_cond_bout"]
            nc.vector.tensor_tensor(ob[:], bias[:, b0:b0 + KT], bias[:, b0 + KT:b0 + 2 * KT], ALU.add).then_inc(g_bias.sem, 1)
            g_bias.wait(v, 0)

            def front_step(n, w, step):
                if step == "row":
                    g_sm.wait(v, n, -1)
                    g_tq.wait(v, n, -1)
                    nc.vector.tensor_tensor(nz[:], x_all[:, n, 0], x_all[:, n, 1], ALU.add).then_inc(g_xs.sem, 1)
                    a = adj.rearrange("p (a l) -> p a l", l=L)
                    k, lb = (t[:, w].rearrange("p a n -> p (a n)") for t in (keep, lbias))
                    g_adj_f.wait(v, n)
                    nc.vector.reduce_sum(k, a, AX.X).then_inc(g_cnt.sem, 1)
                    g_cnt.wait(v, n)
                    nc.vector.tensor_scalar(k, k, 0.0, None, ALU.is_gt).then_inc(g_keep.sem, 1)
                    g_rm.wait(v, n)
                    nc.vector.tensor_scalar(nz[:], ps_f[:, 0], 0.0, None, ALU.not_equal).then_inc(g_nz.sem, 1)
                    g_nz.wait(v, n)
                    nzb = nz[:].rearrange("p (b s) -> p b s", s=S).unsqueeze(1).broadcast_to([P, KT, GB, S])
                    nc.vector.tensor_tensor(tokens(sf[:, w]), nzb, per_batch(K["l2_q"], bass.ds(n * GB, GB)), ALU.mult).then_inc(g_tq.sem, 1)
                    g_lab.wait(v, n)
                    nc.vector.reduce_sum(lb, a, AX.X).then_inc(g_labs.sem, 1)
                    g_labs.wait(v, n)
                    nc.vector.tensor_scalar(lb, lb, K["label_b"], None, ALU.add).then_inc(g_neg.sem, 1)
                    g_neg.wait(v, n)
                    nc.vector.tensor_scalar(adj_neg[:], k, 1.0, NEG, ALU.subtract, ALU.mult).then_inc(g_negs.sem, 1)
                    g_negs.wait(v, n)
                    nc.vector.tensor_tensor(lb, lb, adj_neg[:], ALU.add).then_inc(g_lbias.sem, 1)
                elif step == "self":
                    g_sm.wait(v, n)
                    g_fm.wait(v, n, -1)
                    b0 = V["L2_cond_b_self"]
                    for t in range(KT):
                        last = nc.vector.scalar_tensor_tensor(sfk[:, t], ps_f[:, t], bias[:, b0 + t:b0 + t + 1], sf[:, w, t], ALU.add, ALU.add)
                    last.then_inc(g_sf.sem, 1)
                    g_sf.wait(v, n)
                    for t in range(KT):
                        last = nc.vector.tensor_scalar(sf[:, w, t], sfk[:, t], ob[:, t:t + 1], None, ALU.add)
                    last.then_inc(g_sfb.sem, 1)

            def softmax_a(n, u, p):
                g_s.wait(v, n, p)
                g_t.wait(v, n, 2 * (p - 2) + 1)
                c = slice(0, DIRS * NGT)
                a = sc[:, p % 2].rearrange("p d (h m) -> p d h m", m=NGT)
                ps = ps_s[:, :, 0:H * NGT].rearrange("p d (h m) -> p d h m", m=NGT)
                spread = lambda t: t[:, u, p].rearrange("p (d m) -> p d m", m=NGT).unsqueeze(2).broadcast_to([P, DIRS, H, NGT])
                nc.vector.tensor_tensor(a, ps, spread(keep), ALU.mult).then_inc(g_a0.sem, 1)
                g_a0.wait(v, n, p)
                nc.vector.tensor_tensor(a, a, spread(lbias), ALU.add).then_inc(g_a1.sem, 1)
                g_a1.wait(v, n, p)
                flat = sc[:, p % 2].rearrange("p d (h m) -> p (d h) m", m=NGT)
                nc.vector.reduce_max(mx[:, p % 2], flat, AX.X).then_inc(g_mx.sem, 1)
                g_mx.wait(v, n, p)
                nc.vector.tensor_tensor(flat, flat, mx[:, p % 2].unsqueeze(2).broadcast_to([P, DIRS * H, NGT]), ALU.subtract).then_inc(g_sub.sem, 1)

            def softmax_b(n, p):
                g_exp.wait(v, n, p)
                flat = sc[:, p % 2].rearrange("p d (h m) -> p (d h) m", m=NGT)
                nc.vector.reduce_sum(rs[:, p % 2], flat, AX.X).then_inc(g_rs.sem, 1)
                g_rs.wait(v, n, p)
                nc.vector.reciprocal(rs[:, p % 2], rs[:, p % 2]).then_inc(g_rr.sem, 1)

            def value_rows(n, p):
                g_o.wait(v, n, p - 1)
                for i in range(4):
                    g_v.wait(v, n, 4 * p + i)
                    a = ps_r[0:R, (i + 2) % 3].rearrange("p (t a n) -> p t a n", t=KT, a=4)[:, :, 0:4:3]
                    nc.vector.tensor_copy(value_blocks[0:R, i].rearrange("p (t c) n -> p t c n", t=KT), a).then_inc(g_vb.sem, 1)

            def outputs(n, u, p):
                g_o.wait(v, n, p)
                c = slice(p * P, (p + 1) * P)
                g_x.wait(v, n, p - 1)
                nc.vector.tensor_tensor(ot[:], ps_o[:, 0, 0:KT * P].rearrange("p (t n) -> p t n", n=P), sf[:, u, :, c], ALU.add).then_inc(g_or.sem, 1)
                g_or.wait(v, n, p)
                nc.vector.scalar_tensor_tensor(x_all[:, n, :, c], ot[:], 0.0, x_all[:, n, :, c], ALU.max, ALU.add).then_inc(g_x.sem, 1)

            def both(n, f, u):
                for s in range(NP + 2):
                    if s >= 3:
                        outputs(n, u, s - 3)
                    if s < NP:
                        softmax_a(n, u, s)
                    if 1 <= s <= NP:
                        softmax_b(n, s - 1)
                    if s >= 2:
                        value_rows(n, s - 2)
                    if f is not None:
                        for step in SLOTS[s]:
                            front_step(f, 1 - u, step)
                outputs(n, u, NP - 1)

            def front(n):
                front_step(n, 0, "row")
                front_step(n, 0, "self")

            two_stage(v, front, both, lambda n: both(n, None, 1))
            g_x.wait(v, NG - 1)
    sg.close_layer(NG)



L3_GAPS = [["square1"], ["var1"], [], ["qk0"], ["qk1"], ["perm0", "qk2"],
           ["perm1", "qk3"], ["perm2"], ["perm3"], ["v"], ["kb0"], ["s0", "kb1"],
           ["s1"], ["t0", "kb2"], ["pv0"], ["ot0", "s2"], ["t1", "kb3"], ["pv1"],
           ["ot1", "s3"], ["t2"], ["pv2", "ot2"], ["t3"], ["pv3", "ot3"], ["proj", "var2"]]


def layer3(nc, mem, sg, T, K):
    x_all = K["x"]
    V, bias = K["vec_at"], K["bias"]
    H = 16
    DH = D // H
    HT = H // KT
    HP = H // 2
    with ExitStack() as ctx:
        m = Mem(nc, ctx)
        psum = lambda name, n: ctx.enter_context(nc.psum_tensor(name, [P, n, GT], F32))
        x1 = m.sb("l3_x1", [P, 2, KT, GT])
        min_ = m.sb("l3_m", [P, 2, KT, GT])
        h_in = m.sb("l3_in", [P, KT, GT])
        xc = m.sb("l3_xc", [P, KT, GT])
        sq = m.sb("l3_sq", [P, KT, GT])
        sm = m.sb("l3_sum", [P, GT])
        rstd = m.sb("l3_rstd", [P, GT])
        raw = m.sb("l3_raw", [P, 2, GT])
        rc = m.sb("l3_cosine_part", [P, 2, GT])
        rsn = m.sb("l3_sine_part", [P, 2, GT])
        qk = m.sb("l3_qk", [P, 2 * KT, GT])
        vb = m.sb("l3_value_blocks", [P, 2, NP, D])
        key_blocks = m.sb("l3_key_blocks", [P, 2, 2, KT, HT * S])
        sc = m.sb("l3_scores", [P, 2, H, S])
        pt = m.sb("l3_probs_t", [P, HP, P])
        on = m.sb("l3_attn", [P, 2, D])
        mx = m.sb("l3_max", [P, 2, H])
        rs = m.sb("l3_sums", [P, 2, H])
        sig = m.sb("l3_silu", [P, GT])
        hidden = m.sb("l3_h", [P, 2, GT])
        o = h_in
        ps_ag, ps_o, ps_x, ps_y = psum("l3_psag", 2), psum("l3_pso", 2), psum("l3_psx", 2), psum("l3_psy", 2)

        s_x1, s_ffo = sg.get("x1_ready"), sg.get("ff_out_read")
        g_vz = sg.get("value_blocks_cleared")
        g_qk, g_raw = sg.get("q_products", 4), sg.get("q_ready", 4)
        g_perm, g_rs, g_rc, g_rope = (sg.get(x, 4) for x in ("qk_swapped", "qk_sine_part", "qk_cosine_part", "qk_rotated"))
        g_vm, g_vb = sg.get("v_products"), sg.get("v_ready")
        g_kb, g_s, g_mx, g_sub, g_exp = (sg.get(x, NP) for x in ("key_blocks_ready", "score_products", "scores_max", "scores_minus_max", "probs_exp"))
        g_sum, g_rr, g_t, g_pt = (sg.get(x, NP) for x in ("probs_summed", "probs_inverted", "probs_transposed", "probs_t_ready"))
        g_pv, g_on, g_ot, g_o = (sg.get(x, NP) for x in ("attn_products", "attn_normalised", "attn_transposed", "attn_ready"))
        g_pm = sg.get("proj_products")
        f_a, f_g, f_sig, f_h, f_down = (sg.get(x, HJ) for x in ("ff_a_products", "ff_gate_products", "ff_activated", "ff_hidden_ready", "ff_down"))

        def no_wait(e, n):
            pass

        def x1_ready(e, n):
            s_x1.wait(e, n)

        par = {}
        n1 = Norm(nc, m, sg, K, "norm1", lambda n: x_all[:, n], no_wait, lambda n: h_in[:], no_wait, False, 2,
                  K["l3a_scale"], K["l3a_shift"], ps_y, (sm, xc, sq, rstd))
        n2 = Norm(nc, m, sg, K, "norm2", lambda n: x1[:, par["w"]], x1_ready, lambda n: min_[:, par["w"]], no_wait, False, 2,
                  K["l3b_scale"], K["l3b_shift"], ps_y, (sm, xc, sq, rstd))
        block = ctx.enter_context(nc.Block())

        def run(engine, front_step, ff_part, back_end=None):
            def front(n):
                for gap in L3_GAPS:
                    for step in gap:
                        front_step(n, 0, step)

            def both(n, f, u):
                for g, gap in enumerate(L3_GAPS):
                    ff_part(n, u, g // 3, g % 3)
                    if f is not None:
                        for step in gap:
                            front_step(f, 1 - u, step)
                if back_end:
                    back_end(n, u)

            two_stage(engine, front, both, lambda n: both(n, None, 1))

        @block.sync
        def _(sp):
            for n in range(NG):
                s_ffo.wait(sp, n)
                sp.dma_start(T["out"][:, n], x_all[:, n]).then_inc(K["x_stored"], 16)
            sp.wait_ge(K["x_stored"], 16 * NG)

        @block.tensor
        def _(pe):
            w_qkv, w_fc, w_fo = K["l3_qkv"], K["l3_fc"], K["l3_fo"]

            def front_step(n, w, step):
                kind, p = step[:-1], int(step[-1]) if step[-1].isdigit() else None
                if step == "var1":
                    n1.tensor_variance(pe, n)
                elif step == "var2":
                    n2.tensor_variance(pe, n)
                elif kind == "qk":
                    n1.done.wait(pe, n)
                    if p >= 2:
                        g_raw.wait(pe, n, p - 2)
                    for k in range(KT):
                        last = nc.tensor.matmul(ps_x[:, p % 2], w_qkv[:, k, p * P:(p + 1) * P], h_in[:, k], start=(k == 0), stop=(k == KT - 1))
                    last.then_inc(g_qk.sem, 1)
                elif kind == "perm":
                    g_raw.wait(pe, n, p)
                    if p >= 2:
                        g_rs.wait(pe, n, p - 2)
                    nc.tensor.matmul(ps_y[:, p % 2], K["swap"], raw[:, p % 2], start=True, stop=True).then_inc(g_perm.sem, 1)
                elif step == "v":
                    g_raw.wait(pe, n, 3)
                    for a in range(NP):
                        dst = ps_x[:, a // 2, (a % 2) * D:(a % 2 + 1) * D]
                        for k in range(KT):
                            last = nc.tensor.matmul(dst, h_in[:, k, a * P:(a + 1) * P], w_qkv[:, k, 2 * D:3 * D], start=(k == 0), stop=(k == KT - 1))
                    last.then_inc(g_vm.sem, 1)
                elif kind == "s":
                    g_kb.wait(pe, n, p)
                    if p == 0:
                        g_vb.wait(pe, n)
                    else:
                        g_sub.wait(pe, n, p - 1)
                    for b in range(2):
                        at = (2 * p + b) * S
                        for t in range(KT):
                            last = nc.tensor.matmul(ps_x[b * S:(b + 1) * S, t], qk[:, t, at:at + S], key_blocks[:, p % 2, b, t], start=True, stop=True)
                    last.then_inc(g_s.sem, 1)
                elif kind == "t":
                    g_exp.wait(pe, n, p)
                    if p == 0:
                        g_rs.wait(pe, n, 3)
                    else:
                        g_o.wait(pe, n, p - 1)
                    for i in range(HP):
                        last = nc.tensor.transpose(ps_y[:, i // 4, (i % 4) * P:(i % 4 + 1) * P], sc[:, p % 2, 2 * i:2 * i + 2].rearrange("p h m -> p (h m)"), K["ident"])
                    last.then_inc(g_t.sem, 1)
                elif kind == "pv":
                    g_pt.wait(pe, n, p)
                    for b in range(2):
                        for i in range(HP):
                            c = slice(i * 2 * DH, (i + 1) * 2 * DH)
                            last = nc.tensor.matmul(ps_y[b * S:(b + 1) * S, 0, c], pt[:, i, b * S:(b + 1) * S], vb[:, b, p, c], start=True, stop=True)
                    last.then_inc(g_pv.sem, 1)
                elif kind == "ot":
                    g_on.wait(pe, n, p)
                    for t in range(KT):
                        last = nc.tensor.transpose(ps_y[:, 1, t * P:(t + 1) * P], on[:, p % 2, t * P:(t + 1) * P], K["ident"])
                    last.then_inc(g_ot.sem, 1)
                elif step == "proj":
                    g_o.wait(pe, n)
                    g_sub.wait(pe, n)
                    for t in range(KT):
                        for k in range(KT):
                            last = nc.tensor.matmul(ps_x[:, t], K["l3_ao"][:, k, t * P:(t + 1) * P], o[:, k], start=(k == 0), stop=(k == KT - 1))
                    last.then_inc(g_pm.sem, 1)

            def down(n, j):
                f_h.wait(pe, n, j)
                if j == 0:
                    s_ffo.wait(pe, n, -1)
                for t in range(KT):
                    last = nc.tensor.matmul(ps_o[:, t], w_fo[:, j, t * P:(t + 1) * P], hidden[:, j % 2], start=(j == 0), stop=(j == HJ - 1))
                last.then_inc(f_down.sem, 1)

            def ff_part(n, u, j, part):
                if part == 2:
                    if j >= 1:
                        down(n, j - 1)
                    return
                if j == 0 and part == 0:
                    n2.done.wait(pe, n)
                if part == 0:
                    f_h.wait(pe, n, j - 1)
                for k in range(KT):
                    c = (part * HJ + j) * P
                    last = nc.tensor.matmul(ps_ag[:, part], w_fc[:, k, c:c + P], min_[:, u, k], start=(k == 0), stop=(k == KT - 1))
                last.then_inc((f_g if part else f_a).sem, 1)

            run(pe, front_step, ff_part, lambda n, u: down(n, HJ - 1))

        @block.scalar
        def _(act):
            def front_step(n, w, step):
                par["w"] = w
                kind, p = step[:-1], int(step[-1]) if step[-1].isdigit() else None
                if step == "square1":
                    n1.scalar_square(act, n)
                elif step == "var1":
                    n1.scalar_root(act, n)
                elif step == "var2":
                    n2.scalar_square(act, n)
                    n2.scalar_root(act, n)
                elif kind == "qk":
                    g_qk.wait(act, n, p)
                    if p >= 2:
                        g_rc.wait(act, n, p - 2)
                        g_perm.wait(act, n, p - 2)
                    b0 = V["L3_cond_b_qkv"] + p
                    nc.scalar.activation(raw[:, p % 2], ps_x[:, p % 2], ACT.Identity, bias=bias[:, b0:b0 + 1]).then_inc(g_raw.sem, 1)
                elif kind == "s":
                    g_sub.wait(act, n, p)
                    nc.scalar.activation(sc[:, p % 2], sc[:, p % 2], ACT.Exp, scale=1.0 / np.sqrt(DH)).then_inc(g_exp.sem, 1)
                elif kind == "t":
                    g_t.wait(act, n, p)
                    nc.scalar.copy(pt[:].rearrange("p a n -> p (a n)"), ps_y[:].rearrange("p a n -> p (a n)")).then_inc(g_pt.sem, 1)
                elif kind == "ot":
                    g_ot.wait(act, n, p)
                    b0 = V["L3_cond_b_qkv"] + 2 * KT
                    for t in range(KT):
                        last = nc.scalar.activation(o[:, t, p * P:(p + 1) * P], ps_y[:, 1, t * P:(t + 1) * P], ACT.Identity, bias=bias[:, b0 + t:b0 + t + 1])
                    last.then_inc(g_o.sem, 1)

            def ff_part(n, u, j, part):
                if part == 1:
                    f_g.wait(act, n, j)
                    f_h.wait(act, n, j - 1)
                    b0 = V["L3_cond_b_fc"] + HJ + j
                    nc.scalar.activation(sig[:], ps_ag[:, 1], ACT.Silu, bias=bias[:, b0:b0 + 1]).then_inc(f_sig.sem, 1)

            run(act, front_step, ff_part)

        @block.gpsimd
        def _(pool):
            def front_step(n, w, step):
                kind, p = step[:-1], int(step[-1]) if step[-1].isdigit() else None
                if step == "square1":
                    n1.pool_sum(pool, n)
                elif step == "var2":
                    n2.pool_sum(pool, n)
                elif kind == "perm":
                    g_raw.wait(pool, n, p)
                    cos = K["rope_cos"].unsqueeze(1).broadcast_to([P, GB, S])
                    b3 = lambda a: a.rearrange("p (b s) -> p b s", s=S)
                    nc.gpsimd.tensor_tensor(b3(rc[:, p % 2]), b3(raw[:, p % 2]), cos, ALU.mult).then_inc(g_rc.sem, 1)
                    g_rc.wait(pool, n, p)
                    g_rs.wait(pool, n, p)
                    nc.gpsimd.tensor_tensor(qk[:, p], rc[:, p % 2], rsn[:, p % 2], ALU.add).then_inc(g_rope.sem, 1)
                elif kind == "kb":
                    g_rope.wait(pool, n)
                    g_s.wait(pool, n, p - 2)
                    mask = K["head_mask"].unsqueeze(2).broadcast_to([P, HT, S])
                    for b in range(2):
                        at = (2 * p + b) * S
                        for t in range(KT):
                            a = qk[:, KT + t, at:at + S].unsqueeze(1).broadcast_to([P, HT, S])
                            last = nc.gpsimd.tensor_tensor(key_blocks[:, p % 2, b, t].rearrange("p (h s) -> p h s", s=S), a, mask, ALU.mult)
                    last.then_inc(g_kb.sem, 1)

            run(pool, front_step, lambda n, u, j, part: None)

        @block.vector
        def _(v):
            nc.vector.memset(vb[:], 0.0).then_inc(g_vz.sem, 1)
            g_vz.wait(v, 0)

            def sums(n, p):
                g_exp.wait(v, n, p)
                nc.vector.reduce_sum(rs[:, p % 2], sc[:, p % 2], AX.X).then_inc(g_sum.sem, 1)
                g_sum.wait(v, n, p)
                nc.vector.reciprocal(rs[:, p % 2], rs[:, p % 2]).then_inc(g_rr.sem, 1)

            def front_step(n, w, step):
                par["w"] = w
                kind, p = step[:-1], int(step[-1]) if step[-1].isdigit() else None
                if step == "var1":
                    n1.vector_apply(v, n)
                elif kind == "perm":
                    g_perm.wait(v, n, p)
                    g_rope.wait(v, n, p - 2)
                    sin = K["rope_sin"].unsqueeze(1).broadcast_to([P, GB, S])
                    b3 = lambda a: a.rearrange("p (b s) -> p b s", s=S)
                    nc.vector.tensor_tensor(b3(rsn[:, p % 2]), b3(ps_y[:, p % 2]), sin, ALU.mult).then_inc(g_rs.sem, 1)
                elif step == "v":
                    g_vm.wait(v, n)
                    src = ps_x[:].rearrange("p k (a h e d) -> p (k a) h e d", a=2, e=2, d=DH)
                    dst = vb[:].rearrange("p b a (h e d) -> p b a h e d", e=2, d=DH)
                    for b in range(2):
                        for e in range(2):
                            last = nc.vector.tensor_copy(dst[e * S:(e + 1) * S, b, :, :, e], src[b * S:(b + 1) * S, :, :, e])
                    last.then_inc(g_vb.sem, 1)
                elif kind == "s":
                    g_s.wait(v, n, p)
                    ps = ps_x[:].rearrange("p t (h s) -> p (t h) s", s=S)
                    nc.vector.reduce_max(mx[:, p % 2], ps, AX.X).then_inc(g_mx.sem, 1)
                    g_mx.wait(v, n, p)
                    nc.vector.tensor_tensor(sc[:, p % 2], ps, mx[:, p % 2].unsqueeze(2).broadcast_to([P, H, S]), ALU.subtract).then_inc(g_sub.sem, 1)
                elif kind == "t":
                    sums(n, p)
                elif kind == "pv":
                    g_pv.wait(v, n, p)
                    g_rr.wait(v, n, p)
                    r = rs[:, p % 2].unsqueeze(2).broadcast_to([P, H, DH])
                    nc.vector.tensor_tensor(on[:, p % 2].rearrange("p (h d) -> p h d", d=DH), ps_y[:, 0, 0:D].rearrange("p (h d) -> p h d", d=DH), r,
                                            ALU.mult).then_inc(g_on.sem, 1)
                elif step == "proj":
                    g_pm.wait(v, n)
                    b0 = V["L3_cond_b_ao"]
                    for t in range(KT):
                        last = nc.vector.scalar_tensor_tensor(x1[:, w, t], ps_x[:, t], bias[:, b0 + t:b0 + t + 1], x_all[:, n, t], ALU.add, ALU.add)
                    last.then_inc(s_x1.sem, 1)
                elif step == "var2":
                    n2.vector_apply(v, n)

            def ff_part(n, u, j, part):
                if part == 2:
                    f_a.wait(v, n, j)
                    f_sig.wait(v, n, j)
                    f_down.wait(v, n, j - 2)
                    b0 = V["L3_cond_b_fc"] + j
                    nc.vector.scalar_tensor_tensor(hidden[:, j % 2], ps_ag[:, 0], bias[:, b0:b0 + 1], sig[:], ALU.add, ALU.mult).then_inc(f_h.sem, 1)

            def back_end(n, u):
                f_down.wait(v, n)
                b0 = V["L3_cond_b_fo"]
                for t in range(KT):
                    last = nc.vector.scalar_tensor_tensor(x_all[:, n, t], ps_o[:, t], bias[:, b0 + t:b0 + t + 1], x1[:, u, t], ALU.add, ALU.add)
                last.then_inc(s_ffo.sem, 1)

            run(v, front_step, ff_part, back_end)
    sg.close_layer(NG)



VECTORS = ["L0_cond_bm", "L0_cond_bc", "L0_cond_D_diag", "L0_cond_b1", "L0_cond_b2",
           "L1_cond_norm1_w", "L1_cond_film1_b", "L1_cond_q_b", "L1_cond_k_b", "L1_cond_v_b", "L1_cond_proj_b",
           "L1_cond_norm2_w", "L1_cond_film2_b", "L1_cond_mlp_b1", "L1_cond_mlp_b2",
           "L2_cond_b_self", "L2_cond_bq", "L2_cond_bk", "L2_cond_bout",
           "L3_cond_g1", "L3_cond_g2", "L3_cond_b_qkv", "L3_cond_b_ao", "L3_cond_b_fc", "L3_cond_b_fo",
           "L3_cond_b_t1", "L3_cond_b_t2"]


def program(nc, T, vec_at):
    ctx = ExitStack()
    with ctx:
        mem = Mem(nc, ctx)
        sg = Signals(mem)
        K = {"vec_at": vec_at}
        K["x"] = mem.sb("x_all", [P, NG, KT, GT])
        K["bias"] = mem.sb("bias_columns", [P, T["vectors"].shape[1]])
        K["consts"] = mem.sb("constants", [P, T["consts"].shape[1]])
        K["sign"] = K["consts"][:, 0:1]
        K["eps"] = mem.sb("eps", [P, 4])
        K["ones"] = mem.sb("ones", [P, P])
        K["mean"] = mem.sb("mean_weights", [P, P])
        for name in ("l3a_scale", "l3a_shift", "l3b_scale", "l3b_shift"):
            K[name] = mem.sb(name, [P, KT, B])
        K["x_loaded"], K["w_loaded"] = mem.sem("x_loaded"), mem.sem("weights_loaded")
        arena = mem.sb("weights_a", [P, 2 * KT * FF + 2 * HJ * D])
        c2 = KT * FF
        K["l0_w1"] = arena[:, 0:c2].rearrange("p (k n) -> p k n", k=KT)
        K["l0_w2"] = arena[:, c2:c2 + HJ * D].rearrange("p (k n) -> p k n", k=HJ)
        K["s5_b"] = arena[:, c2 + HJ * D:c2 + HJ * D + 512].rearrange("p (c k n) -> p c k n", c=2, k=KT)
        K["s5_c"] = arena[:, c2 + HJ * D + 512:c2 + HJ * D + 1024].rearrange("p (c n) -> p c n", c=2)
        K["weights_first"] = [
            (K["l0_w1"], T["L0_cond_W1"].rearrange("(k p) n -> p k n", p=P)),
            (K["l0_w2"], T["L0_cond_W2"].rearrange("(k p) n -> p k n", p=P)),
            (K["s5_b"][:], T["s5_b"][:]), (K["s5_c"][:], T["s5_c"][:])]
        def weight(m, name, src, tiles, cols):
            K[name] = m.sb(name, [P, tiles, cols])
            return K[name][:], T[src].rearrange("(k p) n -> p k n", p=P)

        c = K["consts"]
        K["ident"], K["block_mask"], K["value_mask"] = (c[:, 32 + i * P:32 + (i + 1) * P] for i in range(3))
        K["head_mask"], K["label_w"], K["label_b"] = c[:, 1:9], c[:, 9:20], c[:, 20:21]
        K["swap"] = c[:, 32 + 3 * P:32 + 4 * P]
        K["rope_cos"], K["rope_sin"] = (c[:, 32 + 4 * P + i * S:32 + 4 * P + (i + 1) * S] for i in range(2))
        K["x_stored"] = mem.sem("x_stored")
        K["weights_l3"], at = [], 0
        for name, src, tiles, cols in (("l3_qkv", "L3_cond_w_qkv", KT, 3 * D), ("l3_ao", "L3_cond_w_ao", KT, D),
                                       ("l3_fc", "L3_cond_w_fc", KT, 2 * FF), ("l3_fo", "L3_cond_w_fo", HJ, D)):
            K[name] = arena[:, at:at + tiles * cols].rearrange("p (k n) -> p k n", k=tiles)
            at += tiles * cols
            K["weights_l3"].append((K[name], T[src].rearrange("(k p) n -> p k n", p=P)))
        with ExitStack() as l2:
            m2 = Mem(nc, l2)
            K["l2_q"] = m2.sb("l2_q", [P, KT, B])
            K["weights_l2"] = [weight(m2, "l2_ws", "WselfT_v", KT, D), weight(m2, "l2_wq", "l2_WqT", 2 * KT, D),
                               weight(m2, "l2_wk", "l2_WkT", 2 * KT, D), weight(m2, "l2_wv", "l2_WoutT", 2 * KT, D)]
            with ExitStack() as l1:
                m1 = Mem(nc, l1)
                for name in ("l0_shift", "l0_scale", "l0_gate", "l0_gate_ff", "l0_scale_ff", "l0_shift_ff",
                             "l1a_scale", "l1a_shift", "l1b_scale", "l1b_shift"):
                    K[name] = m1.sb(name, [P, KT, B])
                K["turn_in"], K["turn_out"], K["decay"] = m1.sb("turn_in", [P, 2, S]), m1.sb("turn_out", [P, 2, S]), m1.sb("decay", [P, GT])
                K["weights_first"] += [weight(m1, "l1_w1", "L1_cond_mlp_w1", KT, FF), weight(m1, "l1_w2", "L1_cond_mlp_w2", HJ, D)]
                K["weights_first"] += [weight(m1, "l1_w" + c, f"L1_cond_{w}_w", KT, D) for c, w in zip("qkvo", ("q", "k", "v", "proj"))]
                conditioning(nc, mem, sg, T, K)
                layer0(nc, mem, sg, T, K)
                layer1(nc, mem, sg, T, K)
            layer2(nc, mem, sg, T, K)
        layer3(nc, mem, sg, T, K)


def kernel(**inputs):
    import concourse.bacc as bacc
    from concourse.bass_utils import run_bass_kernel_spmd

    a = {k: np.asarray(v) for k, v in inputs.items()}
    lay = {}
    lay["x"] = a["x"].reshape(NG, GT, KT, P).transpose(3, 0, 2, 1)
    lay["condT"] = a["cond_1024"].T.reshape(KT, P, B).transpose(1, 0, 2)
    cols, vec_at, at = [], {}, 0
    for name in VECTORS:
        c = a[name].reshape(-1, P).T
        vec_at[name] = at
        at += c.shape[1]
        cols.append(c)
    lay["vectors"] = np.concatenate(cols, 1)
    lam = np.stack([a["L0_cond_Lam_re"], a["L0_cond_Lam_im"], a["L0_cond_log_step"]], 1)
    lay["lam"] = np.concatenate([lam, lam], 0)
    b_re, b_im = a["L0_cond_B_re"].T, a["L0_cond_B_im"].T
    pair = np.stack([np.concatenate([b_re, b_im], 1), np.concatenate([b_im, b_re], 1)])
    lay["s5_b"] = pair.reshape(2, KT, P, P).transpose(2, 0, 1, 3)
    c_re, c_im = a["L0_cond_C_re"].T, a["L0_cond_C_im"].T
    lay["s5_c"] = np.stack([np.concatenate([c_re, c_im], 0), np.concatenate([c_im, c_re], 0)]).transpose(1, 0, 2)
    lay["WselfT_q"] = a["L2_cond_W_self"].T[D:]
    lanes = np.arange(P)
    consts = np.zeros((P, 32 + 4 * P + 2 * S), np.float32)
    consts[:NS, 0], consts[NS:, 0] = -1.0, 1.0
    consts[:, 1:9] = lanes[:, None] // 16 == np.arange(8)
    consts[:, 9:20] = a["L2_cond_w_bias"]
    consts[:, 20] = a["L2_cond_b_bias"]
    consts[:, 32:32 + P] = np.eye(P)
    consts[:, 32 + P:32 + 2 * P] = np.where(lanes[:, None] // S == lanes // S, 0.0, -1e30)
    consts[:, 32 + 2 * P:32 + 3 * P] = lanes[:, None] // 10 == lanes // 16
    consts[:, 32 + 3 * P:32 + 4 * P] = np.eye(P)[lanes ^ 1]
    inv_freq = (np.float32(1.0) / np.power(np.float32(10000.0), np.arange(0, 16, 2, dtype=np.float32) / np.float32(16))).astype(np.float32)
    angle = np.arange(S, dtype=np.float32)[None] * inv_freq[lanes % 16 // 2][:, None]
    consts[:, 32 + 4 * P:32 + 4 * P + S] = np.cos(angle)
    consts[:, 32 + 4 * P + S:] = np.sin(angle) * np.where(lanes % 2, 1.0, -1.0)[:, None]
    adj = a["mask_BxSxSx11_ik0"]
    both = np.stack([adj[:, :, :20], adj[:, :20].transpose(0, 2, 1, 3)], 2)
    lay["adj"] = both.reshape(NG, NP, P, -1).transpose(0, 2, 1, 3).reshape(NG, P, -1)
    lay["WselfT_v"] = a["L2_cond_W_self"].T[:D]
    lay["l2_WqT"] = a["L2_cond_Wq"].transpose(0, 2, 1).reshape(2 * D, D)
    lay["l2_WkT"] = a["L2_cond_Wk"].transpose(0, 2, 1).reshape(2 * D, D)
    lay["l2_WoutT"] = a["L2_cond_Wout"].reshape(2, D, D).transpose(0, 2, 1).reshape(2 * D, D)
    lay["consts"] = consts
    for name in ("L0_cond_Wm", "L0_cond_Wc", "L1_cond_film1_w", "L1_cond_film2_w", "L3_cond_w_t1", "L3_cond_w_t2", "L0_cond_W1", "L0_cond_W2",
                 "L1_cond_mlp_w1", "L1_cond_mlp_w2", "L1_cond_q_w", "L1_cond_k_w", "L1_cond_v_w", "L1_cond_proj_w",
                 "L3_cond_w_qkv", "L3_cond_w_ao", "L3_cond_w_fc", "L3_cond_w_fo"):
        lay[name] = a[name]

    nc = bacc.Bacc("TRN2", target_bir_lowering=False, num_devices=1)
    arrays, T = {}, {}
    for name, v in lay.items():
        v = np.ascontiguousarray(v)
        arrays[f"in_{name}"] = v
        T[name] = nc.dram_tensor(f"in_{name}", v.shape, mybir.dt.from_np(v.dtype), kind="ExternalInput").ap()
    T["out"] = nc.dram_tensor("out_x", (P, NG, KT, GT), F32, kind="ExternalOutput").ap()
    program(nc, T, vec_at)
    r = run_bass_kernel_spmd(nc, [arrays], core_ids=[0])
    out = np.asarray(r.results[0]["out_x"])
    return out.transpose(1, 3, 2, 0).reshape(B, S, D)
```

```python
import concourse.bass as bass
from concourse import mybir
from contextlib import ExitStack
import numpy as np

F32 = mybir.dt.float32
I32 = mybir.dt.int32
ALU = mybir.AluOpType
ACT = mybir.ActivationFunctionType
AX = mybir.AxisListType

P = 128
B, S, D = 128, 64, 256
KT = D // P
GB = 8
GT = GB * S
NG = B // GB
NP = GB // 2
FF = 4 * D
HJ = FF // P
NS = 64
LAYERS = 4


class Mem:

    def __init__(self, nc, ctx):
        self.nc, self.ctx = nc, ctx

    def sb(self, name, shape, dt=F32):
        return self.ctx.enter_context(self.nc.sbuf_tensor(name, shape, dt))

    def sem(self, name):
        return self.ctx.enter_context(self.nc.semaphore(name))


def per_batch(table, batches):
    return table[:, :, batches].unsqueeze(3).broadcast_to([P, KT, GB, S])


def tokens(t):
    return t.rearrange("p k (b s) -> p k b s", s=S)


class Signal:

    def __init__(self, sem, base, per_group):
        self.sem, self.base, self.k = sem, base, per_group

    def after(self, n, j=None):
        return self.base + n * self.k + (self.k if j is None else j + 1)

    def wait(self, engine, n, j=None):
        value = self.after(n, j)
        if not isinstance(value, int) or value > 0:
            engine.wait_ge(self.sem, value)

    def wait_before(self, engine, n):
        value = self.base + n * self.k
        if not isinstance(value, int) or value > 0:
            engine.wait_ge(self.sem, value)


class Signals:

    def __init__(self, mem):
        self.mem, self.sems, self.base, self.open = mem, {}, {}, {}

    def get(self, name, per_group=1):
        if name not in self.sems:
            self.sems[name], self.base[name] = self.mem.sem(name), 0
        self.open[name] = per_group
        return Signal(self.sems[name], self.base[name], per_group)

    def close_layer(self, groups):
        for name, k in self.open.items():
            self.base[name] += groups * k
        self.open = {}



class Chain:

    def __init__(self, engine, signals, name):
        if name not in signals.sems:
            signals.sems[name], signals.base[name] = signals.mem.sem(name), 0
        self.engine, self.signals, self.name = engine, signals, name

    def __call__(self, instruction):
        instruction.then_inc(self.signals.sems[self.name], 1)
        self.signals.base[self.name] += 1
        self.engine.wait_ge(self.signals.sems[self.name], self.signals.base[self.name])

    def value(self):
        return self.signals.base[self.name]


def conditioning(nc, mem, sg, T, K):
    x_all = K["x"]
    stage = x_all.rearrange("p g k t -> p (g k t)")
    at = [6 * KT * GT]

    def staged(cols):
        a = stage[:, at[0]:at[0] + cols]
        at[0] += cols
        return a

    w_mod = staged(KT * 6 * D).rearrange("p (k n) -> p k n", k=KT)
    w_c = staged(KT * 2 * D).rearrange("p (k n) -> p k n", k=KT)
    w_f1 = staged(KT * 2 * D).rearrange("p (k n) -> p k n", k=KT)
    w_f2 = staged(KT * 2 * D).rearrange("p (k n) -> p k n", k=KT)
    w_sq = staged(KT * D).rearrange("p (k n) -> p k n", k=KT)
    w_t1 = staged(KT * 2 * D).rearrange("p (k n) -> p k n", k=KT)
    w_t2 = staged(KT * 4 * D).rearrange("p (k n) -> p k n", k=KT)
    loads = [(w_mod, "L0_cond_Wm"), (w_c, "L0_cond_Wc"), (w_f1, "L1_cond_film1_w"), (w_f2, "L1_cond_film2_w"),
             (w_sq, "WselfT_q"), (w_t1, "L3_cond_w_t1"), (w_t2, "L3_cond_w_t2")]

    with ExitStack() as ctx:
        m = Mem(nc, ctx)
        cond = m.sb("condT", [P, KT, B])
        raw = m.sb("raw_mod", [P, 12, B])
        cvec = m.sb("cvec", [P, 12])
        q = m.sb("svec", [P, 24])
        cs = m.sb("cs_tab", [P, S])
        sn = m.sb("sn_tab", [P, S])
        tmp = m.sb("tmp_tab", [P, 2, S])
        tp = m.sb("tp_act", [P, KT, B])
        tg = m.sb("tp_gate", [P, KT, B])
        ps = ctx.enter_context(nc.psum_tensor("ps_mod", [P, 4, 4, B], F32))
        d_load = sg.get("cond_loads", 0)
        n_loads = len(loads) + 4
        s_mm, s_ev = mem.sem("mod_products"), mem.sem("mod_evacuated")
        s_tp, s_swi = mem.sem("swiglu_input"), mem.sem("swiglu_gate")
        sn_ready, sn_done = mem.sem("angle_ready"), mem.sem("sine_done")
        bias = K["bias"]

        jobs = [(w_mod, 0, 4), (w_mod, 4, 4), (w_mod, 8, 4), (w_c, 0, 4), (w_f1, 0, 4), (w_f2, 0, 4), (w_sq, 0, 2),
                (w_t1, 0, 4), (w_t2, 0, 4), (w_t2, 4, 4)]

        block = ctx.enter_context(nc.Block())

        @block.sync
        def _(sp):
            for dst, src in ((cond, T["condT"]), (K["bias"], T["vectors"]), (K["consts"], T["consts"]),
                             (cvec[:, 0:3], T["lam"])):
                sp.dma_start(dst[:], src[:]).then_inc(d_load.sem, 16)
            for dst, name in loads:
                sp.dma_start(dst, T[name].rearrange("(k p) n -> p k n", p=P)).then_inc(d_load.sem, 16)
            for g in range(6):
                sp.dma_start(x_all[:, g], T["x"][:, g]).then_inc(K["x_loaded"], 16)
            for dst, src in K["weights_first"]:
                sp.dma_start(dst, src).then_inc(K["w_loaded"], 16)
            sp.wait_ge(K["x_loaded"], 6 * 16)
            sp.wait_ge(K["w_loaded"], 16 * len(K["weights_first"]))

        @block.tensor
        def _(pe):
            pe.wait_ge(d_load.sem, 16 * n_loads)
            for i, (w, first, tiles) in enumerate(jobs):
                if i >= 4:
                    pe.wait_ge(s_ev, i - 3)
                if i == 8:
                    pe.wait_ge(s_swi, 1)
                rhs = tp if i >= 8 else cond
                for t in range(tiles):
                    for k in range(KT):
                        c = (first + t) * P
                        last = nc.tensor.matmul(ps[:, i % 4, t], w[:, k, c:c + P], rhs[:, k], start=(k == 0), stop=(k == KT - 1))
                last.then_inc(s_mm, 1)

        @block.scalar
        def _(act):
            act.wait_ge(d_load.sem, 16 * n_loads)
            act.wait_ge(s_tp, 1)
            nc.scalar.activation(tg[:], tg[:], ACT.Silu).then_inc(s_tp, 1)
            act.wait_ge(sn_ready, 1)
            nc.scalar.activation(q[:, 0:1], cvec[:, 2:3], ACT.Exp).then_inc(sn_done, 1)
            act.wait_ge(sn_ready, 2)
            nc.scalar.activation(q[:, 2:3], q[:, 1:2], ACT.Exp).then_inc(sn_done, 1)
            act.wait_ge(sn_ready, 3)
            nc.scalar.activation(q[:, 6:8], q[:, 4:6], ACT.Sin).then_inc(sn_done, 1)

        @block.vector
        def _(v):
            ch = Chain(v, sg, "vector_chain")
            v.wait_ge(d_load.sem, 16 * n_loads)
            ch(nc.vector.memset(K["minus_half"][:], -0.5))
            ch(nc.vector.memset(K["ones"][:], 1.0))
            ch(nc.vector.memset(K["mean"][:], 1.0 / D))

            def bias_of(col, tiles):
                return bias[:, col:col + tiles].unsqueeze(2).broadcast_to([P, tiles, B])

            def add_bias(i, dst, col, tiles=4, step=1):
                v.wait_ge(s_mm, i + 1)
                nc.vector.tensor_tensor(dst, ps[:, i % 4, 0:tiles], bias_of(col, tiles), ALU.add).then_inc(s_ev, 1)
                v.wait_ge(s_ev, i + 1)

            V = K["vec_at"]
            add_bias(0, raw[:, 0:4], V["L0_cond_bm"])
            add_bias(1, raw[:, 4:8], V["L0_cond_bm"] + 4)
            add_bias(2, raw[:, 8:12], V["L0_cond_bm"] + 8)
            ch(nc.vector.tensor_copy(K["l0_shift"][:], raw[:, 0:2]))
            ch(nc.vector.tensor_scalar_add(K["l0_scale"][:], raw[:, 2:4], 1.0))
            ch(nc.vector.tensor_copy(K["l0_gate"][:], raw[:, 4:6]))
            ch(nc.vector.tensor_copy(K["l0_gate_ff"][:], raw[:, 10:12]))
            add_bias(3, raw[:, 0:4], V["L0_cond_bc"])
            ch(nc.vector.tensor_scalar_add(raw[:, 0:2], raw[:, 0:2], 1.0))
            ch(nc.vector.tensor_scalar_add(raw[:, 8:10], raw[:, 8:10], 1.0))
            ch(nc.vector.tensor_tensor(K["l0_scale_ff"][:], raw[:, 0:2], raw[:, 8:10], ALU.mult))
            ch(nc.vector.tensor_tensor(raw[:, 2:4], raw[:, 2:4], raw[:, 8:10], ALU.mult))
            ch(nc.vector.tensor_tensor(K["l0_shift_ff"][:], raw[:, 2:4], raw[:, 6:8], ALU.add))
            for i, name, norm, film in ((4, "l1a", "L1_cond_norm1_w", "L1_cond_film1_b"), (5, "l1b", "L1_cond_norm2_w", "L1_cond_film2_b")):
                add_bias(i, raw[:, 0:4], V[film])
                ch(nc.vector.tensor_scalar_add(raw[:, 0:2], raw[:, 0:2], 1.0))
                ch(nc.vector.tensor_tensor(K[name + "_scale"][:], raw[:, 0:2], bias_of(V[norm], 2), ALU.mult))
                ch(nc.vector.tensor_copy(K[name + "_shift"][:], raw[:, 2:4]))
            v.wait_ge(s_mm, 7)
            nc.vector.tensor_copy(K["l2_q"][:], ps[:, 6 % 4, 0:2]).then_inc(s_ev, 1)
            v.wait_ge(s_ev, 7)
            add_bias(7, raw[:, 0:4], V["L3_cond_b_t1"])
            ch(nc.vector.tensor_copy(tp[:], raw[:, 0:2]))
            nc.vector.tensor_copy(tg[:], raw[:, 2:4]).then_inc(s_tp, 1)
            v.wait_ge(s_tp, 2)
            nc.vector.tensor_tensor(tp[:], tp[:], tg[:], ALU.mult).then_inc(s_swi, 1)
            for i, name, norm in ((8, "l3a", "L3_cond_g1"), (9, "l3b", "L3_cond_g2")):
                add_bias(i, raw[:, 0:4], V["L3_cond_b_t2"] + 4 * (i - 8))
                ch(nc.vector.tensor_copy(K[name + "_shift"][:], raw[:, 0:2]))
                ch(nc.vector.tensor_scalar_add(raw[:, 2:4], raw[:, 2:4], 1.0))
                ch(nc.vector.tensor_tensor(K[name + "_scale"][:], raw[:, 2:4], bias_of(V[norm], 2), ALU.mult))

            lr, li, sgn = cvec[:, 0:1], cvec[:, 1:2], K["sign"]
            TT, TS = nc.vector.tensor_tensor, nc.vector.tensor_scalar
            nc.vector.memset(q[:, 3:4], 0.0).then_inc(sn_ready, 1)
            v.wait_ge(sn_done, 1)
            TT(q[:, 1:2], lr, q[:, 0:1], ALU.mult).then_inc(sn_ready, 1)
            ch(TT(q[:, 3:4], li, q[:, 0:1], ALU.mult))
            ROUND = 12582912.0
            ch(TS(q[:, 8:9], q[:, 3:4], 1.0 / (2 * np.pi), ROUND, ALU.mult, ALU.add))
            ch(TS(q[:, 8:9], q[:, 8:9], -ROUND, None, ALU.add))
            c1 = 6.28125
            c2 = 0.0019350051879882812
            c3 = 2 * np.pi - c1 - c2
            for c in (c1, c2, c3):
                ch(TS(q[:, 9:10], q[:, 8:9], -c, None, ALU.mult))
                ch(TT(q[:, 3:4], q[:, 3:4], q[:, 9:10], ALU.add))
            ch(TS(q[:, 3:4], q[:, 3:4], float(-np.pi), float(np.pi), ALU.max, ALU.min))
            PI = 3.1415925
            ch(TS(q[:, 4:5], q[:, 3:4], 0.5, None, ALU.mult))
            ch(TS(q[:, 5:6], q[:, 4:5], float(np.pi / 2), PI, ALU.add, ALU.min))
            v.wait_ge(sn_done, 2)
            nc.vector.tensor_scalar_max(q[:, 5:6], q[:, 5:6], 0.0).then_inc(sn_ready, 1)
            v.wait_ge(sn_done, 3)
            s, c = q[:, 10:11], q[:, 11:12]
            ch(TT(s, q[:, 6:7], q[:, 7:8], ALU.mult))
            ch(TS(s, s, 2.0, None, ALU.mult))
            ch(TT(c, q[:, 6:7], q[:, 6:7], ALU.mult))
            ch(TS(c, c, -2.0, 1.0, ALU.mult, ALU.add))
            nr, ni, den, cr, ci = (q[:, k:k + 1] for k in range(12, 17))
            u0, u1 = q[:, 17:18], q[:, 18:19]
            ch(TT(nr, c, q[:, 2:3], ALU.mult))
            ch(TS(nr, nr, -1.0, None, ALU.add))
            ch(TT(ni, s, q[:, 2:3], ALU.mult))
            ch(TT(den, lr, lr, ALU.mult))
            ch(TT(u0, li, li, ALU.mult))
            ch(TT(den, den, u0, ALU.add))
            ch(nc.vector.reciprocal(den, den))
            ch(TT(u0, nr, lr, ALU.mult))
            ch(TT(u1, ni, li, ALU.mult))
            ch(TT(cr, u0, u1, ALU.add))
            ch(TT(cr, cr, den, ALU.mult))
            ch(TT(u0, ni, lr, ALU.mult))
            ch(TT(u1, nr, li, ALU.mult))
            ch(TT(ci, u0, u1, ALU.subtract))
            ch(TT(ci, ci, den, ALU.mult))
            ch(nc.vector.memset(cs[:, 0:1], 1.0))
            ch(nc.vector.memset(sn[:, 0:1], 0.0))
            h = 1
            while h < S:
                ch(TS(cs[:, h:2 * h], cs[:, 0:h], c, None, ALU.mult))
                ch(TS(tmp[:, 0, 0:h], sn[:, 0:h], s, None, ALU.mult))
                ch(TS(sn[:, h:2 * h], sn[:, 0:h], c, None, ALU.mult))
                ch(TS(tmp[:, 1, 0:h], cs[:, 0:h], s, None, ALU.mult))
                ch(TT(cs[:, h:2 * h], cs[:, h:2 * h], tmp[:, 0, 0:h], ALU.subtract))
                ch(TT(sn[:, h:2 * h], sn[:, h:2 * h], tmp[:, 1, 0:h], ALU.add))
                ch(TT(u0, c, s, ALU.mult))
                ch(TT(u1, s, s, ALU.mult))
                ch(TT(c, c, c, ALU.mult))
                ch(TT(c, c, u1, ALU.subtract))
                ch(TS(s, u0, 2.0, None, ALU.mult))
                h *= 2
            ch(TS(K["turn_in"][:, 0], cs[:], cr, None, ALU.mult))
            ch(TS(tmp[:, 0], sn[:], ci, None, ALU.mult))
            ch(TT(K["turn_in"][:, 0], K["turn_in"][:, 0], tmp[:, 0], ALU.add))
            ch(TS(K["turn_in"][:, 1], cs[:], ci, None, ALU.mult))
            ch(TS(tmp[:, 0], sn[:], cr, None, ALU.mult))
            ch(TT(K["turn_in"][:, 1], K["turn_in"][:, 1], tmp[:, 0], ALU.subtract))
            ch(TS(K["turn_in"][:, 1], K["turn_in"][:, 1], sgn, None, ALU.mult))
            ch(TS(K["turn_out"][:, 0], cs[:], sgn, -2.0, ALU.mult, ALU.mult))
            ch(TS(K["turn_out"][:, 1], sn[:], -2.0, None, ALU.mult))
            dec = K["decay"].rearrange("p (b s) -> p b s", s=S)
            ch(nc.vector.memset(K["decay"][:], 1.0))
            ch(TS(K["decay"][:], K["decay"][:], q[:, 2:3], None, ALU.mult))
            ch(nc.vector.memset(dec[:, :, 0:1], 0.0))


class Norm:

    CHUNKS = GT // P

    def __init__(self, nc, sg, K, name, src, src_ready, out, center, eps, scale, shift, ps, buffers):
        self.nc, self.K, self.src, self.src_ready, self.out = nc, K, src, src_ready, out
        self.center, self.eps, self.scale, self.shift, self.ps = center, eps, scale, shift, ps
        self.sum, self.sq, self.inv = buffers
        if center:
            self.summed = sg.get(name + "_summed")
            self.meaned = sg.get(name + "_meaned")
            self.centered = sg.get(name + "_centered")
        self.squared = sg.get(name + "_squared")
        self.squares_summed = sg.get(name + "_squares_summed")
        self.varied = sg.get(name + "_varied")
        self.guarded = sg.get(name + "_guarded")
        self.inverted = sg.get(name + "_inverted")
        self.diagonal = sg.get(name + "_diagonal")
        self.spread = sg.get(name + "_spread")
        self.normed = sg.get(name + "_normed")
        self.scaled = sg.get(name + "_scaled")
        self.done = sg.get(name + "_done")

    def vector_sum(self, v, n, w):
        self.src_ready(v, n)
        x = self.src(n, w)
        self.nc.vector.tensor_tensor(self.sum[:], x[:, 0], x[:, 1], ALU.add).then_inc(self.summed.sem, 1)

    def tensor_mean(self, pe, n, w):
        self.summed.wait(pe, n)
        self.nc.tensor.matmul(self.ps, self.K["mean"][:], self.sum[:], start=True, stop=True).then_inc(self.meaned.sem, 1)

    def vector_center(self, v, n, w):
        self.meaned.wait(v, n)
        mean = self.ps.unsqueeze(1).broadcast_to([P, KT, GT])
        self.nc.vector.tensor_tensor(self.out(w), self.src(n, w), mean, ALU.subtract).then_inc(self.centered.sem, 1)

    def scalar_square(self, act, n, w):
        if self.center:
            self.centered.wait(act, n)
            x = self.out(w)
        else:
            self.src_ready(act, n)
            x = self.src(n, w)
        self.squares_summed.wait(act, n, -1)
        self.nc.scalar.activation(self.sq[:], x, ACT.Square).then_inc(self.squared.sem, 1)

    def pool_sum(self, pool, n, w):
        self.squared.wait(pool, n)
        self.spread.wait(pool, n, -1)
        self.nc.gpsimd.tensor_tensor(self.sum[:], self.sq[:, 0], self.sq[:, 1], ALU.add).then_inc(self.squares_summed.sem, 1)

    def tensor_variance(self, pe, n, w):
        self.squares_summed.wait(pe, n)
        for c in range(self.CHUNKS):
            last = self.nc.tensor.matmul(self.ps[:, c:c + 1], self.sum[:, c * P:(c + 1) * P], self.K["mean"][:, 0:1], start=True, stop=True)
        last.then_inc(self.varied.sem, 1)

    def vector_guard(self, v, n, w):
        self.varied.wait(v, n)
        self.inverted.wait(v, n, -1)
        self.nc.vector.tensor_scalar(self.inv[:], self.ps[:, 0:self.CHUNKS], self.eps, None, ALU.add).then_inc(self.guarded.sem, 1)

    def pool_invert(self, pool, n, w):
        self.guarded.wait(pool, n)
        half = self.K["minus_half"][:, 0:self.CHUNKS]
        self.nc.gpsimd.tensor_tensor(self.inv[:], self.inv[:], half, ALU.pow).then_inc(self.inverted.sem, 1)

    def vector_diagonal(self, v, n, w):
        self.inverted.wait(v, n)
        shape = [P, self.CHUNKS, P]
        self.nc.vector.tensor_tensor(self.sum[:].rearrange("p (c t) -> p c t", t=P), self.K["ident"].unsqueeze(1).broadcast_to(shape),
                                     self.inv[:].unsqueeze(2).broadcast_to(shape), ALU.mult).then_inc(self.diagonal.sem, 1)

    def tensor_spread(self, pe, n, w):
        self.diagonal.wait(pe, n)
        self.nc.tensor.matmul(self.ps, self.K["ones"][:], self.sum[:], start=True, stop=True).then_inc(self.spread.sem, 1)

    def vector_apply(self, v, n, w):
        self.spread.wait(v, n)
        rstd = self.ps.unsqueeze(1).broadcast_to([P, KT, GT])
        out, bs = self.out(w), bass.ds(n * GB, GB)
        x = out if self.center else self.src(n, w)
        self.nc.vector.tensor_tensor(out, x, rstd, ALU.mult).then_inc(self.normed.sem, 1)
        self.normed.wait(v, n)
        self.nc.vector.tensor_tensor(tokens(out), tokens(out), per_batch(self.scale, bs), ALU.mult).then_inc(self.scaled.sem, 1)
        self.scaled.wait(v, n)
        self.nc.vector.tensor_tensor(tokens(out), tokens(out), per_batch(self.shift, bs), ALU.add).then_inc(self.done.sem, 1)

    def steps(self, who, name):
        own = {"pe": ("mean", "variance", "spread"), "act": ("square",), "pool": ("sum", "invert"),
               "dve": ("sum", "center", "guard", "diagonal", "apply")}[who]
        of = {"mean": self.tensor_mean, "variance": self.tensor_variance, "spread": self.tensor_spread, "square": self.scalar_square,
              "invert": self.pool_invert, "center": self.vector_center, "guard": self.vector_guard, "diagonal": self.vector_diagonal,
              "apply": self.vector_apply, "sum": self.pool_sum if who == "pool" else self.vector_sum}
        if not self.center:
            own = [k for k in own if k not in ("mean", "center") and (who, k) != ("dve", "sum")]
        return {f"{name}.{k}": of[k] for k in own}


class FeedForward:

    def __init__(self, nc, sg, w1, w2, b1, func, m, m_ready, ps_h, ps_o, hidden, out_read):
        self.nc, self.w1, self.w2, self.b1, self.func, self.m, self.m_ready = nc, w1, w2, b1, func, m, m_ready
        self.ps_h, self.ps_o, self.h, self.out_read = ps_h, ps_o, hidden, out_read
        self.up = sg.get("ff_up", HJ)
        self.act = sg.get("ff_activated", HJ)
        self.down = sg.get("ff_down", HJ)

    def tensor_up(self, pe, n, j, u):
        if j == 0:
            self.m_ready(pe, n)
        if j >= 2:
            pe.wait_ge(self.act.sem, self.act.after(n, j - 2))
        else:
            self.act.wait_before(pe, n)
        for k in range(KT):
            last = self.nc.tensor.matmul(self.ps_h[:, j % 2], self.w1[:, k, j * P:(j + 1) * P], self.m(u)[:, k], start=(k == 0), stop=(k == KT - 1))
        last.then_inc(self.up.sem, 1)

    def scalar_activate(self, act, n, j):
        act.wait_ge(self.up.sem, self.up.after(n, j))
        if j >= 2:
            act.wait_ge(self.down.sem, self.down.after(n, j - 2))
        else:
            self.down.wait_before(act, n)
        self.nc.scalar.activation(self.h[:, j % 2], self.ps_h[:, j % 2], self.func, bias=self.b1[:, j:j + 1]).then_inc(self.act.sem, 1)

    def tensor_part(self, pe):
        def part(n, u, g):
            if g % 2 == 0:
                self.tensor_up(pe, n, g // 2, u)
            elif g > 1:
                self.tensor_down(pe, n, g // 2 - 1)
        return part

    def tensor_end(self, pe):
        return lambda n, u: self.tensor_down(pe, n, HJ - 1)

    def scalar_part(self, act):
        def part(n, u, g):
            if g % 2 == 0:
                self.scalar_activate(act, n, g // 2)
        return part

    def tensor_down(self, pe, n, j):
        pe.wait_ge(self.act.sem, self.act.after(n, j))
        if j == 0:
            self.out_read(pe, n)
        for t in range(KT):
            last = self.nc.tensor.matmul(self.ps_o[:, t], self.w2[:, j, t * P:(t + 1) * P], self.h[:, j % 2], start=(j == 0), stop=(j == HJ - 1))
        last.then_inc(self.down.sem, 1)


def two_stage(engine, front, both, back):
    front(0)
    both(0, 1, 0)
    with engine.Fori(1, NG - 2, 2) as i:
        both(i, i + 1, 1)
        both(i + 1, i + 2, 0)
    back(NG - 1)


def three_stage(engine, who, table, steps, part, parts, end=None):
    after = [[name for name, at in table if at.get(who) == g] for g in range(parts)]
    assert sum(map(len, after)) == len(steps), (who, sorted(steps), after)

    def body(n, m, p, u):
        for g in range(parts):
            if n is not None:
                part(n, u, g)
            for name in after[g]:
                group, w = (p, u) if name.startswith("norm1") else (m, 1 - u)
                if group is not None:
                    steps[name](engine, group, w)
        if n is not None and end:
            end(n, u)

    body(None, None, 0, 0)
    body(None, 0, 1, 1)
    body(0, 1, 2, 0)
    with engine.Fori(1, NG - 4, 2) as i:
        body(i, i + 1, i + 2, 1)
        body(i + 1, i + 2, i + 3, 0)
    body(NG - 3, NG - 2, NG - 1, 1)
    body(NG - 2, NG - 1, None, 0)
    body(NG - 1, None, None, 1)


L0_TABLE = [
    ("b", dict(pe=0)), ("turn_in", dict(dve=0, pool=0)), ("norm1.sum", dict(dve=1)), ("scan", dict(dve=1, pool=1)),
    ("c", dict(pe=4)), ("skip", dict(dve=4)), ("norm2.sum", dict(dve=4)),
    ("norm1.mean", dict(pe=6)), ("norm1.center", dict(dve=6)), ("norm1.square", dict(act=7)), ("norm2.mean", dict(pe=7)),
    ("norm2.center", dict(dve=7)), ("norm1.sum", dict(pool=7)), ("norm2.square", dict(act=8)), ("norm2.sum", dict(pool=8)),
    ("norm2.variance", dict(pe=9)), ("norm2.guard", dict(dve=9)), ("norm2.invert", dict(pool=9)),
    ("norm1.variance", dict(pe=9)), ("norm1.guard", dict(dve=9)), ("norm1.invert", dict(pool=9)),
    ("norm2.diagonal", dict(dve=10)), ("norm2.spread", dict(pe=11)), ("norm1.diagonal", dict(dve=10)), ("norm2.apply", dict(dve=11)),
    ("norm1.spread", dict(pe=12)), ("norm1.apply", dict(dve=12)),
]
L1_TABLE = [
    ("qk", dict(pe=0)), ("q", dict(dve=0)), ("k", dict(act=1)), ("v", dict(pe=1, act=2)), ("norm1.square", dict(act=2)), ("norm1.sum", dict(pool=2)),
    ("scores", dict(pe=2)), ("softmax_a", dict(dve=2)), ("exp", dict(act=3)), ("softmax_b", dict(dve=3)),
    ("norm1.variance", dict(pe=4)), ("norm1.guard", dict(dve=4)), ("norm1.invert", dict(pool=4)), ("norm1.diagonal", dict(dve=4)),
    ("norm1.spread", dict(pe=6)), ("transposes", dict(pe=6, act=6)), ("attend", dict(pe=7, dve=7)), ("norm1.apply", dict(dve=8)),
    ("proj", dict(pe=8, dve=8)), ("norm2.square", dict(act=9)), ("norm2.sum", dict(pool=9)),
    ("norm2.variance", dict(pe=10)), ("norm2.guard", dict(dve=10)), ("norm2.invert", dict(pool=10)), ("norm2.diagonal", dict(dve=10)),
    ("norm2.spread", dict(pe=12)), ("norm2.apply", dict(dve=12)),
]


def layer0(nc, mem, sg, T, K):
    x_all = K["x"]
    V, bias = K["vec_at"], K["bias"]
    with ExitStack() as ctx:
        m = Mem(nc, ctx)
        psum = lambda name, n: ctx.enter_context(nc.psum_tensor(name, [P, n, GT], F32))
        x1 = m.sb("l0_x1", [P, 2, KT, GT])
        min_ = m.sb("l0_m", [P, 2, KT, GT])
        u_in = m.sb("l0_u", [P, 2, KT, GT])
        norm_bufs = [(m.sb(f"l0_sum{i}", [P, GT]), m.sb(f"l0_sq{i}", [P, KT, GT]), m.sb(f"l0_inv{i}", [P, Norm.CHUNKS])) for i in range(2)]
        bz = m.sb("l0_bz", [P, 2, GT])
        z = m.sb("l0_z", [P, GT])
        zt = m.sb("l0_zt", [P, 2, GT])
        hidden = m.sb("l0_h", [P, 2, GT])
        ps_h, ps_o, ps_n, ps_f = psum("l0_psh", 2), psum("l0_pso", 2), psum("l0_psn", 2), psum("l0_psf", 2)

        s_u = sg.get("s5_inputs")
        s_turn = sg.get("s5_turned", 2)
        s_tsum = sg.get("s5_turned_summed")
        s_scan = sg.get("s5_scanned")
        s_cos = sg.get("s5_cosine_part")
        s_sin = sg.get("s5_sine_part")
        s_y = sg.get("s5_outputs")
        s_ay = sg.get("s5_skip", 2)
        s_g = sg.get("s5_gated")
        s_x1 = sg.get("x1_ready")
        s_ffo = sg.get("ff_out_read")
        s_xo = sg.get("x_updated")

        def x_loaded(e, n):
            e.wait_ge(K["x_loaded"], (n + 1) * 16)

        def x1_ready(e, n):
            e.wait_ge(s_x1.sem, s_x1.after(n))

        def no_wait(e, n):
            pass

        n1 = Norm(nc, sg, K, "norm1", lambda n, w: x_all[:, n], x_loaded, lambda w: u_in[:, w], True, 1e-5, K["l0_scale"], K["l0_shift"], ps_n[:, 0], norm_bufs[0])
        n2 = Norm(nc, sg, K, "norm2", lambda n, w: x1[:, w], x1_ready, lambda w: min_[:, w], True, 1e-5,
                  K["l0_scale_ff"], K["l0_shift_ff"], ps_n[:, 1], norm_bufs[1])

        def m_ready(pe, n):
            pe.wait_ge(n2.done.sem, n2.done.after(n))

        def out_read(pe, n):
            s_ffo.wait_before(pe, n)

        ff = FeedForward(nc, sg, K["l0_w1"], K["l0_w2"], bias[:, V["L0_cond_b1"]:], ACT.Gelu_apprx_tanh,
                         lambda u: min_[:, u], m_ready, ps_h, ps_o, hidden, out_read)

        def bcast_turn(t, k):
            return t[:, k:k + 1].broadcast_to([P, GB, S])

        bs3 = lambda a: a.rearrange("p (b s) -> p b s", s=S)
        block = ctx.enter_context(nc.Block())

        @block.sync
        def _(sp):
            for g in range(6, NG):
                sp.dma_start(x_all[:, g], T["x"][:, g]).then_inc(K["x_loaded"], 16)
                sp.wait_ge(K["x_loaded"], (g + 1) * 16)

        @block.tensor
        def _(pe):
            def b_products(pe, n, w):
                n1.done.wait(pe, n)
                for c in range(2):
                    for k in range(KT):
                        last = nc.tensor.matmul(ps_f[:, c], K["s5_b"][:, c, k], u_in[:, w, k], start=(k == 0), stop=(k == KT - 1))
                last.then_inc(s_u.sem, 1)

            def c_products(pe, n, w):
                s_cos.wait(pe, n)
                s_sin.wait(pe, n)
                for t in range(KT):
                    for c in range(2):
                        last = nc.tensor.matmul(ps_f[:, t], K["s5_c"][:, c, t * P:(t + 1) * P], zt[:, c], start=(c == 0), stop=(c == 1))
                last.then_inc(s_y.sem, 1)

            steps = {"b": b_products, "c": c_products, **n1.steps("pe", "norm1"), **n2.steps("pe", "norm2")}
            three_stage(pe, "pe", L0_TABLE, steps, ff.tensor_part(pe), 2 * HJ, ff.tensor_end(pe))

        @block.scalar
        def _(act):
            steps = {**n1.steps("act", "norm1"), **n2.steps("act", "norm2")}
            three_stage(act, "act", L0_TABLE, steps, ff.scalar_part(act), 2 * HJ)

        @block.gpsimd
        def _(pool):
            def turned_sum(pool, n, w):
                s_turn.wait(pool, n)
                nc.gpsimd.tensor_tensor(bz[:, 0], bz[:, 0], bz[:, 1], ALU.add).then_inc(s_tsum.sem, 1)

            def sine_part(pool, n, w):
                s_scan.wait(pool, n)
                nc.gpsimd.tensor_tensor(bs3(zt[:, 1]), bs3(z[:]), bcast_turn(K["turn_out"], 1), ALU.mult).then_inc(s_sin.sem, 1)

            steps = {"turn_in": turned_sum, "scan": sine_part, **n1.steps("pool", "norm1"), **n2.steps("pool", "norm2")}
            three_stage(pool, "pool", L0_TABLE, steps, lambda n, u, g: None, 2 * HJ)

        @block.vector
        def _(v):
            def turn_in(v, n, w):
                s_u.wait(v, n)
                for c in range(2):
                    nc.vector.tensor_tensor(bs3(bz[:, c]), bs3(ps_f[:, c]), bcast_turn(K["turn_in"], c), ALU.mult).then_inc(s_turn.sem, 1)

            def scan(v, n, w):
                s_tsum.wait(v, n)
                nc.vector.tensor_tensor_scan(z[:], K["decay"][:], bz[:, 0], 0.0, ALU.mult, ALU.add).then_inc(s_scan.sem, 1)
                s_scan.wait(v, n)
                nc.vector.tensor_tensor(bs3(zt[:, 0]), bs3(z[:]), bcast_turn(K["turn_out"], 0), ALU.mult).then_inc(s_cos.sem, 1)

            def skip(v, n, w):
                s_y.wait(v, n)
                d0 = V["L0_cond_D_diag"]
                for t in range(KT):
                    nc.vector.scalar_tensor_tensor(x1[:, w, t], u_in[:, w, t], bias[:, d0 + t:d0 + t + 1], ps_f[:, t], ALU.mult, ALU.add).then_inc(s_ay.sem, 1)
                s_ay.wait(v, n)
                nc.vector.tensor_tensor(tokens(x1[:, w]), tokens(x1[:, w]), per_batch(K["l0_gate"], bass.ds(n * GB, GB)), ALU.mult).then_inc(s_g.sem, 1)
                s_g.wait(v, n)
                nc.vector.tensor_tensor(x1[:, w], x1[:, w], x_all[:, n], ALU.add).then_inc(s_x1.sem, 1)

            def back(n, u):
                v.wait_ge(ff.down.sem, ff.down.after(n))
                b0 = V["L0_cond_b2"]
                gate = K["l0_gate_ff"]
                for t in range(KT):
                    g = gate[:, t, bass.ds(n * GB, GB)].unsqueeze(2).broadcast_to([P, GB, S])
                    last = nc.vector.scalar_tensor_tensor(bs3(x_all[:, n, t]), bs3(ps_o[:, t]), bias[:, b0 + t:b0 + t + 1], g, ALU.add, ALU.mult)
                last.then_inc(s_ffo.sem, 1)
                v.wait_ge(s_ffo.sem, s_ffo.after(n))
                nc.vector.tensor_tensor(x_all[:, n], x_all[:, n], x1[:, u], ALU.add).then_inc(s_xo.sem, 1)

            steps = {"turn_in": turn_in, "scan": scan, "skip": skip, **n1.steps("dve", "norm1"), **n2.steps("dve", "norm2")}
            three_stage(v, "dve", L0_TABLE, steps, lambda n, u, g: None, 2 * HJ, back)
            v.wait_ge(s_xo.sem, s_xo.after(NG - 1))
    sg.close_layer(NG)


def layer1(nc, mem, sg, T, K):
    x_all = K["x"]
    V, bias = K["vec_at"], K["bias"]
    SCALE = float(D) ** -0.5
    with ExitStack() as ctx:
        m = Mem(nc, ctx)
        psum = lambda name, n: ctx.enter_context(nc.psum_tensor(name, [P, n, GT], F32))
        x1 = m.sb("l1_x1", [P, 2, KT, GT])
        min_ = m.sb("l1_m", [P, 2, KT, GT])
        h_in = m.sb("l1_in", [P, 2, KT, GT])
        norm_bufs = [(m.sb(f"l1_sum{i}", [P, GT]), m.sb(f"l1_sq{i}", [P, KT, GT]), m.sb(f"l1_inv{i}", [P, Norm.CHUNKS])) for i in range(2)]
        q = m.sb("l1_q", [P, KT, GT])
        k_ = m.sb("l1_k", [P, KT, GT])
        vt = m.sb("l1_v", [P, NP, D])
        sc = m.sb("l1_scores", [P, NP, P])
        pt = q[:, 0].rearrange("p (a n) -> p a n", n=P)
        mx = m.sb("l1_max", [P, NP])
        rs = m.sb("l1_sums", [P, NP])
        hidden = m.sb("l1_h", [P, 2, GT])
        ps_h, ps_o, ps_n, ps_f = psum("l1_psh", 2), psum("l1_pso", 2), psum("l1_psn", 2), psum("l1_psf", 2)

        s_x1, s_ffo = sg.get("x1_ready"), sg.get("ff_out_read")
        s_qm, s_km, s_vm = sg.get("q_products", KT), sg.get("k_products", KT), sg.get("v_products")
        s_q, s_k, s_v = sg.get("q_ready", KT), sg.get("k_ready", KT), sg.get("v_ready")
        s_sm = sg.get("score_products")
        s_sc, s_mx, s_sub, s_exp = sg.get("scores_masked"), sg.get("scores_max"), sg.get("scores_minus_max"), sg.get("probs_exp")
        s_rs, s_rr, s_pn = sg.get("probs_summed"), sg.get("probs_inverted"), sg.get("probs_ready")
        s_tm, s_pt = sg.get("probs_transposed"), sg.get("probs_t_ready")
        s_om, s_o = sg.get("attn_products"), sg.get("attn_ready")
        s_pm = sg.get("proj_products")

        def no_wait(e, n):
            pass

        def x1_ready(e, n):
            e.wait_ge(s_x1.sem, s_x1.after(n))

        n1 = Norm(nc, sg, K, "norm1", lambda n, w: x_all[:, n], no_wait, lambda w: h_in[:, w], False, 1e-6,
                  K["l1a_scale"], K["l1a_shift"], ps_n[:, 0], norm_bufs[0])
        n2 = Norm(nc, sg, K, "norm2", lambda n, w: x1[:, w], x1_ready, lambda w: min_[:, w], False, 1e-6,
                  K["l1b_scale"], K["l1b_shift"], ps_n[:, 1], norm_bufs[1])
        ps_a = ps_n[:, 1]

        def m_ready(pe, n):
            pe.wait_ge(n2.done.sem, n2.done.after(n))

        def out_read(pe, n):
            s_ffo.wait_before(pe, n)

        ff = FeedForward(nc, sg, K["l1_w1"], K["l1_w2"], bias[:, V["L1_cond_mlp_b1"]:], ACT.Gelu,
                         lambda u: min_[:, u], m_ready, ps_h, ps_o, hidden, out_read)
        block = ctx.enter_context(nc.Block())

        @block.sync
        def _(sp):
            for dst, src in K["weights_l2"] + K["weights_l3"]:
                sp.dma_start(dst, src).then_inc(K["w_loaded"], 16)
            sp.wait_ge(K["w_loaded"], 16 * len(K["weights_first"] + K["weights_l2"] + K["weights_l3"]))

        @block.tensor
        def _(pe):
            def product(ps, w, rhs, t):
                for k in range(KT):
                    last = nc.tensor.matmul(ps, w[:, k, t * P:(t + 1) * P], rhs[:, k], start=(k == 0), stop=(k == KT - 1))
                return last

            def queries_keys(pe, n, w):
                n1.done.wait(pe, n)
                h = h_in[:, w]
                for t in range(KT):
                    product(ps_f[:, t], K["l1_wq"], h, t).then_inc(s_qm.sem, 1)
                product(ps_a, K["l1_wk"], h, 0).then_inc(s_km.sem, 1)
                s_q.wait(pe, n, 0)
                product(ps_f[:, 0], K["l1_wk"], h, 1).then_inc(s_km.sem, 1)

            def values(pe, n, w):
                s_q.wait(pe, n)
                s_k.wait(pe, n)
                for p in range(NP):
                    dst = ps_f[:, p // 2, (p % 2) * D:(p % 2 + 1) * D]
                    for k in range(KT):
                        last = nc.tensor.matmul(dst, h_in[:, w, k, p * P:(p + 1) * P], K["l1_wv"][:, k], start=(k == 0), stop=(k == KT - 1))
                last.then_inc(s_vm.sem, 1)

            def scores(pe, n, w):
                s_k.wait(pe, n)
                for p in range(NP):
                    c = slice(p * P, (p + 1) * P)
                    for k in range(KT):
                        last = nc.tensor.matmul(ps_a[:, c], q[:, k, c], k_[:, k, c], start=(k == 0), stop=(k == KT - 1))
                last.then_inc(s_sm.sem, 1)

            def transposes(pe, n, w):
                s_pn.wait(pe, n)
                for p in range(NP):
                    last = nc.tensor.transpose(ps_a[:, p * P:(p + 1) * P], sc[:, p], K["ident"])
                last.then_inc(s_tm.sem, 1)

            def attend(pe, n, w):
                s_pt.wait(pe, n)
                s_v.wait(pe, n)
                for p in range(NP):
                    for t in range(KT):
                        last = nc.tensor.matmul(ps_f[:, t, p * P:(p + 1) * P], vt[:, p, t * P:(t + 1) * P], pt[:, p], start=True, stop=True)
                last.then_inc(s_om.sem, 1)

            def out_project(pe, n, w):
                s_o.wait(pe, n)
                for t in range(KT):
                    last = product(ps_f[:, t], K["l1_wo"], h_in[:, w], t)
                last.then_inc(s_pm.sem, 1)

            steps = {"qk": queries_keys, "v": values, "scores": scores, "transposes": transposes, "attend": attend, "proj": out_project,
                     **n1.steps("pe", "norm1"), **n2.steps("pe", "norm2")}
            three_stage(pe, "pe", L1_TABLE, steps, ff.tensor_part(pe), 2 * HJ, ff.tensor_end(pe))

        @block.scalar
        def _(act):
            def keys(act, n, w):
                b0 = V["L1_cond_k_b"]
                for t in range(KT):
                    s_km.wait(act, n, t)
                    nc.scalar.activation(k_[:, t], (ps_a, ps_f[:, 0])[t], ACT.Identity, bias=bias[:, b0 + t:b0 + t + 1]).then_inc(s_k.sem, 1)

            def values(act, n, w):
                s_vm.wait(act, n)
                nc.scalar.copy(vt[:].rearrange("p a n -> p (a n)"), ps_f[:].rearrange("p a n -> p (a n)")).then_inc(s_v.sem, 1)

            def exps(act, n, w):
                s_sub.wait(act, n)
                nc.scalar.activation(sc[:], sc[:], ACT.Exp).then_inc(s_exp.sem, 1)

            def probs_t(act, n, w):
                s_tm.wait(act, n)
                nc.scalar.copy(q[:, 0], ps_a).then_inc(s_pt.sem, 1)

            steps = {"k": keys, "v": values, "exp": exps, "transposes": probs_t, **n1.steps("act", "norm1"), **n2.steps("act", "norm2")}
            three_stage(act, "act", L1_TABLE, steps, ff.scalar_part(act), 2 * HJ)

        @block.gpsimd
        def _(pool):
            steps = {**n1.steps("pool", "norm1"), **n2.steps("pool", "norm2")}
            three_stage(pool, "pool", L1_TABLE, steps, lambda n, u, g: None, 2 * HJ)

        @block.vector
        def _(v):
            def queries(v, n, w):
                b0 = V["L1_cond_q_b"]
                for t in range(KT):
                    s_qm.wait(v, n, t)
                    nc.vector.tensor_scalar(q[:, t], ps_f[:, t], bias[:, b0 + t:b0 + t + 1], None, ALU.add).then_inc(s_q.sem, 1)

            def softmax_a(v, n, w):
                v.wait_ge(s_sm.sem, s_sm.after(n))
                mask = K["block_mask"].unsqueeze(1).broadcast_to([P, NP, P])
                ps = ps_a.rearrange("p (a n) -> p a n", n=P)
                nc.vector.scalar_tensor_tensor(sc[:], ps, SCALE, mask, ALU.mult, ALU.add).then_inc(s_sc.sem, 1)
                v.wait_ge(s_sc.sem, s_sc.after(n))
                nc.vector.reduce_max(mx[:], sc[:], AX.X).then_inc(s_mx.sem, 1)
                v.wait_ge(s_mx.sem, s_mx.after(n))
                nc.vector.tensor_tensor(sc[:], sc[:], mx[:].unsqueeze(2).broadcast_to([P, NP, P]), ALU.subtract).then_inc(s_sub.sem, 1)

            def softmax_b(v, n, w):
                v.wait_ge(s_exp.sem, s_exp.after(n))
                nc.vector.reduce_sum(rs[:], sc[:], AX.X).then_inc(s_rs.sem, 1)
                v.wait_ge(s_rs.sem, s_rs.after(n))
                nc.vector.reciprocal(rs[:], rs[:]).then_inc(s_rr.sem, 1)
                v.wait_ge(s_rr.sem, s_rr.after(n))
                nc.vector.tensor_tensor(sc[:], sc[:], rs[:].unsqueeze(2).broadcast_to([P, NP, P]), ALU.mult).then_inc(s_pn.sem, 1)

            def attended(v, n, w):
                v.wait_ge(s_om.sem, s_om.after(n))
                b0 = V["L1_cond_v_b"]
                for t in range(KT):
                    last = nc.vector.tensor_scalar(h_in[:, w, t], ps_f[:, t], bias[:, b0 + t:b0 + t + 1], None, ALU.add)
                last.then_inc(s_o.sem, 1)

            def projected(v, n, w):
                v.wait_ge(s_pm.sem, s_pm.after(n))
                b0 = V["L1_cond_proj_b"]
                for t in range(KT):
                    last = nc.vector.scalar_tensor_tensor(x1[:, w, t], ps_f[:, t], bias[:, b0 + t:b0 + t + 1], x_all[:, n, t], ALU.add, ALU.add)
                last.then_inc(s_x1.sem, 1)

            def back(n, u):
                v.wait_ge(ff.down.sem, ff.down.after(n))
                b0 = V["L1_cond_mlp_b2"]
                for t in range(KT):
                    last = nc.vector.scalar_tensor_tensor(x_all[:, n, t], ps_o[:, t], bias[:, b0 + t:b0 + t + 1], x1[:, u, t], ALU.add, ALU.add)
                last.then_inc(s_ffo.sem, 1)

            steps = {"q": queries, "softmax_a": softmax_a, "softmax_b": softmax_b, "attend": attended, "proj": projected,
                     **n1.steps("dve", "norm1"), **n2.steps("dve", "norm2")}
            three_stage(v, "dve", L1_TABLE, steps, lambda n, u, g: None, 2 * HJ, back)
    sg.close_layer(NG)


def layer2(nc, mem, sg, T, K):
    x_all = K["x"]
    V, bias = K["vec_at"], K["bias"]
    NGT, H, L, DIRS = 20, 16, 11, 2
    DH = D // H
    HT = H // KT
    CH = 4
    R = CH * NGT
    NC = H // CH
    KC = HT * NGT
    NEG = 9000000000000000.0
    with ExitStack() as ctx:
        m = Mem(nc, ctx)
        psum = lambda name, n: ctx.enter_context(nc.psum_tensor(name, [P, n, GT], F32))
        sf = m.sb("l2_self", [P, 2, KT, GT])
        sfk = m.sb("l2_self_plain", [P, KT, GT])
        q = m.sb("l2_queries", [P, 2, DIRS * KT, GT])
        kt = m.sb("l2_k", [P, 2, DIRS * KT, GB * NGT])
        vt = m.sb("l2_v", [P, 2, DIRS * KT, GB * NGT])
        key_blocks = m.sb("l2_key_blocks", [P, 2, 2, DIRS * KT, KC])
        value_cols = m.sb("l2_value_columns", [P, 2, DIRS * KT, KC])
        value_blocks = m.sb("l2_value_blocks", [P, 4, NC, CH * DH])
        sc = m.sb("l2_scores", [P, 2, DIRS, H * NGT])
        pt = m.sb("l2_probs_t", [P, DIRS, NC, P])
        adj_i = m.sb("l2_adj", [P, NP * DIRS * NGT * L], I32)
        adj = adj_i[:].bitcast(F32)
        keep = m.sb("l2_keep", [P, 2, NP, DIRS * NGT])
        lbias = m.sb("l2_label_bias", [P, 2, NP, DIRS * NGT])
        nz = m.sb("l2_nonzero", [P, GT])
        mx = m.sb("l2_max", [P, 2, DIRS * H])
        rs = m.sb("l2_sums", [P, 2, DIRS * H])
        ot = m.sb("l2_out", [P, KT, P])
        adj_neg = m.sb("l2_neg", [P, NP * DIRS * NGT])
        kb = m.sb("l2_scaled_key_bias", [P, DIRS * KT])
        ob = m.sb("l2_out_bias", [P, KT])
        ps_s, ps_r, ps_o, ps_f = psum("l2_pss", 2), psum("l2_psr", 3), psum("l2_pso", 1), psum("l2_psf", 2)

        g_bias = sg.get("l2_biases")
        g_adj_in, g_adj_f = sg.get("adj_loaded", 16), sg.get("adj_converted")
        g_cnt, g_keep, g_neg = sg.get("adj_counted"), sg.get("keep_ready"), sg.get("neg_ready")
        g_lab, g_labs, g_lbias = sg.get("adj_weighted"), sg.get("adj_labels_summed"), sg.get("label_bias_ready")
        g_negs = sg.get("neg_made")
        g_xs, g_rm, g_nz, g_tq = sg.get("row_summed"), sg.get("row_sum_products"), sg.get("row_nonzero"), sg.get("cond_part_ready")
        g_sm, g_sf, g_sfb = sg.get("self_products"), sg.get("self_ready"), sg.get("self_biased")
        g_fm, g_fe = sg.get("front_products", 8), sg.get("front_evacuated", 8)
        g_kb, g_vc = sg.get("key_blocks_ready", NP), sg.get("value_columns_ready", NP)
        g_s, g_a0, g_a1, g_mx = (sg.get(x, NP) for x in ("score_products", "scores_masked", "scores_biased", "scores_max"))
        g_sub, g_exp, g_rs, g_rr, g_pn = (sg.get(x, NP) for x in ("scores_minus_max", "probs_exp", "probs_summed", "probs_inverted", "probs_ready"))
        g_t, g_pt = sg.get("probs_transposed", 2 * NP), sg.get("probs_t_ready", 2 * NP)
        g_v, g_vb = sg.get("values_transposed", 4 * NP), sg.get("value_blocks_ready", 4 * NP)
        g_o, g_or, g_x = sg.get("attn_products", NP), sg.get("attn_ready", NP), sg.get("x_updated", NP)

        w_at = lambda name, d, k: K[name][:, d * KT + k]
        block = ctx.enter_context(nc.Block())

        @block.sync
        def _(sp):
            def load_adj(n):
                g_adj_in.wait(sp, n, -1)
                g_labs.wait(sp, n, -1)
                sp.dma_start(adj_i[:], T["adj"][n]).then_inc(g_adj_in.sem, 16)

            for n in range(NG):
                load_adj(n)

        FRONT = ([("k", d, None) for d in range(DIRS)] + [("q", d, t) for d in range(DIRS) for t in range(KT)]
                 + [("v", d, None) for d in range(DIRS)])
        SLOTS = [["row"], ["self", 0, 1], [2, 3, 4], [5, 6, 7]]

        def front(step_of, n):
            for slot in SLOTS:
                for step in slot:
                    step_of(n, 0, step)

        def lagged(n, s, lag, u):
            if s >= lag:
                return (n, s - lag, u) if not isinstance(n, int) or n < NG else None
            return (n - 1, s - lag + NP, 1 - u) if not isinstance(n, int) or n > 0 else None

        def in_slots(engine, first, slots):
            first(0)
            slots(0, 1, 0)
            with engine.Fori(1, NG - 2, 2) as i:
                slots(i, i + 1, 1)
                slots(i + 1, i + 2, 0)
            slots(NG - 1, None, 1)
            slots(NG, None, 0)

        def first_tokens(a):
            return a.rearrange("p (b s) -> p b s", s=S)[:, :, 0:NGT]

        @block.tensor
        def _(pe):
            def front_step(n, w, step):
                if step == "row":
                    g_xs.wait(pe, n)
                    g_fe.wait(pe, n, -1)
                    nc.tensor.matmul(ps_f[:, 0], K["ones"][:], nz[:], start=True, stop=True).then_inc(g_rm.sem, 1)
                elif step == "self":
                    g_nz.wait(pe, n)
                    for t in range(KT):
                        for k in range(KT):
                            last = nc.tensor.matmul(ps_f[:, t], K["l2_ws"][:, k, t * P:(t + 1) * P], x_all[:, n, k], start=(k == 0), stop=(k == KT - 1))
                    last.then_inc(g_sm.sem, 1)
                else:
                    kind, d, t = FRONT[step]
                    g_sf.wait(pe, n)
                    if step >= 2:
                        g_fe.wait(pe, n, step - 2)
                    ps = ps_f[:, step % 2]
                    if kind == "q":
                        for k in range(KT):
                            last = nc.tensor.matmul(ps, w_at("l2_wq", d, k)[:, t * P:(t + 1) * P], sfk[:, k], start=(k == 0), stop=(k == KT - 1))
                    else:
                        for t in range(KT):
                            dst = ps[:, t * GB * NGT:(t + 1) * GB * NGT]
                            for k in range(KT):
                                last = nc.tensor.matmul(dst, w_at("l2_w" + kind, d, k)[:, t * P:(t + 1) * P], first_tokens(sfk[:, k]), start=(k == 0), stop=(k == KT - 1))
                    last.then_inc(g_fm.sem, 1)

            def scores(n, u, p):
                g_kb.wait(pe, n, p)
                g_fe.wait(pe, n, 5)
                g_a0.wait(pe, n, p - 1)
                for d in range(DIRS):
                    for b in range(2):
                        for t in range(KT):
                            tok = (2 * p + b) * S
                            last = nc.tensor.matmul(ps_s[b * S:(b + 1) * S, d, t * KC:(t + 1) * KC], q[:, u, d * KT + t, tok:tok + S],
                                                    key_blocks[:, p % 2, b, d * KT + t], start=True, stop=True)
                last.then_inc(g_s.sem, 1)

            def probs_t(n, p):
                g_pn.wait(pe, n, p)
                for d in range(DIRS):
                    g_vb.wait(pe, n, 4 * (p - 1) + 1 + d)
                    for i in range(NC):
                        last = nc.tensor.transpose(ps_r[0:R, d, i * P:(i + 1) * P], sc[:, p % 2, d, i * R:(i + 1) * R], K["ident"])
                    last.then_inc(g_t.sem, 1)

            def values_t(n, p, i):
                b, d = i // 2, i % 2
                if i == 0:
                    g_vc.wait(pe, n, p)
                    g_vb.wait(pe, n, 4 * (p - 1) + 3)
                elif i == 3:
                    g_vb.wait(pe, n, 4 * p)
                else:
                    g_pt.wait(pe, n, 2 * p + i - 1)
                for c in range(NC):
                    a = value_cols[:, b, d * KT + c // 2, (c % 2) * R:(c % 2 + 1) * R]
                    last = nc.tensor.transpose(ps_r[0:R, (i + 2) % 3, c * P:(c + 1) * P], a, K["ident"])
                last.then_inc(g_v.sem, 1)

            def attend(n, p):
                g_vb.wait(pe, n, 4 * p + 3)
                g_pt.wait(pe, n, 2 * p + 1)
                g_or.wait(pe, n, p - 1)
                for b in range(2):
                    for c in range(NC):
                        for d in range(DIRS):
                            half = (c % 2) * CH * DH
                            last = nc.tensor.matmul(ps_o[half:half + CH * DH, 0, c // 2 * P + b * S:c // 2 * P + (b + 1) * S], value_blocks[0:R, 2 * b + d, c],
                                                    pt[0:R, d, c, b * S:(b + 1) * S], start=(d == 0), stop=(d == DIRS - 1))
                last.then_inc(g_o.sem, 1)

            def slots(n, f, u):
                for s in range(NP):
                    attending, scored = lagged(n, s, 2, u), lagged(n, s, 0, u)
                    beside = SLOTS[s] if f is not None else []
                    if "self" in beside:
                        front_step(f, 1 - u, "self")
                    if attending:
                        ga, pa, _ = attending
                        probs_t(ga, pa)
                        values_t(ga, pa, 0)
                    if scored:
                        scores(n, u, s)
                    if attending:
                        for i in range(1, 4):
                            values_t(ga, pa, i)
                    for step in beside:
                        if step != "self":
                            front_step(f, 1 - u, step)
                    if attending:
                        attend(ga, pa)

            in_slots(pe, lambda n: front(front_step, n), slots)

        @block.scalar
        def _(act):
            def front_step(n, w, step):
                if step == "row":
                    g_adj_in.wait(act, n)
                    nc.scalar.copy(adj, adj_i[:]).then_inc(g_adj_f.sem, 1)
                elif step != "self":
                    kind, d, t = FRONT[step]
                    g_fm.wait(act, n, step)
                    ps = ps_f[:, step % 2]
                    if kind == "q":
                        if (d, t) == (0, 0):
                            g_s.wait(act, n, -NP - 1)
                        b0 = V["L2_cond_bq"] + d * KT + t
                        last = nc.scalar.activation(q[:, w, d * KT + t], ps, ACT.Identity, bias=bias[:, b0:b0 + 1])
                    elif kind == "k":
                        if d == 0:
                            g_kb.wait(act, n, -NP - 1)
                        for t in range(KT):
                            j = d * KT + t
                            last = nc.scalar.activation(kt[:, w, j], ps[:, t * GB * NGT:(t + 1) * GB * NGT], ACT.Identity,
                                                        bias=kb[:, j:j + 1], scale=1.0 / np.sqrt(DH))
                    else:
                        if d == 0:
                            g_vc.wait(act, n, -NP - 1)
                        last = nc.scalar.copy(vt[:, w, d * KT:(d + 1) * KT].rearrange("p a n -> p (a n)"), ps[:, 0:KT * GB * NGT])
                    last.then_inc(g_fe.sem, 1)

            def probs_t(n, p):
                g_o.wait(act, n, p - 1)
                for d in range(DIRS):
                    g_t.wait(act, n, 2 * p + d)
                    nc.scalar.copy(pt[0:R, d].rearrange("p a n -> p (a n)"), ps_r[0:R, d]).then_inc(g_pt.sem, 1)

            def value_rows(n, p):
                for i in range(4):
                    g_v.wait(act, n, 4 * p + i)
                    a = ps_r[0:R, (i + 2) % 3].rearrange("p (t a n) -> p t a n", t=KT, a=4)[:, :, 0:4:3]
                    nc.scalar.copy(value_blocks[0:R, i].rearrange("p (t c) n -> p t c n", t=KT), a).then_inc(g_vb.sem, 1)

            def exps(n, p):
                g_sub.wait(act, n, p)
                nc.scalar.activation(sc[:, p % 2], sc[:, p % 2], ACT.Exp).then_inc(g_exp.sem, 1)

            def slots(n, f, u):
                for s in range(NP):
                    attending, scored = lagged(n, s, 2, u), lagged(n, s, 0, u)
                    if attending:
                        ga, pa, _ = attending
                        probs_t(ga, pa)
                        value_rows(ga, pa)
                    if f is not None:
                        for step in SLOTS[s]:
                            front_step(f, 1 - u, step)
                    if scored:
                        exps(n, s)

            g_bias.wait(act, 0)
            in_slots(act, lambda n: front(front_step, n), slots)

        @block.gpsimd
        def _(pool):
            def front_step(n, step):
                if step == "row":
                    g_adj_f.wait(pool, n)
                    g_cnt.wait(pool, n)
                    a = adj.rearrange("p (a l) -> p a l", l=L)
                    w = K["label_w"].unsqueeze(1).broadcast_to([P, NP * DIRS * NGT, L])
                    nc.gpsimd.tensor_tensor(a, a, w, ALU.mult).then_inc(g_lab.sem, 1)

            def blocks(n, p, u):
                g_fe.wait(pool, n, 1)
                g_s.wait(pool, n, p - 2)
                mask = K["head_mask"].unsqueeze(1).unsqueeze(3).broadcast_to([P, DIRS * KT, HT, NGT])
                for b in range(2):
                    at = (2 * p + b) * NGT
                    a = kt[:, u, :, at:at + NGT].unsqueeze(2).broadcast_to([P, DIRS * KT, HT, NGT])
                    last = nc.gpsimd.tensor_tensor(key_blocks[:, p % 2, b].rearrange("p j (h m) -> p j h m", m=NGT), a, mask, ALU.mult)
                last.then_inc(g_kb.sem, 1)

            def value_columns(n, p, u):
                g_fe.wait(pool, n, 7)
                g_v.wait(pool, n, 4 * (p - 1) + 3)
                mask = K["head_mask"].unsqueeze(1).unsqueeze(3).broadcast_to([P, DIRS * KT, HT, NGT])
                for b in range(2):
                    at = (2 * p + b) * NGT
                    a = vt[:, u, :, at:at + NGT].unsqueeze(2).broadcast_to([P, DIRS * KT, HT, NGT])
                    last = nc.gpsimd.tensor_tensor(value_cols[:, b].rearrange("p j (h m) -> p j h m", m=NGT), a, mask, ALU.mult)
                last.then_inc(g_vc.sem, 1)

            def normalise(n, p):
                g_rr.wait(pool, n, p)
                r = rs[:, p % 2].unsqueeze(2).broadcast_to([P, DIRS * H, NGT])
                a = sc[:, p % 2].rearrange("p d (h m) -> p (d h) m", m=NGT)
                nc.gpsimd.tensor_tensor(a, a, r, ALU.mult).then_inc(g_pn.sem, 1)

            def slots(n, f, u):
                for s in range(NP):
                    before = lagged(n, s, 1, u)
                    if before:
                        normalise(*before[:2])
                    if s + 1 < NP and lagged(n, s, 0, u):
                        blocks(n, s + 1, u)
                    elif s + 1 == NP and f is not None:
                        blocks(f, 0, 1 - u)
                    if before:
                        value_columns(*before)
                    if f is not None and s == 2:
                        front_step(f, "row")

            def first(n):
                front_step(n, "row")
                blocks(n, 0, 0)

            in_slots(pool, first, slots)

        @block.vector
        def _(v):
            b0 = V["L2_cond_bk"]
            nc.vector.tensor_scalar(kb[:], bias[:, b0:b0 + DIRS * KT], 1.0 / np.sqrt(DH), None, ALU.mult)
            b0 = V["L2_cond_bout"]
            nc.vector.tensor_tensor(ob[:], bias[:, b0:b0 + KT], bias[:, b0 + KT:b0 + 2 * KT], ALU.add).then_inc(g_bias.sem, 1)
            g_bias.wait(v, 0)

            def front_step(n, w, step):
                a = adj.rearrange("p (a l) -> p a l", l=L)
                k, lb = (t[:, w].rearrange("p a n -> p (a n)") for t in (keep, lbias))
                if step == "row_sum":
                    g_tq.wait(v, n, -1)
                    nc.vector.tensor_tensor(nz[:], x_all[:, n, 0], x_all[:, n, 1], ALU.add).then_inc(g_xs.sem, 1)
                elif step == "row":
                    g_rm.wait(v, n)
                    nc.vector.tensor_scalar(nz[:], ps_f[:, 0], 0.0, None, ALU.not_equal).then_inc(g_nz.sem, 1)
                    g_nz.wait(v, n)
                    g_fm.wait(v, n, -1)
                    g_sfb.wait(v, n, -1)
                    nzb = nz[:].rearrange("p (b s) -> p b s", s=S).unsqueeze(1).broadcast_to([P, KT, GB, S])
                    nc.vector.tensor_tensor(tokens(sfk[:]), nzb, per_batch(K["l2_q"], bass.ds(n * GB, GB)), ALU.mult).then_inc(g_tq.sem, 1)
                elif step == "self":
                    g_sm.wait(v, n)
                    g_tq.wait(v, n)
                    b0 = V["L2_cond_b_self"]
                    for t in range(KT):
                        last = nc.vector.scalar_tensor_tensor(sfk[:, t], ps_f[:, t], bias[:, b0 + t:b0 + t + 1], sfk[:, t], ALU.add, ALU.add)
                    last.then_inc(g_sf.sem, 1)
                elif step == "keep":
                    g_adj_f.wait(v, n)
                    nc.vector.reduce_sum(k, a, AX.X).then_inc(g_cnt.sem, 1)
                    g_cnt.wait(v, n)
                    nc.vector.tensor_scalar(k, k, 0.0, None, ALU.is_gt).then_inc(g_keep.sem, 1)
                elif step == "labels":
                    g_lab.wait(v, n)
                    nc.vector.reduce_sum(lb, a, AX.X).then_inc(g_labs.sem, 1)
                    g_labs.wait(v, n)
                    nc.vector.tensor_scalar(lb, lb, K["label_b"], None, ALU.add).then_inc(g_neg.sem, 1)
                    g_neg.wait(v, n)
                    nc.vector.tensor_scalar(adj_neg[:], k, 1.0, NEG, ALU.subtract, ALU.mult).then_inc(g_negs.sem, 1)
                    g_negs.wait(v, n)
                    nc.vector.tensor_tensor(lb, lb, adj_neg[:], ALU.add).then_inc(g_lbias.sem, 1)
                elif step == "biased":
                    g_sf.wait(v, n)
                    for t in range(KT):
                        last = nc.vector.tensor_scalar(sf[:, w, t], sfk[:, t], ob[:, t:t + 1], None, ALU.add)
                    last.then_inc(g_sfb.sem, 1)

            def softmax_a(n, u, p):
                g_s.wait(v, n, p)
                g_t.wait(v, n, 2 * (p - 2) + 1)
                a = sc[:, p % 2].rearrange("p d (h m) -> p d h m", m=NGT)
                ps = ps_s[:, :, 0:H * NGT].rearrange("p d (h m) -> p d h m", m=NGT)
                spread = lambda t: t[:, u, p].rearrange("p (d m) -> p d m", m=NGT).unsqueeze(2).broadcast_to([P, DIRS, H, NGT])
                nc.vector.tensor_tensor(a, ps, spread(keep), ALU.mult).then_inc(g_a0.sem, 1)
                g_a0.wait(v, n, p)
                nc.vector.tensor_tensor(a, a, spread(lbias), ALU.add).then_inc(g_a1.sem, 1)
                g_a1.wait(v, n, p)
                flat = sc[:, p % 2].rearrange("p d (h m) -> p (d h) m", m=NGT)
                nc.vector.reduce_max(mx[:, p % 2], flat, AX.X).then_inc(g_mx.sem, 1)
                g_mx.wait(v, n, p)
                nc.vector.tensor_tensor(flat, flat, mx[:, p % 2].unsqueeze(2).broadcast_to([P, DIRS * H, NGT]), ALU.subtract).then_inc(g_sub.sem, 1)

            def softmax_b(n, p):
                g_exp.wait(v, n, p)
                flat = sc[:, p % 2].rearrange("p d (h m) -> p (d h) m", m=NGT)
                nc.vector.reduce_sum(rs[:, p % 2], flat, AX.X).then_inc(g_rs.sem, 1)
                g_rs.wait(v, n, p)
                nc.vector.reciprocal(rs[:, p % 2], rs[:, p % 2]).then_inc(g_rr.sem, 1)

            def outputs(n, u, p):
                g_o.wait(v, n, p)
                c = slice(p * P, (p + 1) * P)
                g_x.wait(v, n, p - 1)
                nc.vector.tensor_tensor(ot[:], ps_o[:, 0, 0:KT * P].rearrange("p (t n) -> p t n", n=P), sf[:, u, :, c], ALU.add).then_inc(g_or.sem, 1)
                g_or.wait(v, n, p)
                nc.vector.scalar_tensor_tensor(x_all[:, n, :, c], ot[:], 0.0, x_all[:, n, :, c], ALU.max, ALU.add).then_inc(g_x.sem, 1)

            BEFORE = [["row_sum"], ["self"], [], []]
            AFTER = [["row"], ["keep"], [], ["biased", "labels"]]

            def slots(n, f, u):
                for s in range(NP):
                    outgoing, before = lagged(n, s, 3, u), lagged(n, s, 1, u)
                    if outgoing:
                        outputs(outgoing[0], outgoing[2], outgoing[1])
                    if before:
                        softmax_b(*before[:2])
                    if f is not None:
                        for step in BEFORE[s]:
                            front_step(f, 1 - u, step)
                    if lagged(n, s, 0, u):
                        softmax_a(n, u, s)
                    if f is not None:
                        for step in AFTER[s]:
                            front_step(f, 1 - u, step)

            def first(n):
                for before, after in zip(BEFORE, AFTER):
                    for step in before + after:
                        front_step(n, 0, step)

            in_slots(v, first, slots)
            g_x.wait(v, NG - 1)
    sg.close_layer(NG)



L3_TABLE = [
    ("qk0", dict(pe=0, act=0)), ("qk1", dict(pe=0, act=0)), ("perm0", dict(pe=1, pool=1, dve=1)), ("qk2", dict(pe=1, act=1)),
    ("perm1", dict(pe=2, pool=2, dve=2)), ("qk3", dict(pe=2, act=2)), ("perm2", dict(pe=3, pool=3, dve=3)), ("perm3", dict(pe=4, pool=4, dve=4)),
    ("v", dict(pe=4, dve=5)), ("kb0", dict(pool=5, dve=4)), ("s0", dict(pe=6, dve=6)), ("kb1", dict(pool=6)),
    ("s1", dict(pe=8, dve=8)), ("exp0", dict(act=7)), ("sum0", dict(dve=8)), ("kb2", dict(pool=8)),
    ("t0", dict(pe=9, act=9)), ("exp1", dict(act=9)), ("pv0", dict(pe=10, dve=10)),
    ("ot0", dict(pe=11, act=11)), ("sum1", dict(dve=10)), ("s2", dict(pe=11, dve=11)), ("kb3", dict(pool=11)), ("exp2", dict(act=12)),
    ("t1", dict(pe=12, act=12)), ("pv1", dict(pe=13, dve=13)), ("ot1", dict(pe=14, act=14)), ("sum2", dict(dve=13)),
    ("s3", dict(pe=14, dve=14)), ("norm1.square", dict(act=13)), ("norm1.sum", dict(pool=13)),
    ("t2", dict(pe=15, act=15)), ("exp3", dict(act=15)), ("norm1.variance", dict(pe=15)), ("norm1.guard", dict(dve=15)), ("norm1.invert", dict(pool=15)),
    ("pv2", dict(pe=16, dve=16)), ("norm1.diagonal", dict(dve=16)), ("sum3", dict(dve=16)),
    ("ot2", dict(pe=17, act=17)), ("t3", dict(pe=17, act=17)), ("norm1.spread", dict(pe=17)),
    ("pv3", dict(pe=18, dve=18)), ("norm1.apply", dict(dve=18)), ("ot3", dict(pe=19, act=19)), ("proj", dict(pe=20, dve=20)),
    ("norm2.square", dict(act=20)), ("norm2.sum", dict(pool=20)), ("norm2.variance", dict(pe=22)), ("norm2.guard", dict(dve=22)),
    ("norm2.invert", dict(pool=22)), ("norm2.diagonal", dict(dve=22)), ("norm2.spread", dict(pe=23)), ("norm2.apply", dict(dve=23)),
]


def layer3(nc, mem, sg, T, K):
    x_all = K["x"]
    V, bias = K["vec_at"], K["bias"]
    H = 16
    DH = D // H
    HT = H // KT
    HP = H // 2
    with ExitStack() as ctx:
        m = Mem(nc, ctx)
        psum = lambda name, n: ctx.enter_context(nc.psum_tensor(name, [P, n, GT], F32))
        x1 = m.sb("l3_x1", [P, 2, KT, GT])
        min_ = m.sb("l3_m", [P, 2, KT, GT])
        h_in = m.sb("l3_in", [P, 2, KT, GT])
        norm_bufs = [(m.sb(f"l3_sum{i}", [P, GT]), m.sb(f"l3_sq{i}", [P, KT, GT]), m.sb(f"l3_inv{i}", [P, Norm.CHUNKS])) for i in range(2)]
        raw = m.sb("l3_raw", [P, 2, GT])
        rc = m.sb("l3_cosine_part", [P, 2, GT])
        rsn = m.sb("l3_sine_part", [P, 2, GT])
        qk = m.sb("l3_qk", [P, 2 * KT, GT])
        vb = m.sb("l3_value_blocks", [P, 2, NP, D])
        key_blocks = m.sb("l3_key_blocks", [P, 2, 2, KT, HT * S])
        sc = m.sb("l3_scores", [P, 2, H, S])
        pt = m.sb("l3_probs_t", [P, HP, P])
        on = m.sb("l3_attn", [P, 2, D])
        mx = m.sb("l3_max", [P, 2, H])
        rs = m.sb("l3_sums", [P, 2, H])
        sig = m.sb("l3_silu", [P, GT])
        hidden = m.sb("l3_h", [P, 2, GT])
        ps_ag, ps_o, ps_x, ps_y = psum("l3_psag", 2), psum("l3_pso", 2), psum("l3_psx", 2), psum("l3_psy", 2)

        s_x1, s_ffo = sg.get("x1_ready"), sg.get("ff_out_read")
        g_vz = sg.get("value_blocks_cleared")
        g_qk, g_raw = sg.get("q_products", 4), sg.get("q_ready", 4)
        g_perm, g_rs, g_rc, g_rope = (sg.get(x, 4) for x in ("qk_swapped", "qk_sine_part", "qk_cosine_part", "qk_rotated"))
        g_vm, g_vb = sg.get("v_products"), sg.get("v_ready")
        g_kbv = sg.get("key_blocks_halved")
        g_kb, g_s, g_mx, g_sub, g_exp = (sg.get(x, NP) for x in ("key_blocks_ready", "score_products", "scores_max", "scores_minus_max", "probs_exp"))
        g_sum, g_rr, g_t, g_pt = (sg.get(x, NP) for x in ("probs_summed", "probs_inverted", "probs_transposed", "probs_t_ready"))
        g_pv, g_on, g_ot, g_o = (sg.get(x, NP) for x in ("attn_products", "attn_normalised", "attn_transposed", "attn_ready"))
        g_pm = sg.get("proj_products")
        f_a, f_g, f_sig, f_h, f_down = (sg.get(x, HJ) for x in ("ff_a_products", "ff_gate_products", "ff_activated", "ff_hidden_ready", "ff_down"))

        def no_wait(e, n):
            pass

        def x1_ready(e, n):
            s_x1.wait(e, n)

        n1 = Norm(nc, sg, K, "norm1", lambda n, w: x_all[:, n], no_wait, lambda w: h_in[:, w], False, float(np.finfo(np.float32).eps),
                  K["l3a_scale"], K["l3a_shift"], ps_x[:, 0], norm_bufs[0])
        n2 = Norm(nc, sg, K, "norm2", lambda n, w: x1[:, w], x1_ready, lambda w: min_[:, w], False, float(np.finfo(np.float32).eps),
                  K["l3b_scale"], K["l3b_shift"], ps_y[:, 1], norm_bufs[1])
        block = ctx.enter_context(nc.Block())

        def by_name(front_step, who, norms):
            def step_of(name):
                return lambda engine, n, w: front_step(n, w, name)
            names = [name for name, at in L3_TABLE if who in at and not name.startswith("norm")]
            return {**{name: step_of(name) for name in names}, **norms}

        @block.sync
        def _(sp):
            for n in range(NG):
                s_ffo.wait(sp, n)
                sp.dma_start(T["out"][:, n], x_all[:, n]).then_inc(K["x_stored"], 16)
            sp.wait_ge(K["x_stored"], 16 * NG)

        @block.tensor
        def _(pe):
            w_qkv, w_fc, w_fo = K["l3_qkv"], K["l3_fc"], K["l3_fo"]

            def front_step(n, w, step):
                kind, p = step[:-1], int(step[-1]) if step[-1].isdigit() else None
                if kind == "qk":
                    n1.done.wait(pe, n)
                    if p >= 2:
                        g_raw.wait(pe, n, p - 2)
                    for k in range(KT):
                        last = nc.tensor.matmul(ps_x[:, p % 2], w_qkv[:, k, p * P:(p + 1) * P], h_in[:, w, k], start=(k == 0), stop=(k == KT - 1))
                    last.then_inc(g_qk.sem, 1)
                elif kind == "perm":
                    g_raw.wait(pe, n, p)
                    if p >= 2:
                        g_rs.wait(pe, n, p - 2)
                    nc.tensor.matmul(ps_y[:, p % 2], K["swap"], raw[:, p % 2], start=True, stop=True).then_inc(g_perm.sem, 1)
                elif step == "v":
                    g_raw.wait(pe, n, 3)
                    for a in range(NP):
                        dst = ps_x[:, a // 2, (a % 2) * D:(a % 2 + 1) * D]
                        for k in range(KT):
                            last = nc.tensor.matmul(dst, h_in[:, w, k, a * P:(a + 1) * P], w_qkv[:, k, 2 * D:3 * D], start=(k == 0), stop=(k == KT - 1))
                    last.then_inc(g_vm.sem, 1)
                elif kind == "s":
                    g_kb.wait(pe, n, p)
                    if p == 0:
                        g_kbv.wait(pe, n)
                        g_vb.wait(pe, n)
                    else:
                        g_sub.wait(pe, n, p - 1)
                    for b in range(2):
                        at = (2 * p + b) * S
                        for t in range(KT):
                            last = nc.tensor.matmul(ps_x[b * S:(b + 1) * S, t], qk[:, t, at:at + S], key_blocks[:, p % 2, b, t], start=True, stop=True)
                    last.then_inc(g_s.sem, 1)
                elif kind == "t":
                    g_exp.wait(pe, n, p)
                    if p == 0:
                        g_rs.wait(pe, n, 3)
                    else:
                        g_o.wait(pe, n, p - 1)
                    for i in range(HP):
                        last = nc.tensor.transpose(ps_y[:, i // 4, (i % 4) * P:(i % 4 + 1) * P], sc[:, p % 2, 2 * i:2 * i + 2].rearrange("p h m -> p (h m)"), K["ident"])
                    last.then_inc(g_t.sem, 1)
                elif kind == "pv":
                    g_pt.wait(pe, n, p)
                    for b in range(2):
                        for i in range(HP):
                            c = slice(i * 2 * DH, (i + 1) * 2 * DH)
                            last = nc.tensor.matmul(ps_y[b * S:(b + 1) * S, 0, c], pt[:, i, b * S:(b + 1) * S], vb[:, b, p, c], start=True, stop=True)
                    last.then_inc(g_pv.sem, 1)
                elif kind == "ot":
                    g_on.wait(pe, n, p)
                    for t in range(KT):
                        last = nc.tensor.transpose(ps_y[:, 1, t * P:(t + 1) * P], on[:, p % 2, t * P:(t + 1) * P], K["ident"])
                    last.then_inc(g_ot.sem, 1)
                elif step == "proj":
                    g_o.wait(pe, n)
                    if isinstance(n, int) and n == NG - 1:
                        g_sub.wait(pe, n)
                    else:
                        n1.normed.wait(pe, n + 1)
                    for t in range(KT):
                        for k in range(KT):
                            last = nc.tensor.matmul(ps_x[:, t], K["l3_ao"][:, k, t * P:(t + 1) * P], h_in[:, w, k], start=(k == 0), stop=(k == KT - 1))
                    last.then_inc(g_pm.sem, 1)

            def down(n, j):
                f_h.wait(pe, n, j)
                if j == 0:
                    s_ffo.wait(pe, n, -1)
                for t in range(KT):
                    last = nc.tensor.matmul(ps_o[:, t], w_fo[:, j, t * P:(t + 1) * P], hidden[:, j % 2], start=(j == 0), stop=(j == HJ - 1))
                last.then_inc(f_down.sem, 1)

            def ff_part(n, u, j, part):
                if part == 2:
                    if j >= 1:
                        down(n, j - 1)
                    return
                if j == 0 and part == 0:
                    n2.done.wait(pe, n)
                (f_h if part else f_sig).wait(pe, n, j - 1)
                for k in range(KT):
                    c = ((1 - part) * HJ + j) * P
                    last = nc.tensor.matmul(ps_ag[:, part], w_fc[:, k, c:c + P], min_[:, u, k], start=(k == 0), stop=(k == KT - 1))
                last.then_inc((f_a if part else f_g).sem, 1)

            def norm1_variance(engine, n, w):
                g_sub.wait(pe, n, -1)
                n1.tensor_variance(pe, n, w)

            norms = {**n1.steps("pe", "norm1"), **n2.steps("pe", "norm2"), "norm1.variance": norm1_variance}
            three_stage(pe, "pe", L3_TABLE, by_name(front_step, "pe", norms),
                        lambda n, u, g: ff_part(n, u, g // 3, g % 3), 3 * HJ, lambda n, u: down(n, HJ - 1))

        @block.scalar
        def _(act):
            def front_step(n, w, step):
                kind, p = step[:-1], int(step[-1]) if step[-1].isdigit() else None
                if kind == "qk":
                    g_qk.wait(act, n, p)
                    if p >= 2:
                        g_rc.wait(act, n, p - 2)
                        g_perm.wait(act, n, p - 2)
                    b0 = V["L3_cond_b_qkv"] + p
                    nc.scalar.activation(raw[:, p % 2], ps_x[:, p % 2], ACT.Identity, bias=bias[:, b0:b0 + 1]).then_inc(g_raw.sem, 1)
                elif kind == "exp":
                    g_sub.wait(act, n, p)
                    nc.scalar.activation(sc[:, p % 2], sc[:, p % 2], ACT.Exp, scale=1.0 / np.sqrt(DH)).then_inc(g_exp.sem, 1)
                elif kind == "t":
                    g_t.wait(act, n, p)
                    nc.scalar.copy(pt[:].rearrange("p a n -> p (a n)"), ps_y[:].rearrange("p a n -> p (a n)")).then_inc(g_pt.sem, 1)
                elif kind == "ot":
                    g_ot.wait(act, n, p)
                    b0 = V["L3_cond_b_qkv"] + 2 * KT
                    for t in range(KT):
                        last = nc.scalar.activation(h_in[:, w, t, p * P:(p + 1) * P], ps_y[:, 1, t * P:(t + 1) * P], ACT.Identity, bias=bias[:, b0 + t:b0 + t + 1])
                    last.then_inc(g_o.sem, 1)

            def ff_part(n, u, j, part):
                if part == 0:
                    f_g.wait(act, n, j)
                    f_h.wait(act, n, j - 1)
                    b0 = V["L3_cond_b_fc"] + HJ + j
                    nc.scalar.activation(sig[:], ps_ag[:, 0], ACT.Silu, bias=bias[:, b0:b0 + 1]).then_inc(f_sig.sem, 1)

            three_stage(act, "act", L3_TABLE, by_name(front_step, "act", {**n1.steps("act", "norm1"), **n2.steps("act", "norm2")}),
                        lambda n, u, g: ff_part(n, u, g // 3, g % 3), 3 * HJ)

        @block.gpsimd
        def _(pool):
            def front_step(n, w, step):
                kind, p = step[:-1], int(step[-1]) if step[-1].isdigit() else None
                if kind == "perm":
                    g_raw.wait(pool, n, p)
                    g_rope.wait(pool, n, p - 2)
                    cos = K["rope_cos"].unsqueeze(1).broadcast_to([P, GB, S])
                    b3 = lambda a: a.rearrange("p (b s) -> p b s", s=S)
                    nc.gpsimd.tensor_tensor(b3(rc[:, p % 2]), b3(raw[:, p % 2]), cos, ALU.mult).then_inc(g_rc.sem, 1)
                elif kind == "kb":
                    g_rope.wait(pool, n)
                    g_s.wait(pool, n, p - 2)
                    batches = (1,) if p == 0 else (0, 1)
                    mask = K["head_mask"].unsqueeze(2).broadcast_to([P, HT, S])
                    for b in batches:
                        at = (2 * p + b) * S
                        for t in range(KT):
                            a = qk[:, KT + t, at:at + S].unsqueeze(1).broadcast_to([P, HT, S])
                            last = nc.gpsimd.tensor_tensor(key_blocks[:, p % 2, b, t].rearrange("p (h s) -> p h s", s=S), a, mask, ALU.mult)
                    last.then_inc(g_kb.sem, 1)

            three_stage(pool, "pool", L3_TABLE, by_name(front_step, "pool", {**n1.steps("pool", "norm1"), **n2.steps("pool", "norm2")}),
                        lambda n, u, g: None, 3 * HJ)

        @block.vector
        def _(v):
            nc.vector.memset(vb[:], 0.0).then_inc(g_vz.sem, 1)
            g_vz.wait(v, 0)

            def sums(n, p):
                g_exp.wait(v, n, p)
                nc.vector.reduce_sum(rs[:, p % 2], sc[:, p % 2], AX.X).then_inc(g_sum.sem, 1)
                g_sum.wait(v, n, p)
                nc.vector.reciprocal(rs[:, p % 2], rs[:, p % 2]).then_inc(g_rr.sem, 1)

            def front_step(n, w, step):
                kind, p = step[:-1], int(step[-1]) if step[-1].isdigit() else None
                if kind == "kb":
                    g_rope.wait(v, n)
                    g_s.wait(v, n, -2)
                    mask = K["head_mask"].unsqueeze(2).broadcast_to([P, HT, S])
                    for t in range(KT):
                        a = qk[:, KT + t, 0:S].unsqueeze(1).broadcast_to([P, HT, S])
                        last = nc.vector.tensor_tensor(key_blocks[:, 0, 0, t].rearrange("p (h s) -> p h s", s=S), a, mask, ALU.mult)
                    last.then_inc(g_kbv.sem, 1)
                elif kind == "perm":
                    g_perm.wait(v, n, p)
                    g_rope.wait(v, n, p - 2)
                    sin = K["rope_sin"].unsqueeze(1).broadcast_to([P, GB, S])
                    b3 = lambda a: a.rearrange("p (b s) -> p b s", s=S)
                    nc.vector.tensor_tensor(b3(rsn[:, p % 2]), b3(ps_y[:, p % 2]), sin, ALU.mult).then_inc(g_rs.sem, 1)
                    g_rs.wait(v, n, p)
                    g_rc.wait(v, n, p)
                    nc.vector.tensor_tensor(qk[:, p], rc[:, p % 2], rsn[:, p % 2], ALU.add).then_inc(g_rope.sem, 1)
                elif step == "v":
                    g_vm.wait(v, n)
                    src = ps_x[:].rearrange("p k (a h e d) -> p (k a) h e d", a=2, e=2, d=DH)
                    dst = vb[:].rearrange("p b a (h e d) -> p b a h e d", e=2, d=DH)
                    for b in range(2):
                        for e in range(2):
                            last = nc.vector.tensor_copy(dst[e * S:(e + 1) * S, b, :, :, e], src[b * S:(b + 1) * S, :, :, e])
                    last.then_inc(g_vb.sem, 1)
                elif kind == "s":
                    g_s.wait(v, n, p)
                    ps = ps_x[:].rearrange("p t (h s) -> p (t h) s", s=S)
                    nc.vector.reduce_max(mx[:, p % 2], ps, AX.X).then_inc(g_mx.sem, 1)
                    g_mx.wait(v, n, p)
                    nc.vector.tensor_tensor(sc[:, p % 2], ps, mx[:, p % 2].unsqueeze(2).broadcast_to([P, H, S]), ALU.subtract).then_inc(g_sub.sem, 1)
                elif kind == "sum":
                    sums(n, p)
                elif kind == "pv":
                    g_pv.wait(v, n, p)
                    g_rr.wait(v, n, p)
                    r = rs[:, p % 2].unsqueeze(2).broadcast_to([P, H, DH])
                    nc.vector.tensor_tensor(on[:, p % 2].rearrange("p (h d) -> p h d", d=DH), ps_y[:, 0, 0:D].rearrange("p (h d) -> p h d", d=DH), r,
                                            ALU.mult).then_inc(g_on.sem, 1)
                elif step == "proj":
                    g_pm.wait(v, n)
                    b0 = V["L3_cond_b_ao"]
                    for t in range(KT):
                        last = nc.vector.scalar_tensor_tensor(x1[:, w, t], ps_x[:, t], bias[:, b0 + t:b0 + t + 1], x_all[:, n, t], ALU.add, ALU.add)
                    last.then_inc(s_x1.sem, 1)

            def ff_part(n, u, j, part):
                if part == 1:
                    f_a.wait(v, n, j)
                    f_sig.wait(v, n, j)
                    f_down.wait(v, n, j - 2)
                    b0 = V["L3_cond_b_fc"] + j
                    nc.vector.scalar_tensor_tensor(hidden[:, j % 2], ps_ag[:, 1], bias[:, b0:b0 + 1], sig[:], ALU.add, ALU.mult).then_inc(f_h.sem, 1)

            def back_end(n, u):
                f_down.wait(v, n)
                b0 = V["L3_cond_b_fo"]
                for t in range(KT):
                    last = nc.vector.scalar_tensor_tensor(x_all[:, n, t], ps_o[:, t], bias[:, b0 + t:b0 + t + 1], x1[:, u, t], ALU.add, ALU.add)
                last.then_inc(s_ffo.sem, 1)

            three_stage(v, "dve", L3_TABLE, by_name(front_step, "dve", {**n1.steps("dve", "norm1"), **n2.steps("dve", "norm2")}),
                        lambda n, u, g: ff_part(n, u, g // 3, g % 3), 3 * HJ, back_end)
    sg.close_layer(NG)



VECTORS = ["L0_cond_bm", "L0_cond_bc", "L0_cond_D_diag", "L0_cond_b1", "L0_cond_b2",
           "L1_cond_norm1_w", "L1_cond_film1_b", "L1_cond_q_b", "L1_cond_k_b", "L1_cond_v_b", "L1_cond_proj_b",
           "L1_cond_norm2_w", "L1_cond_film2_b", "L1_cond_mlp_b1", "L1_cond_mlp_b2",
           "L2_cond_b_self", "L2_cond_bq", "L2_cond_bk", "L2_cond_bout",
           "L3_cond_g1", "L3_cond_g2", "L3_cond_b_qkv", "L3_cond_b_ao", "L3_cond_b_fc", "L3_cond_b_fo",
           "L3_cond_b_t1", "L3_cond_b_t2"]


def program(nc, T, vec_at):
    ctx = ExitStack()
    with ctx:
        mem = Mem(nc, ctx)
        sg = Signals(mem)
        K = {"vec_at": vec_at}
        K["x"] = mem.sb("x_all", [P, NG, KT, GT])
        K["bias"] = mem.sb("bias_columns", [P, T["vectors"].shape[1]])
        K["consts"] = mem.sb("constants", [P, T["consts"].shape[1]])
        K["sign"] = K["consts"][:, 0:1]
        K["minus_half"] = mem.sb("minus_half", [P, 4])
        K["ones"] = mem.sb("ones", [P, P])
        K["mean"] = mem.sb("mean_weights", [P, P])
        for name in ("l3a_scale", "l3a_shift", "l3b_scale", "l3b_shift"):
            K[name] = mem.sb(name, [P, KT, B])
        K["x_loaded"], K["w_loaded"] = mem.sem("x_loaded"), mem.sem("weights_loaded")
        arena = mem.sb("weights_a", [P, 2 * KT * FF + 2 * HJ * D])
        c2 = KT * FF
        K["l0_w1"] = arena[:, 0:c2].rearrange("p (k n) -> p k n", k=KT)
        K["l0_w2"] = arena[:, c2:c2 + HJ * D].rearrange("p (k n) -> p k n", k=HJ)
        K["s5_b"] = arena[:, c2 + HJ * D:c2 + HJ * D + 512].rearrange("p (c k n) -> p c k n", c=2, k=KT)
        K["s5_c"] = arena[:, c2 + HJ * D + 512:c2 + HJ * D + 1024].rearrange("p (c n) -> p c n", c=2)
        K["weights_first"] = [
            (K["l0_w1"], T["L0_cond_W1"].rearrange("(k p) n -> p k n", p=P)),
            (K["l0_w2"], T["L0_cond_W2"].rearrange("(k p) n -> p k n", p=P)),
            (K["s5_b"][:], T["s5_b"][:]), (K["s5_c"][:], T["s5_c"][:])]
        def weight(m, name, src, tiles, cols):
            K[name] = m.sb(name, [P, tiles, cols])
            return K[name][:], T[src].rearrange("(k p) n -> p k n", p=P)

        c = K["consts"]
        K["ident"], K["block_mask"], K["value_mask"] = (c[:, 32 + i * P:32 + (i + 1) * P] for i in range(3))
        K["head_mask"], K["label_w"], K["label_b"] = c[:, 1:9], c[:, 9:20], c[:, 20:21]
        K["swap"] = c[:, 32 + 3 * P:32 + 4 * P]
        K["rope_cos"], K["rope_sin"] = (c[:, 32 + 4 * P + i * S:32 + 4 * P + (i + 1) * S] for i in range(2))
        K["x_stored"] = mem.sem("x_stored")
        K["weights_l3"], at = [], 0
        for name, src, tiles, cols in (("l3_qkv", "L3_cond_w_qkv", KT, 3 * D), ("l3_ao", "L3_cond_w_ao", KT, D),
                                       ("l3_fc", "L3_cond_w_fc", KT, 2 * FF), ("l3_fo", "L3_cond_w_fo", HJ, D)):
            K[name] = arena[:, at:at + tiles * cols].rearrange("p (k n) -> p k n", k=tiles)
            at += tiles * cols
            K["weights_l3"].append((K[name], T[src].rearrange("(k p) n -> p k n", p=P)))
        with ExitStack() as l2:
            m2 = Mem(nc, l2)
            K["l2_q"] = m2.sb("l2_q", [P, KT, B])
            K["weights_l2"] = [weight(m2, "l2_ws", "WselfT_v", KT, D), weight(m2, "l2_wq", "l2_WqT", 2 * KT, D),
                               weight(m2, "l2_wk", "l2_WkT", 2 * KT, D), weight(m2, "l2_wv", "l2_WoutT", 2 * KT, D)]
            with ExitStack() as l1:
                m1 = Mem(nc, l1)
                for name in ("l1a_scale", "l1a_shift", "l1b_scale", "l1b_shift"):
                    K[name] = m1.sb(name, [P, KT, B])
                K["weights_first"] += [weight(m1, "l1_w1", "L1_cond_mlp_w1", KT, FF), weight(m1, "l1_w2", "L1_cond_mlp_w2", HJ, D)]
                K["weights_first"] += [weight(m1, "l1_w" + c, f"L1_cond_{w}_w", KT, D) for c, w in zip("qkvo", ("q", "k", "v", "proj"))]
                with ExitStack() as l0:
                    m0 = Mem(nc, l0)
                    for name in ("l0_shift", "l0_scale", "l0_gate", "l0_gate_ff", "l0_scale_ff", "l0_shift_ff"):
                        K[name] = m0.sb(name, [P, KT, B])
                    K["turn_in"], K["turn_out"], K["decay"] = m0.sb("turn_in", [P, 2, S]), m0.sb("turn_out", [P, 2, S]), m0.sb("decay", [P, GT])
                    conditioning(nc, mem, sg, T, K)
                    layer0(nc, mem, sg, T, K)
                layer1(nc, mem, sg, T, K)
            layer2(nc, mem, sg, T, K)
        layer3(nc, mem, sg, T, K)


def kernel(**inputs):
    import concourse.bacc as bacc
    from concourse.bass_utils import run_bass_kernel_spmd

    a = {k: np.asarray(v) for k, v in inputs.items()}
    lay = {}
    lay["x"] = a["x"].reshape(NG, GT, KT, P).transpose(3, 0, 2, 1)
    lay["condT"] = a["cond_1024"].T.reshape(KT, P, B).transpose(1, 0, 2)
    cols, vec_at, at = [], {}, 0
    for name in VECTORS:
        c = a[name].reshape(-1, P).T
        vec_at[name] = at
        at += c.shape[1]
        cols.append(c)
    lay["vectors"] = np.concatenate(cols, 1)
    lam = np.stack([a["L0_cond_Lam_re"], a["L0_cond_Lam_im"], a["L0_cond_log_step"]], 1)
    lay["lam"] = np.concatenate([lam, lam], 0)
    b_re, b_im = a["L0_cond_B_re"].T, a["L0_cond_B_im"].T
    pair = np.stack([np.concatenate([b_re, b_im], 1), np.concatenate([b_im, b_re], 1)])
    lay["s5_b"] = pair.reshape(2, KT, P, P).transpose(2, 0, 1, 3)
    c_re, c_im = a["L0_cond_C_re"].T, a["L0_cond_C_im"].T
    lay["s5_c"] = np.stack([np.concatenate([c_re, c_im], 0), np.concatenate([c_im, c_re], 0)]).transpose(1, 0, 2)
    lay["WselfT_q"] = a["L2_cond_W_self"].T[D:]
    lanes = np.arange(P)
    consts = np.zeros((P, 32 + 4 * P + 2 * S), np.float32)
    consts[:NS, 0], consts[NS:, 0] = -1.0, 1.0
    consts[:, 1:9] = lanes[:, None] // 16 == np.arange(8)
    consts[:, 9:20] = a["L2_cond_w_bias"]
    consts[:, 20] = a["L2_cond_b_bias"]
    consts[:, 32:32 + P] = np.eye(P)
    consts[:, 32 + P:32 + 2 * P] = np.where(lanes[:, None] // S == lanes // S, 0.0, -1e30)
    consts[:, 32 + 2 * P:32 + 3 * P] = lanes[:, None] // 10 == lanes // 16
    consts[:, 32 + 3 * P:32 + 4 * P] = np.eye(P)[lanes ^ 1]
    inv_freq = (np.float32(1.0) / np.power(np.float32(10000.0), np.arange(0, 16, 2, dtype=np.float32) / np.float32(16))).astype(np.float32)
    angle = np.arange(S, dtype=np.float32)[None] * inv_freq[lanes % 16 // 2][:, None]
    consts[:, 32 + 4 * P:32 + 4 * P + S] = np.cos(angle)
    consts[:, 32 + 4 * P + S:] = np.sin(angle) * np.where(lanes % 2, 1.0, -1.0)[:, None]
    adj = a["mask_BxSxSx11_ik0"]
    both = np.stack([adj[:, :, :20], adj[:, :20].transpose(0, 2, 1, 3)], 2)
    lay["adj"] = both.reshape(NG, NP, P, -1).transpose(0, 2, 1, 3).reshape(NG, P, -1)
    lay["WselfT_v"] = a["L2_cond_W_self"].T[:D]
    lay["l2_WqT"] = a["L2_cond_Wq"].transpose(0, 2, 1).reshape(2 * D, D)
    lay["l2_WkT"] = a["L2_cond_Wk"].transpose(0, 2, 1).reshape(2 * D, D)
    lay["l2_WoutT"] = a["L2_cond_Wout"].reshape(2, D, D).transpose(0, 2, 1).reshape(2 * D, D)
    lay["consts"] = consts
    for name in ("L0_cond_Wm", "L0_cond_Wc", "L1_cond_film1_w", "L1_cond_film2_w", "L3_cond_w_t1", "L3_cond_w_t2", "L0_cond_W1", "L0_cond_W2",
                 "L1_cond_mlp_w1", "L1_cond_mlp_w2", "L1_cond_q_w", "L1_cond_k_w", "L1_cond_v_w", "L1_cond_proj_w",
                 "L3_cond_w_qkv", "L3_cond_w_ao", "L3_cond_w_fc", "L3_cond_w_fo"):
        lay[name] = a[name]

    nc = bacc.Bacc("TRN2", target_bir_lowering=False, num_devices=1)
    arrays, T = {}, {}
    for name, v in lay.items():
        v = np.ascontiguousarray(v)
        arrays[f"in_{name}"] = v
        T[name] = nc.dram_tensor(f"in_{name}", v.shape, mybir.dt.from_np(v.dtype), kind="ExternalInput").ap()
    T["out"] = nc.dram_tensor("out_x", (P, NG, KT, GT), F32, kind="ExternalOutput").ap()
    program(nc, T, vec_at)
    r = run_bass_kernel_spmd(nc, [arrays], core_ids=[0])
    out = np.asarray(r.results[0]["out_x"])
    return out.transpose(1, 3, 2, 0).reshape(B, S, D)
```

```python
import concourse.bass as bass
from concourse import mybir
from contextlib import ExitStack
import numpy as np

F32 = mybir.dt.float32
I32 = mybir.dt.int32
R32 = mybir.dt.float32r
ALU = mybir.AluOpType
ACT = mybir.ActivationFunctionType
AX = mybir.AxisListType

P = 128
B, S, D = 128, 64, 256
KT = D // P
GB = 8
GT = GB * S
NG = B // GB
NP = GB // 2
FF = 4 * D
HJ = FF // P
NS = 64


class Mem:

    def __init__(self, nc, ctx):
        self.nc, self.ctx = nc, ctx

    def sb(self, name, shape, dt=F32):
        return self.ctx.enter_context(self.nc.sbuf_tensor(name, shape, dt))

    def sb_and_place(self, name, shape):
        t = self.sb(name, shape)
        return t, self.nc.sbuf_base - 4 * int(np.prod(shape[1:]))

    def rounded_at(self, name, shape, place):
        return self.nc.alloc_sbuf_tensor_at(name, shape, R32, offset=place)

    def sb_in_place(self, name, shape):
        t, place = self.sb_and_place(name, shape)
        return t, self.rounded_at(name + "_low", shape, place)

    def sem(self, name):
        return self.ctx.enter_context(self.nc.semaphore(name))


def per_batch(table, batches):
    return table[:, :, batches].unsqueeze(3).broadcast_to([P, KT, GB, S])


def tokens(t):
    return t.rearrange("p k (b s) -> p k b s", s=S)


class Signal:

    def __init__(self, sem, base, per_group):
        self.sem, self.base, self.k = sem, base, per_group

    def after(self, n, j=None):
        return self.base + n * self.k + (self.k if j is None else j + 1)

    def wait(self, engine, n, j=None):
        value = self.after(n, j)
        if not isinstance(value, int) or value > 0:
            engine.wait_ge(self.sem, value)

    def wait_before(self, engine, n):
        value = self.base + n * self.k
        if not isinstance(value, int) or value > 0:
            engine.wait_ge(self.sem, value)


class Signals:

    def __init__(self, mem):
        self.mem, self.sems, self.base, self.open = mem, {}, {}, {}

    def get(self, name, per_group=1):
        if name not in self.sems:
            self.sems[name], self.base[name] = self.mem.sem(name), 0
        self.open[name] = per_group
        return Signal(self.sems[name], self.base[name], per_group)

    def once(self, name, count):
        signal = self.get(name)
        del self.open[name]
        self.base[name] += count
        return signal

    def close_layer(self, groups):
        for name, k in self.open.items():
            self.base[name] += groups * k
        self.open = {}



class Chain:

    def __init__(self, engine, signals, name):
        if name not in signals.sems:
            signals.sems[name], signals.base[name] = signals.mem.sem(name), 0
        self.engine, self.signals, self.name = engine, signals, name

    def __call__(self, instruction):
        instruction.then_inc(self.signals.sems[self.name], 1)
        self.signals.base[self.name] += 1
        self.engine.wait_ge(self.signals.sems[self.name], self.signals.base[self.name])

    def value(self):
        return self.signals.base[self.name]


def conditioning(nc, mem, sg, T, K):
    x_all = K["x"]
    stage = x_all.rearrange("p g k t -> p (g k t)")
    at = [6 * KT * GT]

    def staged(cols):
        a = stage[:, at[0]:at[0] + cols]
        at[0] += cols
        return a

    w_mod = staged(KT * 6 * D).rearrange("p (k n) -> p k n", k=KT)
    w_c = staged(KT * 2 * D).rearrange("p (k n) -> p k n", k=KT)
    w_f1 = staged(KT * 2 * D).rearrange("p (k n) -> p k n", k=KT)
    w_f2 = staged(KT * 2 * D).rearrange("p (k n) -> p k n", k=KT)
    w_sq = staged(KT * D).rearrange("p (k n) -> p k n", k=KT)
    w_t1 = staged(KT * 2 * D).rearrange("p (k n) -> p k n", k=KT)
    w_t2 = staged(KT * 4 * D).rearrange("p (k n) -> p k n", k=KT)
    loads = [(w_mod, "L0_cond_Wm"), (w_c, "L0_cond_Wc"), (w_f1, "L1_cond_film1_w"), (w_f2, "L1_cond_film2_w"),
             (w_sq, "WselfT_q"), (w_t1, "L3_cond_w_t1"), (w_t2, "L3_cond_w_t2")]

    with ExitStack() as ctx:
        m = Mem(nc, ctx)
        cond = m.sb("condT", [P, KT, B])
        raw = m.sb("raw_mod", [P, 12, B])
        cvec = m.sb("cvec", [P, 12])
        q = m.sb("svec", [P, 24])
        cs = m.sb("cs_tab", [P, S])
        sn = m.sb("sn_tab", [P, S])
        tmp = m.sb("tmp_tab", [P, 2, S])
        tp = m.sb("tp_act", [P, KT, B])
        tg = m.sb("tp_gate", [P, KT, B])
        ps = ctx.enter_context(nc.psum_tensor("ps_mod", [P, 4, 4, B], F32))
        d_load = sg.get("cond_loads", 0)
        d_small = sg.get("small_loads", 0)
        s_mm, s_ev = mem.sem("mod_products"), mem.sem("mod_evacuated")
        s_tp, s_swi = mem.sem("swiglu_input"), mem.sem("swiglu_gate")
        sn_ready, sn_done = mem.sem("angle_ready"), mem.sem("sine_done")
        bias = K["bias"]

        jobs = [(w_mod, 0, 4), (w_mod, 4, 4), (w_mod, 8, 4), (w_c, 0, 4), (w_f1, 0, 4), (w_f2, 0, 4), (w_sq, 0, 2),
                (w_t1, 0, 4), (w_t2, 0, 4), (w_t2, 4, 4)]

        block = ctx.enter_context(nc.Block())

        @block.sync
        def _(sp):
            for dst, src in ((cond, T["condT"]), (K["bias"], T["vectors"]), (K["consts"], T["consts"]),
                             (cvec[:, 0:3], T["lam"])):
                sp.dma_start(dst[:], src[:]).then_inc(d_small.sem, 16)
            for dst, name in loads:
                sp.dma_start(dst, T[name].rearrange("(k p) n -> p k n", p=P)).then_inc(d_load.sem, 16)
            for g in range(6):
                sp.dma_start(x_all[:, g], T["x"][:, g]).then_inc(K["x_loaded"], 16)
            for dst, src in K["weights_first"]:
                sp.dma_start(dst, src).then_inc(K["w_loaded"], 16)
            sp.wait_ge(K["x_loaded"], 6 * 16)
            sp.wait_ge(K["w_loaded"], 16 * len(K["weights_first"]))

        @block.tensor
        def _(pe):
            pe.wait_ge(d_small.sem, 16 * 4)
            pe.wait_ge(d_load.sem, 16 * len(loads))
            for i, (w, first, tiles) in enumerate(jobs):
                if i >= 4:
                    pe.wait_ge(s_ev, i - 3)
                if i == 8:
                    pe.wait_ge(s_swi, 1)
                rhs = tp if i >= 8 else cond
                for t in range(tiles):
                    for k in range(KT):
                        c = (first + t) * P
                        last = nc.tensor.matmul(ps[:, i % 4, t], w[:, k, c:c + P], rhs[:, k], start=(k == 0), stop=(k == KT - 1))
                last.then_inc(s_mm, 1)

        @block.scalar
        def _(act):
            act.wait_ge(d_small.sem, 16 * 4)
            act.wait_ge(sn_ready, 1)
            nc.scalar.activation(q[:, 0:1], cvec[:, 2:3], ACT.Exp).then_inc(sn_done, 1)
            act.wait_ge(sn_ready, 2)
            nc.scalar.activation(q[:, 2:3], q[:, 1:2], ACT.Exp).then_inc(sn_done, 1)
            act.wait_ge(sn_ready, 3)
            nc.scalar.activation(q[:, 6:8], q[:, 4:6], ACT.Sin).then_inc(sn_done, 1)
            act.wait_ge(s_tp, 1)
            nc.scalar.activation(tg[:], tg[:], ACT.Silu).then_inc(s_tp, 1)

        @block.vector
        def _(v):
            ch = Chain(v, sg, "vector_chain")
            v.wait_ge(d_small.sem, 16 * 4)
            ch(nc.vector.memset(K["minus_half"][:], -0.5))
            ch(nc.vector.memset(K["ones"][:], 1.0))
            ch(nc.vector.memset(K["mean"][:], 1.0 / D))

            lr, li, sgn = cvec[:, 0:1], cvec[:, 1:2], K["sign"]
            TT, TS = nc.vector.tensor_tensor, nc.vector.tensor_scalar
            nc.vector.memset(q[:, 3:4], 0.0).then_inc(sn_ready, 1)
            v.wait_ge(sn_done, 1)
            TT(q[:, 1:2], lr, q[:, 0:1], ALU.mult).then_inc(sn_ready, 1)
            ch(TT(q[:, 3:4], li, q[:, 0:1], ALU.mult))
            ROUND = 12582912.0
            ch(TS(q[:, 8:9], q[:, 3:4], 1.0 / (2 * np.pi), ROUND, ALU.mult, ALU.add))
            ch(TS(q[:, 8:9], q[:, 8:9], -ROUND, None, ALU.add))
            c1 = 6.28125
            c2 = 0.0019350051879882812
            c3 = 2 * np.pi - c1 - c2
            for c in (c1, c2, c3):
                ch(TS(q[:, 9:10], q[:, 8:9], -c, None, ALU.mult))
                ch(TT(q[:, 3:4], q[:, 3:4], q[:, 9:10], ALU.add))
            ch(TS(q[:, 3:4], q[:, 3:4], float(-np.pi), float(np.pi), ALU.max, ALU.min))
            PI = 3.1415925
            ch(TS(q[:, 4:5], q[:, 3:4], 0.5, None, ALU.mult))
            ch(TS(q[:, 5:6], q[:, 4:5], float(np.pi / 2), PI, ALU.add, ALU.min))
            v.wait_ge(sn_done, 2)
            nc.vector.tensor_scalar_max(q[:, 5:6], q[:, 5:6], 0.0).then_inc(sn_ready, 1)
            v.wait_ge(sn_done, 3)
            s, c = q[:, 10:11], q[:, 11:12]
            ch(TT(s, q[:, 6:7], q[:, 7:8], ALU.mult))
            ch(TS(s, s, 2.0, None, ALU.mult))
            ch(TT(c, q[:, 6:7], q[:, 6:7], ALU.mult))
            ch(TS(c, c, -2.0, 1.0, ALU.mult, ALU.add))
            nr, ni, den, cr, ci = (q[:, k:k + 1] for k in range(12, 17))
            u0, u1 = q[:, 17:18], q[:, 18:19]
            ch(TT(nr, c, q[:, 2:3], ALU.mult))
            ch(TS(nr, nr, -1.0, None, ALU.add))
            ch(TT(ni, s, q[:, 2:3], ALU.mult))
            ch(TT(den, lr, lr, ALU.mult))
            ch(TT(u0, li, li, ALU.mult))
            ch(TT(den, den, u0, ALU.add))
            ch(nc.vector.reciprocal(den, den))
            ch(TT(u0, nr, lr, ALU.mult))
            ch(TT(u1, ni, li, ALU.mult))
            ch(TT(cr, u0, u1, ALU.add))
            ch(TT(cr, cr, den, ALU.mult))
            ch(TT(u0, ni, lr, ALU.mult))
            ch(TT(u1, nr, li, ALU.mult))
            ch(TT(ci, u0, u1, ALU.subtract))
            ch(TT(ci, ci, den, ALU.mult))
            ch(nc.vector.memset(cs[:, 0:1], 1.0))
            ch(nc.vector.memset(sn[:, 0:1], 0.0))
            h = 1
            while h < S:
                ch(TS(cs[:, h:2 * h], cs[:, 0:h], c, None, ALU.mult))
                ch(TS(tmp[:, 0, 0:h], sn[:, 0:h], s, None, ALU.mult))
                ch(TS(sn[:, h:2 * h], sn[:, 0:h], c, None, ALU.mult))
                ch(TS(tmp[:, 1, 0:h], cs[:, 0:h], s, None, ALU.mult))
                ch(TT(cs[:, h:2 * h], cs[:, h:2 * h], tmp[:, 0, 0:h], ALU.subtract))
                ch(TT(sn[:, h:2 * h], sn[:, h:2 * h], tmp[:, 1, 0:h], ALU.add))
                ch(TT(u0, c, s, ALU.mult))
                ch(TT(u1, s, s, ALU.mult))
                ch(TT(c, c, c, ALU.mult))
                ch(TT(c, c, u1, ALU.subtract))
                ch(TS(s, u0, 2.0, None, ALU.mult))
                h *= 2
            ch(TS(K["turn_in"][:, 0], cs[:], cr, None, ALU.mult))
            ch(TS(tmp[:, 0], sn[:], ci, None, ALU.mult))
            ch(TT(K["turn_in"][:, 0], K["turn_in"][:, 0], tmp[:, 0], ALU.add))
            ch(TS(K["turn_in"][:, 1], cs[:], ci, None, ALU.mult))
            ch(TS(tmp[:, 0], sn[:], cr, None, ALU.mult))
            ch(TT(K["turn_in"][:, 1], K["turn_in"][:, 1], tmp[:, 0], ALU.subtract))
            ch(TS(K["turn_in"][:, 1], K["turn_in"][:, 1], sgn, None, ALU.mult))
            ch(TS(K["turn_out"][:, 0], cs[:], sgn, -2.0, ALU.mult, ALU.mult))
            ch(TS(K["turn_out"][:, 1], sn[:], -2.0, None, ALU.mult))
            dec = K["decay"].rearrange("p (b s) -> p b s", s=S)
            ch(nc.vector.memset(K["decay"][:], 1.0))
            ch(TS(K["decay"][:], K["decay"][:], q[:, 2:3], None, ALU.mult))
            ch(nc.vector.memset(dec[:, :, 0:1], 0.0))

            v.wait_ge(d_load.sem, 16 * len(loads))

            def bias_of(col, tiles):
                return bias[:, col:col + tiles].unsqueeze(2).broadcast_to([P, tiles, B])

            def add_bias(i, dst, col, tiles=4, step=1):
                v.wait_ge(s_mm, i + 1)
                nc.vector.tensor_tensor(dst, ps[:, i % 4, 0:tiles], bias_of(col, tiles), ALU.add).then_inc(s_ev, 1)
                v.wait_ge(s_ev, i + 1)

            V = K["vec_at"]
            add_bias(0, raw[:, 0:4], V["L0_cond_bm"])
            add_bias(1, raw[:, 4:8], V["L0_cond_bm"] + 4)
            add_bias(2, raw[:, 8:12], V["L0_cond_bm"] + 8)
            ch(nc.vector.tensor_copy(K["l0_shift"][:], raw[:, 0:2]))
            ch(nc.vector.tensor_scalar_add(K["l0_scale"][:], raw[:, 2:4], 1.0))
            ch(nc.vector.tensor_copy(K["l0_gate"][:], raw[:, 4:6]))
            ch(nc.vector.tensor_copy(K["l0_gate_ff"][:], raw[:, 10:12]))
            add_bias(3, raw[:, 0:4], V["L0_cond_bc"])
            ch(nc.vector.tensor_scalar_add(raw[:, 0:2], raw[:, 0:2], 1.0))
            ch(nc.vector.tensor_scalar_add(raw[:, 8:10], raw[:, 8:10], 1.0))
            ch(nc.vector.tensor_tensor(K["l0_scale_ff"][:], raw[:, 0:2], raw[:, 8:10], ALU.mult))
            ch(nc.vector.tensor_tensor(raw[:, 2:4], raw[:, 2:4], raw[:, 8:10], ALU.mult))
            ch(nc.vector.tensor_tensor(K["l0_shift_ff"][:], raw[:, 2:4], raw[:, 6:8], ALU.add))
            for i, name, norm, film in ((4, "l1a", "L1_cond_norm1_w", "L1_cond_film1_b"), (5, "l1b", "L1_cond_norm2_w", "L1_cond_film2_b")):
                add_bias(i, raw[:, 0:4], V[film])
                ch(nc.vector.tensor_scalar_add(raw[:, 0:2], raw[:, 0:2], 1.0))
                ch(nc.vector.tensor_tensor(K[name + "_scale"][:], raw[:, 0:2], bias_of(V[norm], 2), ALU.mult))
                ch(nc.vector.tensor_copy(K[name + "_shift"][:], raw[:, 2:4]))
            v.wait_ge(s_mm, 7)
            nc.vector.tensor_copy(K["l2_q"][:], ps[:, 6 % 4, 0:2]).then_inc(s_ev, 1)
            v.wait_ge(s_ev, 7)
            add_bias(7, raw[:, 0:4], V["L3_cond_b_t1"])
            ch(nc.vector.tensor_copy(tp[:], raw[:, 0:2]))
            nc.vector.tensor_copy(tg[:], raw[:, 2:4]).then_inc(s_tp, 1)
            v.wait_ge(s_tp, 2)
            nc.vector.tensor_tensor(tp[:], tp[:], tg[:], ALU.mult).then_inc(s_swi, 1)
            for i, name, norm in ((8, "l3a", "L3_cond_g1"), (9, "l3b", "L3_cond_g2")):
                add_bias(i, raw[:, 0:4], V["L3_cond_b_t2"] + 4 * (i - 8))
                ch(nc.vector.tensor_copy(K[name + "_shift"][:], raw[:, 0:2]))
                ch(nc.vector.tensor_scalar_add(raw[:, 2:4], raw[:, 2:4], 1.0))
                ch(nc.vector.tensor_tensor(K[name + "_scale"][:], raw[:, 2:4], bias_of(V[norm], 2), ALU.mult))


class Norm:

    CHUNKS = GT // P

    def __init__(self, nc, sg, K, name, src, src_ready, out, center, eps, scale, shift, ps, buffers):
        self.nc, self.K, self.src, self.src_ready, self.out = nc, K, src, src_ready, out
        self.center, self.eps, self.scale, self.shift, self.ps = center, eps, scale, shift, ps
        self.sum, self.sq, self.inv = buffers
        if center:
            self.summed = sg.get(name + "_summed")
            self.meaned = sg.get(name + "_meaned")
            self.centered = sg.get(name + "_centered")
        self.squared = sg.get(name + "_squared")
        self.squares_summed = sg.get(name + "_squares_summed")
        self.varied = sg.get(name + "_varied")
        self.guarded = sg.get(name + "_guarded")
        self.inverted = sg.get(name + "_inverted")
        self.diagonal = sg.get(name + "_diagonal")
        self.spread = sg.get(name + "_spread")
        self.normed = sg.get(name + "_normed")
        self.scaled = sg.get(name + "_scaled")
        self.done = sg.get(name + "_done")

    def vector_sum(self, v, n, w):
        self.src_ready(v, n)
        x = self.src(n, w)
        self.nc.vector.tensor_tensor(self.sum[:], x[:, 0], x[:, 1], ALU.add).then_inc(self.summed.sem, 1)

    def tensor_mean(self, pe, n, w):
        pe.wait_ge(self.summed.sem, self.summed.after(n))
        self.nc.tensor.matmul(self.ps, self.K["mean"][:], self.sum[:], start=True, stop=True).then_inc(self.meaned.sem, 1)

    def vector_center(self, v, n, w):
        v.wait_ge(self.meaned.sem, self.meaned.after(n))
        mean = self.ps.unsqueeze(1).broadcast_to([P, KT, GT])
        self.nc.vector.tensor_tensor(self.out(w), self.src(n, w), mean, ALU.subtract).then_inc(self.centered.sem, 1)

    def scalar_square(self, act, n, w):
        if self.center:
            act.wait_ge(self.centered.sem, self.centered.after(n))
            x = self.out(w)
        else:
            self.src_ready(act, n)
            x = self.src(n, w)
        self.squares_summed.wait(act, n, -1)
        self.nc.scalar.activation(self.sq[:], x, ACT.Square).then_inc(self.squared.sem, 1)

    def pool_sum(self, pool, n, w):
        pool.wait_ge(self.squared.sem, self.squared.after(n))
        self.spread.wait(pool, n, -1)
        self.nc.gpsimd.tensor_tensor(self.sum[:], self.sq[:, 0], self.sq[:, 1], ALU.add).then_inc(self.squares_summed.sem, 1)

    def tensor_variance(self, pe, n, w):
        pe.wait_ge(self.squares_summed.sem, self.squares_summed.after(n))
        for c in range(self.CHUNKS):
            last = self.nc.tensor.matmul(self.ps[:, c:c + 1], self.sum[:, c * P:(c + 1) * P], self.K["mean"][:, 0:1], start=True, stop=True)
        last.then_inc(self.varied.sem, 1)

    def vector_guard(self, v, n, w):
        v.wait_ge(self.varied.sem, self.varied.after(n))
        self.inverted.wait(v, n, -1)
        self.nc.vector.tensor_scalar(self.inv[:], self.ps[:, 0:self.CHUNKS], self.eps, None, ALU.add).then_inc(self.guarded.sem, 1)

    def pool_invert(self, pool, n, w):
        pool.wait_ge(self.guarded.sem, self.guarded.after(n))
        half = self.K["minus_half"][:, 0:self.CHUNKS]
        self.nc.gpsimd.tensor_tensor(self.inv[:], self.inv[:], half, ALU.pow).then_inc(self.inverted.sem, 1)

    def vector_diagonal(self, v, n, w):
        v.wait_ge(self.inverted.sem, self.inverted.after(n))
        shape = [P, self.CHUNKS, P]
        self.nc.vector.tensor_tensor(self.sum[:].rearrange("p (c t) -> p c t", t=P), self.K["ident"].unsqueeze(1).broadcast_to(shape),
                                     self.inv[:].unsqueeze(2).broadcast_to(shape), ALU.mult).then_inc(self.diagonal.sem, 1)

    def tensor_spread(self, pe, n, w):
        pe.wait_ge(self.diagonal.sem, self.diagonal.after(n))
        self.nc.tensor.matmul(self.ps, self.K["ones"][:], self.sum[:], start=True, stop=True).then_inc(self.spread.sem, 1)

    def vector_apply(self, v, n, w):
        v.wait_ge(self.spread.sem, self.spread.after(n))
        rstd = self.ps.unsqueeze(1).broadcast_to([P, KT, GT])
        out, bs = self.out(w), bass.ds(n * GB, GB)
        x = out if self.center else self.src(n, w)
        self.nc.vector.tensor_tensor(out, x, rstd, ALU.mult).then_inc(self.normed.sem, 1)
        v.wait_ge(self.normed.sem, self.normed.after(n))
        self.nc.vector.tensor_tensor(tokens(out), tokens(out), per_batch(self.scale, bs), ALU.mult).then_inc(self.scaled.sem, 1)
        v.wait_ge(self.scaled.sem, self.scaled.after(n))
        self.nc.vector.tensor_tensor(tokens(out), tokens(out), per_batch(self.shift, bs), ALU.add).then_inc(self.done.sem, 1)

    def steps(self, who, name):
        own = {"pe": ("mean", "variance", "spread"), "act": ("square",), "pool": ("sum", "invert"),
               "dve": ("sum", "center", "guard", "diagonal", "apply")}[who]
        of = {"mean": self.tensor_mean, "variance": self.tensor_variance, "spread": self.tensor_spread, "square": self.scalar_square,
              "invert": self.pool_invert, "center": self.vector_center, "guard": self.vector_guard, "diagonal": self.vector_diagonal,
              "apply": self.vector_apply, "sum": self.pool_sum if who == "pool" else self.vector_sum}
        if not self.center:
            own = [k for k in own if k not in ("mean", "center") and (who, k) != ("dve", "sum")]
        return {f"{name}.{k}": of[k] for k in own}


def split_products(nc, ps, pairs, start=True, stop=True):
    products = [(w[i], x[0]) for w, x in pairs for i in range(2)] + [(w[0], x[1]) for w, x in pairs]
    for i, (w, x) in enumerate(products):
        last = nc.tensor.matmul(ps, w, x, start=(start and i == 0), stop=(stop and i == len(products) - 1))
    return last


class SplitWeights:

    def __init__(self, nc, sg, weights):
        self.nc, self.weights = nc, weights
        self.high, self.low = sg.once("weights_high", len(weights)), sg.once("weights_low", len(weights))

    def scalar_high(self, act):
        for whole, high, _ in self.weights:
            self.nc.scalar.copy(high, whole).then_inc(self.high.sem, 1)

    def pool_low(self, pool):
        for i, (whole, high, low) in enumerate(self.weights):
            self.high.wait(pool, i)
            self.nc.gpsimd.tensor_tensor(low, whole, high, ALU.subtract).then_inc(self.low.sem, 1)

    def parts(self, i):
        return self.weights[i][1:]


class Split:

    def __init__(self, nc, sg, name, whole, high, low, ready):
        self.nc, self.whole, self.high, self.low, self.ready = nc, whole, high, low, ready
        self.highs, self.done = sg.get(name + "_high"), sg.get(name + "_low")

    def scalar_high(self, act, n, w):
        act.wait_ge(self.ready.sem, self.ready.after(n))
        self.nc.scalar.copy(self.high[:, w], self.whole[:, w]).then_inc(self.highs.sem, 1)

    def vector_low(self, v, n, w):
        v.wait_ge(self.highs.sem, self.highs.after(n))
        self.nc.vector.tensor_tensor(self.low[:, w], self.whole[:, w], self.high[:, w], ALU.subtract).then_inc(self.done.sem, 1)

    def parts(self, w, k):
        return self.high[:, w, k], self.low[:, w, k]


class FeedForward:

    LAG = 2
    BUFFERS = 3

    def __init__(self, nc, sg, weights, b1, func, m, ps_h, ps_o, hidden, out_read):
        self.nc, self.weights, self.b1, self.func, self.m = nc, weights, b1, func, m
        self.ps_h, self.ps_o, self.out_read = ps_h, ps_o, out_read
        self.h, self.h_high, self.h_low = hidden
        self.up = sg.get("ff_up", HJ)
        self.act = sg.get("ff_activated", HJ)
        self.high = sg.get("ff_hidden_high", HJ)
        self.low = sg.get("ff_hidden_low", HJ)
        self.down = sg.get("ff_down", HJ)

    def tensor_up(self, pe, n, j, u):
        if j == 0:
            pe.wait_ge(self.m.done.sem, self.m.done.after(n))
            if isinstance(n, int) and n == 0:
                self.weights.low.wait(pe, 1)
        self.act.wait(pe, n, j - 2)
        high, low = self.weights.parts(0)
        c = slice(j * P, (j + 1) * P)
        pairs = [((high[:, k, c], low[:, k, c]), self.m.parts(u, k)) for k in range(KT)]
        split_products(self.nc, self.ps_h[:, j % 2], pairs).then_inc(self.up.sem, 1)

    def scalar_activate(self, act, n, j):
        b = j % self.BUFFERS
        act.wait_ge(self.up.sem, self.up.after(n, j))
        self.down.wait(act, n, j - self.BUFFERS if j >= self.BUFFERS else -1)
        self.nc.scalar.activation(self.h[:, b], self.ps_h[:, j % 2], self.func, bias=self.b1[:, j:j + 1]).then_inc(self.act.sem, 1)
        act.wait_ge(self.act.sem, self.act.after(n, j))
        self.nc.scalar.copy(self.h_high[:, b], self.h[:, b]).then_inc(self.high.sem, 1)

    def pool_low(self, pool, n, j):
        b = j % self.BUFFERS
        pool.wait_ge(self.high.sem, self.high.after(n, j))
        self.nc.gpsimd.tensor_tensor(self.h_low[:, b], self.h[:, b], self.h_high[:, b], ALU.subtract).then_inc(self.low.sem, 1)

    def tensor_down(self, pe, n, j):
        b = j % self.BUFFERS
        pe.wait_ge(self.low.sem, self.low.after(n, j))
        if j == 0:
            self.out_read(pe, n)
        high, low = self.weights.parts(1)
        for t in range(KT):
            c = slice(t * P, (t + 1) * P)
            pairs = [((high[:, j, c], low[:, j, c]), (self.h_high[:, b], self.h_low[:, b]))]
            last = split_products(self.nc, self.ps_o[:, t], pairs, start=(j == 0), stop=(j == HJ - 1))
        last.then_inc(self.down.sem, 1)

    def part(self, who, engine):
        def part(n, u, g):
            j = g // 2
            if g % 2 == 0:
                if who == "pe":
                    self.tensor_up(engine, n, j, u)
                elif who == "act":
                    self.scalar_activate(engine, n, j)
                elif who == "pool":
                    self.pool_low(engine, n, j)
            elif who == "pe" and j >= self.LAG:
                self.tensor_down(engine, n, j - self.LAG)
        return part

    def tensor_end(self, pe):
        def end(n, u):
            for j in range(HJ - self.LAG, HJ):
                self.tensor_down(pe, n, j)
        return end


def three_stage(engine, who, table, steps, part, parts, end=None):
    after = [[name for name, at in table if at.get(who) == g] for g in range(parts)]
    early = {name for name, at in table if at.get("ahead") == 2}
    assert sum(map(len, after)) == len(steps), (who, sorted(steps), after)

    def body(n, m, p, u):
        for g in range(parts):
            if n is not None:
                part(n, u, g)
            for name in after[g]:
                group, w = (p, u) if name.startswith("norm1") or name in early else (m, 1 - u)
                if group is not None:
                    steps[name](engine, group, w)
        if n is not None and end:
            end(n, u)

    body(None, None, 0, 0)
    body(None, 0, 1, 1)
    body(0, 1, 2, 0)
    with engine.Fori(1, NG - 4, 2) as i:
        body(i, i + 1, i + 2, 1)
        body(i + 1, i + 2, i + 3, 0)
    body(NG - 3, NG - 2, NG - 1, 1)
    body(NG - 2, NG - 1, None, 0)
    body(NG - 1, None, None, 1)


L0_TABLE = [
    ("norm1.sum", dict(dve=0)), ("c", dict(pe=4)), ("norm1.mean", dict(pe=4)), ("norm1.center", dict(dve=2)), ("norm1.square", dict(act=4)), ("norm1.sum", dict(pool=4)),
    ("skip", dict(dve=4)), ("norm2.sum", dict(dve=4)),
    ("norm1.variance", dict(pe=8)), ("norm1.guard", dict(dve=6)), ("norm1.invert", dict(pool=6)), ("norm1.diagonal", dict(dve=6)),
    ("norm2.mean", dict(pe=8)), ("norm1.spread", dict(pe=10)), ("norm2.center", dict(dve=8)), ("norm2.square", dict(act=8)), ("norm2.sum", dict(pool=8)),
    ("norm1.apply", dict(dve=8)),
    ("norm2.variance", dict(pe=11)), ("norm2.guard", dict(dve=10)), ("norm2.invert", dict(pool=9)), ("norm2.diagonal", dict(dve=11)),
    ("norm2.spread", dict(pe=14)), ("norm2.apply", dict(dve=12)), ("m_high", dict(act=14)), ("m_low", dict(dve=13)),
    ("b", dict(pe=15, ahead=2)), ("turn_in", dict(dve=15, pool=15, ahead=2)), ("scan", dict(dve=15, pool=15, ahead=2)),
]
L1_TABLE = [
    ("scores", dict(pe=0)), ("softmax_a", dict(dve=0)), ("exp", dict(act=0)), ("v", dict(pe=0, act=0)), ("softmax_b", dict(dve=1)),
    ("norm1.square", dict(act=3)), ("norm1.sum", dict(pool=3)), ("transposes", dict(pe=5, act=5)),
    ("norm1.variance", dict(pe=7)), ("norm1.guard", dict(dve=5)), ("norm1.invert", dict(pool=5)),
    ("attend", dict(pe=7, dve=6)), ("norm1.diagonal", dict(dve=6)), ("proj", dict(pe=9, dve=8)), ("norm2.square", dict(act=9)), ("norm2.sum", dict(pool=9)),
    ("norm1.spread", dict(pe=9)), ("norm1.apply", dict(dve=9)), ("in_high", dict(act=12, ahead=2)), ("in_low", dict(dve=12, ahead=2)),
    ("norm2.variance", dict(pe=12)), ("norm2.guard", dict(dve=11)), ("norm2.invert", dict(pool=11)), ("norm2.diagonal", dict(dve=11)),
    ("norm2.spread", dict(pe=14)), ("norm2.apply", dict(dve=13)), ("m_high", dict(act=14)), ("q", dict(dve=14, ahead=2)), ("m_low", dict(dve=14)),
    ("qk", dict(pe=15, ahead=2)), ("k", dict(act=15, ahead=2)),
]


def layer0(nc, mem, sg, T, K):
    x_all = K["x"]
    V, bias = K["vec_at"], K["bias"]
    with ExitStack() as ctx:
        m = Mem(nc, ctx)
        psum = lambda name, n: ctx.enter_context(nc.psum_tensor(name, [P, n, GT], F32))
        x1 = m.sb("l0_x1", [P, 2, KT, GT])
        min_, m_low = m.sb_in_place("l0_m", [P, 2, KT, GT])
        u_in = m.sb("l0_u", [P, 2, KT, GT])
        m_high = m.sb("l0_m_high", [P, 2, KT, GT], R32)
        bz = m.sb("l0_bz", [P, 2, GT])
        z = m.sb("l0_z", [P, GT])
        zt = m.sb("l0_zt", [P, 2, GT])
        norm_bufs = [(m.sb(f"l0_sum{i}", [P, GT]), m.sb(f"l0_sq{i}", [P, KT, GT]), m.sb(f"l0_inv{i}", [P, Norm.CHUNKS])) for i in range(2)]
        hidden, hidden_low = m.sb_in_place("l0_h", [P, FeedForward.BUFFERS, GT])
        hidden_high = m.sb("l0_h_high", [P, FeedForward.BUFFERS, GT], R32)
        ps_h, ps_o, ps_n, ps_f = psum("l0_psh", 2), psum("l0_pso", 2), psum("l0_psn", 2), psum("l0_psf", 2)

        s_u = sg.get("s5_inputs")
        s_turn = sg.get("s5_turned", 2)
        s_tsum = sg.get("s5_turned_summed")
        s_scan = sg.get("s5_scanned")
        s_cos = sg.get("s5_cosine_part")
        s_sin = sg.get("s5_sine_part")
        s_y = sg.get("s5_outputs")
        s_ay = sg.get("s5_skip", 2)
        s_g = sg.get("s5_gated")
        s_x1 = sg.get("x1_ready")
        s_ffo = sg.get("ff_out_read")
        s_xo = sg.get("x_updated")

        def x_loaded(e, n):
            e.wait_ge(K["x_loaded"], (n + 1) * 16)

        def x1_ready(e, n):
            e.wait_ge(s_x1.sem, s_x1.after(n))

        def no_wait(e, n):
            pass

        n1 = Norm(nc, sg, K, "norm1", lambda n, w: x_all[:, n], x_loaded, lambda w: u_in[:, w], True, 1e-5, K["l0_scale"], K["l0_shift"], ps_n[:, 0], norm_bufs[0])
        n2 = Norm(nc, sg, K, "norm2", lambda n, w: x1[:, w], x1_ready, lambda w: min_[:, w], True, 1e-5,
                  K["l0_scale_ff"], K["l0_shift_ff"], ps_n[:, 1], norm_bufs[1])

        def out_read(pe, n):
            s_ffo.wait_before(pe, n)

        weights = SplitWeights(nc, sg, [(K["l0_w1"], K["l0_w1_high"][:], K["l0_w1_low"][:]),
                                        (K["l0_w2"], m.sb("l0_w2_high", [P, HJ, D], R32)[:], K["l0_w2_low"][:])])
        split = Split(nc, sg, "m", min_, m_high, m_low, n2.done)
        ff = FeedForward(nc, sg, weights, bias[:, V["L0_cond_b1"]:], ACT.Gelu_apprx_tanh, split, ps_h, ps_o, (hidden, hidden_high, hidden_low), out_read)

        def bcast_turn(t, k):
            return t[:, k:k + 1].broadcast_to([P, GB, S])

        bs3 = lambda a: a.rearrange("p (b s) -> p b s", s=S)
        block = ctx.enter_context(nc.Block())

        @block.sync
        def _(sp):
            for g in range(6, NG):
                sp.dma_start(x_all[:, g], T["x"][:, g]).then_inc(K["x_loaded"], 16)
                sp.wait_ge(K["x_loaded"], (g + 1) * 16)

        @block.tensor
        def _(pe):
            def b_products(pe, n, w):
                pe.wait_ge(n1.done.sem, n1.done.after(n))
                for c in range(2):
                    for k in range(KT):
                        last = nc.tensor.matmul(ps_f[:, c], K["s5_b"][:, c, k], u_in[:, w, k], start=(k == 0), stop=(k == KT - 1))
                last.then_inc(s_u.sem, 1)

            def c_products(pe, n, w):
                pe.wait_ge(s_cos.sem, s_cos.after(n))
                pe.wait_ge(s_sin.sem, s_sin.after(n))
                for t in range(KT):
                    for c in range(2):
                        last = nc.tensor.matmul(ps_f[:, t], K["s5_c"][:, c, t * P:(t + 1) * P], zt[:, c], start=(c == 0), stop=(c == 1))
                last.then_inc(s_y.sem, 1)

            steps = {"b": b_products, "c": c_products, **n1.steps("pe", "norm1"), **n2.steps("pe", "norm2")}
            three_stage(pe, "pe", L0_TABLE, steps, ff.part("pe", pe), 2 * HJ, ff.tensor_end(pe))

        @block.scalar
        def _(act):
            weights.scalar_high(act)
            steps = {**n1.steps("act", "norm1"), **n2.steps("act", "norm2"), "m_high": split.scalar_high}
            three_stage(act, "act", L0_TABLE, steps, ff.part("act", act), 2 * HJ)

        @block.gpsimd
        def _(pool):
            def turned_sum(pool, n, w):
                pool.wait_ge(s_turn.sem, s_turn.after(n))
                nc.gpsimd.tensor_tensor(bz[:, 0], bz[:, 0], bz[:, 1], ALU.add).then_inc(s_tsum.sem, 1)

            def sine_part(pool, n, w):
                pool.wait_ge(s_scan.sem, s_scan.after(n))
                nc.gpsimd.tensor_tensor(bs3(zt[:, 1]), bs3(z[:]), bcast_turn(K["turn_out"], 1), ALU.mult).then_inc(s_sin.sem, 1)

            weights.pool_low(pool)
            steps = {"turn_in": turned_sum, "scan": sine_part, **n1.steps("pool", "norm1"), **n2.steps("pool", "norm2")}
            three_stage(pool, "pool", L0_TABLE, steps, ff.part("pool", pool), 2 * HJ)

        @block.vector
        def _(v):
            def turn_in(v, n, w):
                v.wait_ge(s_u.sem, s_u.after(n))
                for c in range(2):
                    nc.vector.tensor_tensor(bs3(bz[:, c]), bs3(ps_f[:, c]), bcast_turn(K["turn_in"], c), ALU.mult).then_inc(s_turn.sem, 1)

            def scan(v, n, w):
                v.wait_ge(s_tsum.sem, s_tsum.after(n))
                nc.vector.tensor_tensor_scan(z[:], K["decay"][:], bz[:, 0], 0.0, ALU.mult, ALU.add).then_inc(s_scan.sem, 1)
                v.wait_ge(s_scan.sem, s_scan.after(n))
                nc.vector.tensor_tensor(bs3(zt[:, 0]), bs3(z[:]), bcast_turn(K["turn_out"], 0), ALU.mult).then_inc(s_cos.sem, 1)

            def skip(v, n, w):
                v.wait_ge(s_y.sem, s_y.after(n))
                s_xo.wait(v, n, -2)
                d0 = V["L0_cond_D_diag"]
                for t in range(KT):
                    nc.vector.scalar_tensor_tensor(x1[:, w, t], u_in[:, w, t], bias[:, d0 + t:d0 + t + 1], ps_f[:, t], ALU.mult, ALU.add).then_inc(s_ay.sem, 1)
                v.wait_ge(s_ay.sem, s_ay.after(n))
                nc.vector.tensor_tensor(tokens(x1[:, w]), tokens(x1[:, w]), per_batch(K["l0_gate"], bass.ds(n * GB, GB)), ALU.mult).then_inc(s_g.sem, 1)
                v.wait_ge(s_g.sem, s_g.after(n))
                nc.vector.tensor_tensor(x1[:, w], x1[:, w], x_all[:, n], ALU.add).then_inc(s_x1.sem, 1)

            def back(n, u):
                v.wait_ge(ff.down.sem, ff.down.after(n))
                b0 = V["L0_cond_b2"]
                gate = K["l0_gate_ff"]
                for t in range(KT):
                    g = gate[:, t, bass.ds(n * GB, GB)].unsqueeze(2).broadcast_to([P, GB, S])
                    last = nc.vector.scalar_tensor_tensor(bs3(x_all[:, n, t]), bs3(ps_o[:, t]), bias[:, b0 + t:b0 + t + 1], g, ALU.add, ALU.mult)
                last.then_inc(s_ffo.sem, 1)
                v.wait_ge(s_ffo.sem, s_ffo.after(n))
                nc.vector.tensor_tensor(x_all[:, n], x_all[:, n], x1[:, u], ALU.add).then_inc(s_xo.sem, 1)

            steps = {"turn_in": turn_in, "scan": scan, "skip": skip, "m_low": split.vector_low, **n1.steps("dve", "norm1"), **n2.steps("dve", "norm2")}
            three_stage(v, "dve", L0_TABLE, steps, lambda n, u, g: None, 2 * HJ, back)
            v.wait_ge(s_xo.sem, s_xo.after(NG - 1))
    sg.close_layer(NG)


def layer1(nc, mem, sg, T, K):
    x_all = K["x"]
    V, bias = K["vec_at"], K["bias"]
    SCALE = float(D) ** -0.5
    with ExitStack() as ctx:
        m = Mem(nc, ctx)
        psum = lambda name, n: ctx.enter_context(nc.psum_tensor(name, [P, n, GT], F32))
        x1 = m.sb("l1_x1", [P, 2, KT, GT])
        min_, m_low = m.sb_in_place("l1_m", [P, 2, KT, GT])
        h_in, h_low = m.sb_in_place("l1_in", [P, 2, KT, GT])
        h_high = m.sb("l1_in_high", [P, KT, GT], R32)
        squares = m.sb("l1_squares", [P, KT, GT])
        norm_bufs = [(m.sb(f"l1_sum{i}", [P, GT]), squares, m.sb(f"l1_inv{i}", [P, Norm.CHUNKS])) for i in range(2)]
        q = m.sb("l1_q", [P, KT, GT])
        k_ = m.sb("l1_k", [P, KT, GT])
        vt = m.sb("l1_v", [P, NP, D])
        sc = m.sb("l1_scores", [P, NP, P])
        pt = q[:, 0].rearrange("p (a n) -> p a n", n=P)
        mx = m.sb("l1_max", [P, NP])
        rs = m.sb("l1_sums", [P, NP])
        m_high = m.sb("l1_m_high", [P, 2, KT, GT], R32)
        hidden, hidden_low = m.sb_in_place("l1_h", [P, FeedForward.BUFFERS, GT])
        hidden_high = m.sb("l1_h_high", [P, FeedForward.BUFFERS, GT], R32)
        ps_h, ps_o, ps_n, ps_f = psum("l1_psh", 2), psum("l1_pso", 2), psum("l1_psn", 2), psum("l1_psf", 2)

        s_x1, s_ffo = sg.get("x1_ready"), sg.get("ff_out_read")
        s_qm, s_km, s_vm = sg.get("q_products", KT), sg.get("k_products", KT), sg.get("v_products")
        s_q, s_k, s_v = sg.get("q_ready", KT), sg.get("k_ready", KT), sg.get("v_ready")
        s_sm = sg.get("score_products")
        s_sc, s_mx, s_sub, s_exp = sg.get("scores_masked"), sg.get("scores_max"), sg.get("scores_minus_max"), sg.get("probs_exp")
        s_rs, s_rr, s_pn = sg.get("probs_summed"), sg.get("probs_inverted"), sg.get("probs_ready")
        s_tm, s_pt = sg.get("probs_transposed"), sg.get("probs_t_ready")
        s_om, s_o = sg.get("attn_products"), sg.get("attn_ready")
        s_pm = sg.get("proj_products")

        def no_wait(e, n):
            pass

        def x1_ready(e, n):
            e.wait_ge(s_x1.sem, s_x1.after(n))

        n1 = Norm(nc, sg, K, "norm1", lambda n, w: x_all[:, n], no_wait, lambda w: h_in[:, w], False, 1e-6,
                  K["l1a_scale"], K["l1a_shift"], ps_n[:, 0], norm_bufs[0])
        n2 = Norm(nc, sg, K, "norm2", lambda n, w: x1[:, w], x1_ready, lambda w: min_[:, w], False, 1e-6,
                  K["l1b_scale"], K["l1b_shift"], ps_n[:, 1], norm_bufs[1])
        ps_a = ps_n[:, 1]

        def out_read(pe, n):
            s_ffo.wait_before(pe, n)

        (w1, w1_low), (w2, w2_low) = m.sb_in_place("l1_w1", [P, KT, FF]), m.sb_in_place("l1_w2", [P, HJ, D])
        mlp_weights = [(w1[:], T["L1_cond_mlp_w1"].rearrange("(k p) n -> p k n", p=P)), (w2[:], T["L1_cond_mlp_w2"].rearrange("(k p) n -> p k n", p=P))]
        qkv_weights = SplitWeights(nc, sg, [(K["l1_w" + c][:], K["l1_wv_high"][:] if c == "v" else m.sb(f"l1_w{c}_high", [P, KT, D], R32)[:],
                                             K[f"l1_w{c}_low"][:]) for c in "qkv"])
        weights = SplitWeights(nc, sg, [(w1[:], K["l1_w1_high"][:], w1_low[:]), (w2[:], K["l1_w2_high"][:], w2_low[:])])
        split = Split(nc, sg, "m", min_, m_high, m_low, n2.done)
        ff = FeedForward(nc, sg, weights, bias[:, V["L1_cond_mlp_b1"]:], ACT.Gelu, split, ps_h, ps_o, (hidden, hidden_high, hidden_low), out_read)
        g_high, g_low = sg.get("in_high"), sg.get("in_low")

        def h_parts(w, k):
            return h_high[:, k], h_low[:, w, k]

        block = ctx.enter_context(nc.Block())

        @block.sync
        def _(sp):
            for dst, src in mlp_weights:
                sp.dma_start(dst, src).then_inc(K["w_loaded"], 16)
            sp.wait_ge(K["w_loaded"], 16 * len(K["weights_first"] + mlp_weights))
            for dst, src in K["weights_l2"]:
                sp.dma_start(dst, src).then_inc(K["w_loaded"], 16)
            sp.wait_ge(K["w_loaded"], 16 * len(K["weights_first"] + mlp_weights + K["weights_l2"]))

        @block.tensor
        def _(pe):
            def product(ps, w, rhs, t):
                for k in range(KT):
                    last = nc.tensor.matmul(ps, w[:, k, t * P:(t + 1) * P], rhs[:, k], start=(k == 0), stop=(k == KT - 1))
                return last

            def split_product(ps, i, w, t):
                high, low = qkv_weights.parts(i)
                c = slice(t * P, (t + 1) * P)
                return split_products(nc, ps, [((high[:, k, c], low[:, k, c]), h_parts(w, k)) for k in range(KT)])

            def queries_keys(pe, n, w):
                if isinstance(n, int) and n == 0:
                    pe.wait_ge(qkv_weights.low.sem, qkv_weights.low.after(2))
                pe.wait_ge(g_low.sem, g_low.after(n))
                for t in range(KT):
                    split_product(ps_f[:, t], 0, w, t).then_inc(s_qm.sem, 1)
                n2.done.wait(pe, n, -1)
                split_product(ps_a, 1, w, 0).then_inc(s_km.sem, 1)
                pe.wait_ge(s_q.sem, s_q.after(n, 0))
                split_product(ps_f[:, 0], 1, w, 1).then_inc(s_km.sem, 1)

            def values(pe, n, w):
                pe.wait_ge(s_q.sem, s_q.after(n))
                pe.wait_ge(s_k.sem, s_k.after(n))
                for p in range(NP):
                    dst = ps_f[:, p // 2, (p % 2) * D:(p % 2 + 1) * D]
                    c = slice(p * P, (p + 1) * P)
                    high, low = qkv_weights.parts(2)
                    pairs = [((h_high[:, k, c], h_low[:, w, k, c]), (high[:, k], low[:, k])) for k in range(KT)]
                    last = split_products(nc, dst, pairs)
                last.then_inc(s_vm.sem, 1)

            def scores(pe, n, w):
                pe.wait_ge(s_q.sem, s_q.after(n))
                pe.wait_ge(s_k.sem, s_k.after(n))
                for p in range(NP):
                    c = slice(p * P, (p + 1) * P)
                    for k in range(KT):
                        last = nc.tensor.matmul(ps_a[:, c], q[:, k, c], k_[:, k, c], start=(k == 0), stop=(k == KT - 1))
                last.then_inc(s_sm.sem, 1)

            def transposes(pe, n, w):
                pe.wait_ge(s_pn.sem, s_pn.after(n))
                for p in range(NP):
                    last = nc.tensor.transpose(ps_a[:, p * P:(p + 1) * P], sc[:, p], K["ident"])
                last.then_inc(s_tm.sem, 1)

            def attend(pe, n, w):
                pe.wait_ge(s_pt.sem, s_pt.after(n))
                pe.wait_ge(s_v.sem, s_v.after(n))
                for p in range(NP):
                    for t in range(KT):
                        last = nc.tensor.matmul(ps_f[:, t, p * P:(p + 1) * P], vt[:, p, t * P:(t + 1) * P], pt[:, p], start=True, stop=True)
                last.then_inc(s_om.sem, 1)

            def out_project(pe, n, w):
                pe.wait_ge(s_o.sem, s_o.after(n))
                for t in range(KT):
                    last = product(ps_f[:, t], K["l1_wo"], h_in[:, w], t)
                last.then_inc(s_pm.sem, 1)

            steps = {"qk": queries_keys, "v": values, "scores": scores, "transposes": transposes, "attend": attend, "proj": out_project,
                     **n1.steps("pe", "norm1"), **n2.steps("pe", "norm2")}
            three_stage(pe, "pe", L1_TABLE, steps, ff.part("pe", pe), 2 * HJ, ff.tensor_end(pe))

        @block.scalar
        def _(act):
            def keys(act, n, w):
                b0 = V["L1_cond_k_b"]
                for t in range(KT):
                    act.wait_ge(s_km.sem, s_km.after(n, t))
                    nc.scalar.activation(k_[:, t], (ps_a, ps_f[:, 0])[t], ACT.Identity, bias=bias[:, b0 + t:b0 + t + 1]).then_inc(s_k.sem, 1)

            def values(act, n, w):
                act.wait_ge(s_vm.sem, s_vm.after(n))
                nc.scalar.copy(vt[:].rearrange("p a n -> p (a n)"), ps_f[:].rearrange("p a n -> p (a n)")).then_inc(s_v.sem, 1)

            def exps(act, n, w):
                act.wait_ge(s_sub.sem, s_sub.after(n))
                nc.scalar.activation(sc[:], sc[:], ACT.Exp).then_inc(s_exp.sem, 1)

            def probs_t(act, n, w):
                act.wait_ge(s_tm.sem, s_tm.after(n))
                nc.scalar.copy(q[:, 0], ps_a).then_inc(s_pt.sem, 1)

            def m_high(act, n, w):
                split.scalar_high(act, n, w)
                if isinstance(n, int) and n == 0:
                    act.wait_ge(K["w_loaded"], 16 * len(K["weights_first"] + mlp_weights))
                    weights.scalar_high(act)

            def high(act, n, w):
                act.wait_ge(n1.done.sem, n1.done.after(n))
                s_vm.wait(act, n, -1)
                nc.scalar.copy(h_high[:], h_in[:, w]).then_inc(g_high.sem, 1)

            def norm1_square(act, n, w):
                n2.squares_summed.wait(act, n, -2)
                n1.scalar_square(act, n, w)

            def norm2_square(act, n, w):
                at = n if isinstance(n, int) and n == NG - 1 else n + 1
                act.wait_ge(n1.squares_summed.sem, n1.squares_summed.after(at))
                n2.scalar_square(act, n, w)

            qkv_weights.scalar_high(act)
            steps = {"k": keys, "in_high": high, "v": values, "exp": exps, "transposes": probs_t, "m_high": m_high, **n1.steps("act", "norm1"), **n2.steps("act", "norm2"),
                     "norm1.square": norm1_square, "norm2.square": norm2_square}
            three_stage(act, "act", L1_TABLE, steps, ff.part("act", act), 2 * HJ)

        @block.gpsimd
        def _(pool):
            def norm2_invert(pool, n, w):
                n2.pool_invert(pool, n, w)
                if isinstance(n, int) and n == 0:
                    weights.pool_low(pool)

            qkv_weights.pool_low(pool)
            steps = {**n1.steps("pool", "norm1"), **n2.steps("pool", "norm2"), "norm2.invert": norm2_invert}
            three_stage(pool, "pool", L1_TABLE, steps, ff.part("pool", pool), 2 * HJ)

        @block.vector
        def _(v):
            def queries(v, n, w):
                b0 = V["L1_cond_q_b"]
                for t in range(KT):
                    v.wait_ge(s_qm.sem, s_qm.after(n, t))
                    nc.vector.tensor_scalar(q[:, t], ps_f[:, t], bias[:, b0 + t:b0 + t + 1], None, ALU.add).then_inc(s_q.sem, 1)

            def softmax_a(v, n, w):
                v.wait_ge(s_sm.sem, s_sm.after(n))
                mask = K["block_mask"].unsqueeze(1).broadcast_to([P, NP, P])
                ps = ps_a.rearrange("p (a n) -> p a n", n=P)
                nc.vector.scalar_tensor_tensor(sc[:], ps, SCALE, mask, ALU.mult, ALU.add).then_inc(s_sc.sem, 1)
                v.wait_ge(s_sc.sem, s_sc.after(n))
                nc.vector.reduce_max(mx[:], sc[:], AX.X).then_inc(s_mx.sem, 1)
                v.wait_ge(s_mx.sem, s_mx.after(n))
                nc.vector.tensor_tensor(sc[:], sc[:], mx[:].unsqueeze(2).broadcast_to([P, NP, P]), ALU.subtract).then_inc(s_sub.sem, 1)

            def softmax_b(v, n, w):
                v.wait_ge(s_exp.sem, s_exp.after(n))
                nc.vector.reduce_sum(rs[:], sc[:], AX.X).then_inc(s_rs.sem, 1)
                v.wait_ge(s_rs.sem, s_rs.after(n))
                nc.vector.reciprocal(rs[:], rs[:]).then_inc(s_rr.sem, 1)
                v.wait_ge(s_rr.sem, s_rr.after(n))
                nc.vector.tensor_tensor(sc[:], sc[:], rs[:].unsqueeze(2).broadcast_to([P, NP, P]), ALU.mult).then_inc(s_pn.sem, 1)

            def attended(v, n, w):
                v.wait_ge(s_om.sem, s_om.after(n))
                b0 = V["L1_cond_v_b"]
                for t in range(KT):
                    last = nc.vector.tensor_scalar(h_in[:, w, t], ps_f[:, t], bias[:, b0 + t:b0 + t + 1], None, ALU.add)
                last.then_inc(s_o.sem, 1)

            def projected(v, n, w):
                v.wait_ge(s_pm.sem, s_pm.after(n))
                s_ffo.wait(v, n, -2)
                b0 = V["L1_cond_proj_b"]
                for t in range(KT):
                    last = nc.vector.scalar_tensor_tensor(x1[:, w, t], ps_f[:, t], bias[:, b0 + t:b0 + t + 1], x_all[:, n, t], ALU.add, ALU.add)
                last.then_inc(s_x1.sem, 1)

            def back(n, u):
                v.wait_ge(ff.down.sem, ff.down.after(n))
                b0 = V["L1_cond_mlp_b2"]
                for t in range(KT):
                    last = nc.vector.scalar_tensor_tensor(x_all[:, n, t], ps_o[:, t], bias[:, b0 + t:b0 + t + 1], x1[:, u, t], ALU.add, ALU.add)
                last.then_inc(s_ffo.sem, 1)

            def in_low(v, n, w):
                v.wait_ge(g_high.sem, g_high.after(n))
                nc.vector.tensor_tensor(h_low[:, w], h_in[:, w], h_high[:], ALU.subtract).then_inc(g_low.sem, 1)

            steps = {"in_low": in_low, "q": queries, "softmax_a": softmax_a, "softmax_b": softmax_b, "attend": attended, "proj": projected, "m_low": split.vector_low,
                     **n1.steps("dve", "norm1"), **n2.steps("dve", "norm2")}
            three_stage(v, "dve", L1_TABLE, steps, lambda n, u, g: None, 2 * HJ, back)
    sg.close_layer(NG)


def layer2(nc, mem, sg, T, K):
    x_all = K["x"]
    V, bias = K["vec_at"], K["bias"]
    NGT, H, L, DIRS = 20, 16, 11, 2
    DH = D // H
    HT = H // KT
    CH = 4
    R = CH * NGT
    NC = H // CH
    KC = HT * NGT
    NEG = 9000000000000000.0
    with ExitStack() as ctx:
        m = Mem(nc, ctx)
        psum = lambda name, n: ctx.enter_context(nc.psum_tensor(name, [P, n, GT], F32))
        sf = m.sb("l2_self", [P, 2, KT, GT])
        sfk = m.sb("l2_self_plain", [P, KT, GT])
        q = m.sb("l2_queries", [P, 2, DIRS * KT, GT])
        kt = m.sb("l2_k", [P, 2, DIRS * KT, GB * NGT])
        vt = m.sb("l2_v", [P, 2, DIRS * KT, GB * NGT])
        key_blocks = m.sb("l2_key_blocks", [P, 2, 2, DIRS * KT, KC])
        value_cols = m.sb("l2_value_columns", [P, 2, DIRS * KT, KC])
        value_blocks = m.sb("l2_value_blocks", [P, 4, NC, CH * DH])
        sc = m.sb("l2_scores", [P, 2, DIRS, H * NGT])
        pt = m.sb("l2_probs_t", [P, DIRS, NC, P])
        adj_i = m.sb("l2_adj", [P, NP * DIRS * NGT * L], I32)
        adj = adj_i[:].bitcast(F32)
        keep = m.sb("l2_keep", [P, 2, NP, DIRS * NGT])
        lbias = m.sb("l2_label_bias", [P, 2, NP, DIRS * NGT])
        nz = m.sb("l2_nonzero", [P, GT])
        mx = m.sb("l2_max", [P, 2, DIRS * H])
        rs = m.sb("l2_sums", [P, 2, DIRS * H])
        ot = m.sb("l2_out", [P, KT, P])
        adj_neg = m.sb("l2_neg", [P, NP * DIRS * NGT])
        kb = m.sb("l2_scaled_key_bias", [P, DIRS * KT])
        ob = m.sb("l2_out_bias", [P, KT])
        ps_s, ps_r, ps_o, ps_f = psum("l2_pss", 2), psum("l2_psr", 3), psum("l2_pso", 1), psum("l2_psf", 2)

        g_bias = sg.get("l2_biases")
        g_adj_in, g_adj_f = sg.get("adj_loaded", 16), sg.get("adj_converted")
        g_cnt, g_keep, g_neg = sg.get("adj_counted"), sg.get("keep_ready"), sg.get("neg_ready")
        g_lab, g_labs, g_lbias = sg.get("adj_weighted"), sg.get("adj_labels_summed"), sg.get("label_bias_ready")
        g_negs = sg.get("neg_made")
        g_xs, g_rm, g_nz, g_tq = sg.get("row_summed"), sg.get("row_sum_products"), sg.get("row_nonzero"), sg.get("cond_part_ready")
        g_sm, g_sf, g_sfb = sg.get("self_products"), sg.get("self_ready"), sg.get("self_biased")
        g_fm, g_fe = sg.get("front_products", 8), sg.get("front_evacuated", 8)
        g_kb, g_vc = sg.get("key_blocks_ready", NP), sg.get("value_columns_ready", NP)
        g_s, g_a0, g_a1, g_mx = (sg.get(x, NP) for x in ("score_products", "scores_masked", "scores_biased", "scores_max"))
        g_sub, g_exp, g_rs, g_rr, g_pn = (sg.get(x, NP) for x in ("scores_minus_max", "probs_exp", "probs_summed", "probs_inverted", "probs_ready"))
        g_t, g_pt = sg.get("probs_transposed", 2 * NP), sg.get("probs_t_ready", 2 * NP)
        g_v, g_vb = sg.get("values_transposed", 4 * NP), sg.get("value_blocks_ready", 4 * NP)
        g_o, g_or, g_x = sg.get("attn_products", NP), sg.get("attn_ready", NP), sg.get("x_updated", NP)

        w_at = lambda name, d, k: K[name][:, d * KT + k]
        block = ctx.enter_context(nc.Block())

        @block.sync
        def _(sp):
            def load_adj(n):
                g_adj_in.wait(sp, n, -1)
                g_labs.wait(sp, n, -1)
                sp.dma_start(adj_i[:], T["adj"][n]).then_inc(g_adj_in.sem, 16)

            load_adj(0)
            for dst, src in K["weights_l3"]:
                sp.dma_start(dst, src).then_inc(K["w_loaded"], 16)
            for n in range(1, NG):
                load_adj(n)
            sp.wait_ge(K["w_loaded"], 16 * (len(K["weights_first"] + K["weights_l2"] + K["weights_l3"]) + 2))

        FRONT = ([("k", d, None) for d in range(DIRS)] + [("q", d, t) for d in range(DIRS) for t in range(KT)]
                 + [("v", d, None) for d in range(DIRS)])
        SLOTS = [["row"], ["self", 0, 1], [2, 3, 4], [5, 6, 7]]

        def front(step_of, n):
            for slot in SLOTS:
                for step in slot:
                    step_of(n, 0, step)

        def lagged(n, s, lag, u):
            if s >= lag:
                return (n, s - lag, u) if not isinstance(n, int) or n < NG else None
            return (n - 1, s - lag + NP, 1 - u) if not isinstance(n, int) or n > 0 else None

        def in_slots(engine, first, slots):
            first(0)
            slots(0, 1, 0)
            with engine.Fori(1, NG - 2, 2) as i:
                slots(i, i + 1, 1)
                slots(i + 1, i + 2, 0)
            slots(NG - 1, None, 1)
            slots(NG, None, 0)

        def first_tokens(a):
            return a.rearrange("p (b s) -> p b s", s=S)[:, :, 0:NGT]

        @block.tensor
        def _(pe):
            def front_step(n, w, step):
                if step == "row":
                    pe.wait_ge(g_xs.sem, g_xs.after(n))
                    g_fe.wait(pe, n, -1)
                    nc.tensor.matmul(ps_f[:, 0], K["ones"][:], nz[:], start=True, stop=True).then_inc(g_rm.sem, 1)
                elif step == "self":
                    pe.wait_ge(g_nz.sem, g_nz.after(n))
                    for t in range(KT):
                        for k in range(KT):
                            last = nc.tensor.matmul(ps_f[:, t], K["l2_ws"][:, k, t * P:(t + 1) * P], x_all[:, n, k], start=(k == 0), stop=(k == KT - 1))
                    last.then_inc(g_sm.sem, 1)
                else:
                    kind, d, t = FRONT[step]
                    pe.wait_ge(g_sf.sem, g_sf.after(n))
                    if step >= 2:
                        g_fe.wait(pe, n, step - 2)
                    ps = ps_f[:, step % 2]
                    if kind == "q":
                        for k in range(KT):
                            last = nc.tensor.matmul(ps, w_at("l2_wq", d, k)[:, t * P:(t + 1) * P], sfk[:, k], start=(k == 0), stop=(k == KT - 1))
                    else:
                        for t in range(KT):
                            dst = ps[:, t * GB * NGT:(t + 1) * GB * NGT]
                            for k in range(KT):
                                last = nc.tensor.matmul(dst, w_at("l2_w" + kind, d, k)[:, t * P:(t + 1) * P], first_tokens(sfk[:, k]), start=(k == 0), stop=(k == KT - 1))
                    last.then_inc(g_fm.sem, 1)

            def scores(n, u, p):
                pe.wait_ge(g_kb.sem, g_kb.after(n, p))
                pe.wait_ge(g_fe.sem, g_fe.after(n, 5))
                g_a0.wait(pe, n, p - 1)
                for d in range(DIRS):
                    for b in range(2):
                        for t in range(KT):
                            tok = (2 * p + b) * S
                            last = nc.tensor.matmul(ps_s[b * S:(b + 1) * S, d, t * KC:(t + 1) * KC], q[:, u, d * KT + t, tok:tok + S],
                                                    key_blocks[:, p % 2, b, d * KT + t], start=True, stop=True)
                last.then_inc(g_s.sem, 1)

            def probs_t(n, p):
                pe.wait_ge(g_pn.sem, g_pn.after(n, p))
                for d in range(DIRS):
                    g_vb.wait(pe, n, 4 * (p - 1) + 1 + d)
                    for i in range(NC):
                        last = nc.tensor.transpose(ps_r[0:R, d, i * P:(i + 1) * P], sc[:, p % 2, d, i * R:(i + 1) * R], K["ident"])
                    last.then_inc(g_t.sem, 1)

            def values_t(n, p, i):
                b, d = i // 2, i % 2
                if i == 0:
                    pe.wait_ge(g_vc.sem, g_vc.after(n, p))
                    g_vb.wait(pe, n, 4 * (p - 1) + 3)
                elif i == 3:
                    pe.wait_ge(g_vb.sem, g_vb.after(n, 4 * p))
                else:
                    g_pt.wait(pe, n, 2 * p + i - 1)
                for c in range(NC):
                    a = value_cols[:, b, d * KT + c // 2, (c % 2) * R:(c % 2 + 1) * R]
                    last = nc.tensor.transpose(ps_r[0:R, (i + 2) % 3, c * P:(c + 1) * P], a, K["ident"])
                last.then_inc(g_v.sem, 1)

            def attend(n, p):
                pe.wait_ge(g_vb.sem, g_vb.after(n, 4 * p + 3))
                pe.wait_ge(g_pt.sem, g_pt.after(n, 2 * p + 1))
                g_or.wait(pe, n, p - 1)
                for b in range(2):
                    for c in range(NC):
                        for d in range(DIRS):
                            half = (c % 2) * CH * DH
                            last = nc.tensor.matmul(ps_o[half:half + CH * DH, 0, c // 2 * P + b * S:c // 2 * P + (b + 1) * S], value_blocks[0:R, 2 * b + d, c],
                                                    pt[0:R, d, c, b * S:(b + 1) * S], start=(d == 0), stop=(d == DIRS - 1))
                last.then_inc(g_o.sem, 1)

            def slots(n, f, u):
                for s in range(NP):
                    attending, scored = lagged(n, s, 2, u), lagged(n, s, 0, u)
                    beside = SLOTS[s] if f is not None else []
                    if attending:
                        ga, pa, _ = attending
                        probs_t(ga, pa)
                    if "self" in beside:
                        front_step(f, 1 - u, "self")
                    if scored:
                        scores(n, u, s)
                    if attending:
                        for i in range(4):
                            values_t(ga, pa, i)
                    for step in beside:
                        if step != "self":
                            front_step(f, 1 - u, step)
                    if attending:
                        attend(ga, pa)

            in_slots(pe, lambda n: front(front_step, n), slots)

        @block.scalar
        def _(act):
            def front_step(n, w, step):
                if step == "row":
                    act.wait_ge(g_adj_in.sem, g_adj_in.after(n))
                    nc.scalar.copy(adj, adj_i[:]).then_inc(g_adj_f.sem, 1)
                elif step != "self":
                    kind, d, t = FRONT[step]
                    act.wait_ge(g_fm.sem, g_fm.after(n, step))
                    ps = ps_f[:, step % 2]
                    if kind == "q":
                        if (d, t) == (0, 0):
                            g_s.wait(act, n, -NP - 1)
                        b0 = V["L2_cond_bq"] + d * KT + t
                        last = nc.scalar.activation(q[:, w, d * KT + t], ps, ACT.Identity, bias=bias[:, b0:b0 + 1])
                    elif kind == "k":
                        if d == 0:
                            g_kb.wait(act, n, -NP - 1)
                        for t in range(KT):
                            j = d * KT + t
                            last = nc.scalar.activation(kt[:, w, j], ps[:, t * GB * NGT:(t + 1) * GB * NGT], ACT.Identity,
                                                        bias=kb[:, j:j + 1], scale=1.0 / np.sqrt(DH))
                    else:
                        if d == 0:
                            g_vc.wait(act, n, -NP - 1)
                        last = nc.scalar.copy(vt[:, w, d * KT:(d + 1) * KT].rearrange("p a n -> p (a n)"), ps[:, 0:KT * GB * NGT])
                    last.then_inc(g_fe.sem, 1)

            def probs_t(n, p):
                g_o.wait(act, n, p - 1)
                for d in range(DIRS):
                    act.wait_ge(g_t.sem, g_t.after(n, 2 * p + d))
                    nc.scalar.copy(pt[0:R, d].rearrange("p a n -> p (a n)"), ps_r[0:R, d]).then_inc(g_pt.sem, 1)

            def value_rows(n, p):
                for i in range(4):
                    act.wait_ge(g_v.sem, g_v.after(n, 4 * p + i))
                    a = ps_r[0:R, (i + 2) % 3].rearrange("p (t a n) -> p t a n", t=KT, a=4)[:, :, 0:4:3]
                    nc.scalar.copy(value_blocks[0:R, i].rearrange("p (t c) n -> p t c n", t=KT), a).then_inc(g_vb.sem, 1)

            def exps(n, p):
                act.wait_ge(g_sub.sem, g_sub.after(n, p))
                nc.scalar.activation(sc[:, p % 2], sc[:, p % 2], ACT.Exp).then_inc(g_exp.sem, 1)

            def slots(n, f, u):
                for s in range(NP):
                    attending, scored = lagged(n, s, 2, u), lagged(n, s, 0, u)
                    if attending:
                        ga, pa, _ = attending
                        probs_t(ga, pa)
                        value_rows(ga, pa)
                    if f is not None:
                        for step in SLOTS[s]:
                            front_step(f, 1 - u, step)
                    if scored:
                        exps(n, s)

            g_bias.wait(act, 0)
            in_slots(act, lambda n: front(front_step, n), slots)

        @block.gpsimd
        def _(pool):
            def front_step(n, step):
                if step == "row":
                    pool.wait_ge(g_adj_f.sem, g_adj_f.after(n))
                    pool.wait_ge(g_cnt.sem, g_cnt.after(n))
                    a = adj.rearrange("p (a l) -> p a l", l=L)
                    w = K["label_w"].unsqueeze(1).broadcast_to([P, NP * DIRS * NGT, L])
                    nc.gpsimd.tensor_tensor(a, a, w, ALU.mult).then_inc(g_lab.sem, 1)

            def blocks(n, p, u):
                pool.wait_ge(g_fe.sem, g_fe.after(n, 1))
                g_s.wait(pool, n, p - 2)
                mask = K["head_mask"].unsqueeze(1).unsqueeze(3).broadcast_to([P, DIRS * KT, HT, NGT])
                for b in range(2):
                    at = (2 * p + b) * NGT
                    a = kt[:, u, :, at:at + NGT].unsqueeze(2).broadcast_to([P, DIRS * KT, HT, NGT])
                    last = nc.gpsimd.tensor_tensor(key_blocks[:, p % 2, b].rearrange("p j (h m) -> p j h m", m=NGT), a, mask, ALU.mult)
                last.then_inc(g_kb.sem, 1)

            def value_columns(n, p, u):
                pool.wait_ge(g_fe.sem, g_fe.after(n, 7))
                g_v.wait(pool, n, 4 * (p - 1) + 3)
                mask = K["head_mask"].unsqueeze(1).unsqueeze(3).broadcast_to([P, DIRS * KT, HT, NGT])
                for b in range(2):
                    at = (2 * p + b) * NGT
                    a = vt[:, u, :, at:at + NGT].unsqueeze(2).broadcast_to([P, DIRS * KT, HT, NGT])
                    last = nc.gpsimd.tensor_tensor(value_cols[:, b].rearrange("p j (h m) -> p j h m", m=NGT), a, mask, ALU.mult)
                last.then_inc(g_vc.sem, 1)

            def normalise(n, p):
                pool.wait_ge(g_rr.sem, g_rr.after(n, p))
                r = rs[:, p % 2].unsqueeze(2).broadcast_to([P, DIRS * H, NGT])
                a = sc[:, p % 2].rearrange("p d (h m) -> p (d h) m", m=NGT)
                nc.gpsimd.tensor_tensor(a, a, r, ALU.mult).then_inc(g_pn.sem, 1)

            def slots(n, f, u):
                for s in range(NP):
                    before = lagged(n, s, 1, u)
                    if before:
                        normalise(*before[:2])
                    if s + 1 < NP and lagged(n, s, 0, u):
                        blocks(n, s + 1, u)
                    elif s + 1 == NP and f is not None:
                        blocks(f, 0, 1 - u)
                    if before:
                        value_columns(*before)
                    if f is not None and s == 2:
                        front_step(f, "row")

            def first(n):
                front_step(n, "row")
                blocks(n, 0, 0)

            in_slots(pool, first, slots)

        @block.vector
        def _(v):
            b0 = V["L2_cond_bk"]
            nc.vector.tensor_scalar(kb[:], bias[:, b0:b0 + DIRS * KT], 1.0 / np.sqrt(DH), None, ALU.mult)
            b0 = V["L2_cond_bout"]
            nc.vector.tensor_tensor(ob[:], bias[:, b0:b0 + KT], bias[:, b0 + KT:b0 + 2 * KT], ALU.add).then_inc(g_bias.sem, 1)
            g_bias.wait(v, 0)

            def front_step(n, w, step):
                a = adj.rearrange("p (a l) -> p a l", l=L)
                k, lb = (t[:, w].rearrange("p a n -> p (a n)") for t in (keep, lbias))
                if step == "row_sum":
                    g_tq.wait(v, n, -1)
                    nc.vector.tensor_tensor(nz[:], x_all[:, n, 0], x_all[:, n, 1], ALU.add).then_inc(g_xs.sem, 1)
                elif step == "row":
                    v.wait_ge(g_rm.sem, g_rm.after(n))
                    nc.vector.tensor_scalar(nz[:], ps_f[:, 0], 0.0, None, ALU.not_equal).then_inc(g_nz.sem, 1)
                    v.wait_ge(g_nz.sem, g_nz.after(n))
                    g_fm.wait(v, n, -1)
                    g_sfb.wait(v, n, -1)
                    nzb = nz[:].rearrange("p (b s) -> p b s", s=S).unsqueeze(1).broadcast_to([P, KT, GB, S])
                    nc.vector.tensor_tensor(tokens(sfk[:]), nzb, per_batch(K["l2_q"], bass.ds(n * GB, GB)), ALU.mult).then_inc(g_tq.sem, 1)
                elif step == "self":
                    v.wait_ge(g_sm.sem, g_sm.after(n))
                    v.wait_ge(g_tq.sem, g_tq.after(n))
                    b0 = V["L2_cond_b_self"]
                    for t in range(KT):
                        last = nc.vector.scalar_tensor_tensor(sfk[:, t], ps_f[:, t], bias[:, b0 + t:b0 + t + 1], sfk[:, t], ALU.add, ALU.add)
                    last.then_inc(g_sf.sem, 1)
                elif step == "keep":
                    v.wait_ge(g_adj_f.sem, g_adj_f.after(n))
                    nc.vector.reduce_sum(k, a, AX.X).then_inc(g_cnt.sem, 1)
                    v.wait_ge(g_cnt.sem, g_cnt.after(n))
                    nc.vector.tensor_scalar(k, k, 0.0, None, ALU.is_gt).then_inc(g_keep.sem, 1)
                elif step == "labels":
                    v.wait_ge(g_lab.sem, g_lab.after(n))
                    nc.vector.reduce_sum(lb, a, AX.X).then_inc(g_labs.sem, 1)
                    v.wait_ge(g_labs.sem, g_labs.after(n))
                    nc.vector.tensor_scalar(lb, lb, K["label_b"], None, ALU.add).then_inc(g_neg.sem, 1)
                    v.wait_ge(g_neg.sem, g_neg.after(n))
                    nc.vector.tensor_scalar(adj_neg[:], k, 1.0, NEG, ALU.subtract, ALU.mult).then_inc(g_negs.sem, 1)
                    v.wait_ge(g_negs.sem, g_negs.after(n))
                    nc.vector.tensor_tensor(lb, lb, adj_neg[:], ALU.add).then_inc(g_lbias.sem, 1)
                elif step == "biased":
                    v.wait_ge(g_sf.sem, g_sf.after(n))
                    for t in range(KT):
                        last = nc.vector.tensor_scalar(sf[:, w, t], sfk[:, t], ob[:, t:t + 1], None, ALU.add)
                    last.then_inc(g_sfb.sem, 1)

            def softmax_a(n, u, p):
                v.wait_ge(g_s.sem, g_s.after(n, p))
                g_t.wait(v, n, 2 * (p - 2) + 1)
                a = sc[:, p % 2].rearrange("p d (h m) -> p d h m", m=NGT)
                ps = ps_s[:, :, 0:H * NGT].rearrange("p d (h m) -> p d h m", m=NGT)
                spread = lambda t: t[:, u, p].rearrange("p (d m) -> p d m", m=NGT).unsqueeze(2).broadcast_to([P, DIRS, H, NGT])
                nc.vector.tensor_tensor(a, ps, spread(keep), ALU.mult).then_inc(g_a0.sem, 1)
                v.wait_ge(g_a0.sem, g_a0.after(n, p))
                nc.vector.tensor_tensor(a, a, spread(lbias), ALU.add).then_inc(g_a1.sem, 1)
                v.wait_ge(g_a1.sem, g_a1.after(n, p))
                flat = sc[:, p % 2].rearrange("p d (h m) -> p (d h) m", m=NGT)
                nc.vector.reduce_max(mx[:, p % 2], flat, AX.X).then_inc(g_mx.sem, 1)
                v.wait_ge(g_mx.sem, g_mx.after(n, p))
                nc.vector.tensor_tensor(flat, flat, mx[:, p % 2].unsqueeze(2).broadcast_to([P, DIRS * H, NGT]), ALU.subtract).then_inc(g_sub.sem, 1)

            def softmax_b(n, p):
                v.wait_ge(g_exp.sem, g_exp.after(n, p))
                flat = sc[:, p % 2].rearrange("p d (h m) -> p (d h) m", m=NGT)
                nc.vector.reduce_sum(rs[:, p % 2], flat, AX.X).then_inc(g_rs.sem, 1)
                v.wait_ge(g_rs.sem, g_rs.after(n, p))
                nc.vector.reciprocal(rs[:, p % 2], rs[:, p % 2]).then_inc(g_rr.sem, 1)

            def outputs(n, u, p):
                v.wait_ge(g_o.sem, g_o.after(n, p))
                c = slice(p * P, (p + 1) * P)
                g_x.wait(v, n, p - 1)
                nc.vector.tensor_tensor(ot[:], ps_o[:, 0, 0:KT * P].rearrange("p (t n) -> p t n", n=P), sf[:, u, :, c], ALU.add).then_inc(g_or.sem, 1)
                v.wait_ge(g_or.sem, g_or.after(n, p))
                nc.vector.scalar_tensor_tensor(x_all[:, n, :, c], ot[:], 0.0, x_all[:, n, :, c], ALU.max, ALU.add).then_inc(g_x.sem, 1)

            BEFORE = [["row_sum"], ["self"], [], []]
            AFTER = [["row"], ["keep"], [], ["biased", "labels"]]

            def slots(n, f, u):
                for s in range(NP):
                    outgoing, before = lagged(n, s, 3, u), lagged(n, s, 1, u)
                    if outgoing:
                        outputs(outgoing[0], outgoing[2], outgoing[1])
                    if before:
                        softmax_b(*before[:2])
                    if f is not None:
                        for step in BEFORE[s]:
                            front_step(f, 1 - u, step)
                    if lagged(n, s, 0, u):
                        softmax_a(n, u, s)
                    if f is not None:
                        for step in AFTER[s]:
                            front_step(f, 1 - u, step)

            def first(n):
                for before, after in zip(BEFORE, AFTER):
                    for step in before + after:
                        front_step(n, 0, step)

            in_slots(v, first, slots)
            g_x.wait(v, NG - 1)
    sg.close_layer(NG)



L3_TABLE = [
    ("perm0", dict(pe=1, pool=1, dve=1)), ("qk2", dict(pe=1, act=1)),
    ("perm1", dict(pe=2, pool=2, dve=2)), ("qk3", dict(pe=2, act=2)), ("perm2", dict(pe=3, pool=3, dve=3)), ("perm3", dict(pe=4, pool=4, dve=4)),
    ("v", dict(pe=4, dve=5)), ("kb0", dict(pool=5, dve=4)), ("s0", dict(pe=6, dve=6)), ("kb1", dict(pool=6)),
    ("s1", dict(pe=8, dve=8)), ("exp0", dict(act=7)), ("sum0", dict(dve=8)), ("kb2", dict(pool=8)),
    ("t0", dict(pe=9, act=9)), ("exp1", dict(act=9)), ("pv0", dict(pe=10, dve=10)),
    ("ot0", dict(pe=11, act=11)), ("sum1", dict(dve=10)), ("s2", dict(pe=11, dve=11)), ("kb3", dict(pool=11)),
    ("t1", dict(pe=12, act=12)), ("exp2", dict(act=12)), ("pv1", dict(pe=13, dve=13)), ("ot1", dict(pe=14, act=14)), ("sum2", dict(dve=13)),
    ("s3", dict(pe=14, dve=14)), ("norm1.square", dict(act=13)), ("norm1.sum", dict(pool=13)),
    ("t2", dict(pe=15, act=15)), ("exp3", dict(act=15)), ("norm1.variance", dict(pe=15)), ("norm1.guard", dict(dve=15)), ("norm1.invert", dict(pool=15)),
    ("pv2", dict(pe=16, dve=16)), ("norm1.diagonal", dict(dve=16)), ("sum3", dict(dve=16)),
    ("ot2", dict(pe=17, act=17)), ("norm1.spread", dict(pe=17)), ("t3", dict(pe=17, act=17)),
    ("pv3", dict(pe=18, dve=18)), ("norm1.apply", dict(dve=18)), ("ot3", dict(pe=19, act=19)), ("proj", dict(pe=20, dve=20)),
    ("norm2.square", dict(act=20)), ("norm2.sum", dict(pool=20)), ("norm2.variance", dict(pe=23)), ("norm2.guard", dict(dve=22)),
    ("norm2.invert", dict(pool=22)), ("norm2.diagonal", dict(dve=22)), ("qk0", dict(pe=23, act=23, ahead=2)), ("norm2.spread", dict(pe=23)),
    ("norm2.apply", dict(dve=23)), ("qk1", dict(pe=23, act=23, ahead=2)),
]


def layer3(nc, mem, sg, T, K):
    x_all = K["x"]
    V, bias = K["vec_at"], K["bias"]
    H = 16
    DH = D // H
    HT = H // KT
    HP = H // 2
    with ExitStack() as ctx:
        m = Mem(nc, ctx)
        psum = lambda name, n: ctx.enter_context(nc.psum_tensor(name, [P, n, GT], F32))
        x1 = m.sb("l3_x1", [P, 2, KT, GT])
        min_ = m.sb("l3_m", [P, 2, KT, GT])
        h_in = m.sb("l3_in", [P, 2, KT, GT])
        norm_bufs = [(m.sb(f"l3_sum{i}", [P, GT]), m.sb(f"l3_sq{i}", [P, KT, GT]), m.sb(f"l3_inv{i}", [P, Norm.CHUNKS])) for i in range(2)]
        raw = m.sb("l3_raw", [P, 2, GT])
        rc = m.sb("l3_cosine_part", [P, 2, GT])
        rsn = m.sb("l3_sine_part", [P, 2, GT])
        qk = m.sb("l3_qk", [P, 2 * KT, GT])
        vb = m.sb("l3_value_blocks", [P, 2, NP, D])
        key_blocks = K["arena_rest"].rearrange("p (u b k n) -> p u b k n", u=2, b=2, k=KT)
        sc = m.sb("l3_scores", [P, 2, H, S])
        pt = m.sb("l3_probs_t", [P, HP, P])
        on = m.sb("l3_attn", [P, 2, D])
        mx = m.sb("l3_max", [P, 2, H])
        rs = m.sb("l3_sums", [P, 2, H])
        sig = m.sb("l3_silu", [P, GT])
        hidden = m.sb("l3_h", [P, 2, GT])
        ps_ag, ps_o, ps_x, ps_y = psum("l3_psag", 2), psum("l3_pso", 2), psum("l3_psx", 2), psum("l3_psy", 2)

        s_x1, s_ffo = sg.get("x1_ready"), sg.get("ff_out_read")
        g_vz = sg.get("value_blocks_cleared")
        g_qk, g_raw = sg.get("q_products", 4), sg.get("q_ready", 4)
        g_perm, g_rs, g_rc, g_rope = (sg.get(x, 4) for x in ("qk_swapped", "qk_sine_part", "qk_cosine_part", "qk_rotated"))
        g_vm, g_vb = sg.get("v_products"), sg.get("v_ready")
        g_kbv = sg.get("key_blocks_halved")
        g_kb, g_s, g_mx, g_sub, g_exp = (sg.get(x, NP) for x in ("key_blocks_ready", "score_products", "scores_max", "scores_minus_max", "probs_exp"))
        g_sum, g_rr, g_t, g_pt = (sg.get(x, NP) for x in ("probs_summed", "probs_inverted", "probs_transposed", "probs_t_ready"))
        g_pv, g_on, g_ot, g_o = (sg.get(x, NP) for x in ("attn_products", "attn_normalised", "attn_transposed", "attn_ready"))
        g_pm = sg.get("proj_products")
        f_a, f_g, f_sig, f_h, f_down = (sg.get(x, HJ) for x in ("ff_a_products", "ff_gate_products", "ff_activated", "ff_hidden_ready", "ff_down"))

        def no_wait(e, n):
            pass

        def x1_ready(e, n):
            s_x1.wait(e, n)

        n1 = Norm(nc, sg, K, "norm1", lambda n, w: x_all[:, n], no_wait, lambda w: h_in[:, w], False, float(np.finfo(np.float32).eps),
                  K["l3a_scale"], K["l3a_shift"], ps_x[:, 0], norm_bufs[0])
        n2 = Norm(nc, sg, K, "norm2", lambda n, w: x1[:, w], x1_ready, lambda w: min_[:, w], False, float(np.finfo(np.float32).eps),
                  K["l3b_scale"], K["l3b_shift"], ps_y[:, 1], norm_bufs[1])
        block = ctx.enter_context(nc.Block())

        def by_name(front_step, who, norms):
            def step_of(name):
                return lambda engine, n, w: front_step(n, w, name)
            names = [name for name, at in L3_TABLE if who in at and not name.startswith("norm")]
            return {**{name: step_of(name) for name in names}, **norms}

        @block.sync
        def _(sp):
            for n in range(NG):
                sp.wait_ge(s_ffo.sem, s_ffo.after(n))
                sp.dma_start(T["out"][:, n], x_all[:, n]).then_inc(K["x_stored"], 16)
            sp.wait_ge(K["x_stored"], 16 * NG)

        @block.tensor
        def _(pe):
            w_qkv, w_fc, w_fo = K["l3_qkv"], K["l3_fc"], K["l3_fo"]

            def front_step(n, w, step):
                kind, p = step[:-1], int(step[-1]) if step[-1].isdigit() else None
                if kind == "qk":
                    pe.wait_ge(n1.done.sem, n1.done.after(n))
                    if p == 0:
                        s_x1.wait(pe, n, -1)
                    elif p >= 2:
                        pe.wait_ge(g_raw.sem, g_raw.after(n, p - 2))
                    for k in range(KT):
                        last = nc.tensor.matmul(ps_x[:, p % 2], w_qkv[:, k, p * P:(p + 1) * P], h_in[:, w, k], start=(k == 0), stop=(k == KT - 1))
                    last.then_inc(g_qk.sem, 1)
                elif kind == "perm":
                    pe.wait_ge(g_raw.sem, g_raw.after(n, p))
                    if p >= 2:
                        g_rs.wait(pe, n, p - 2)
                    nc.tensor.matmul(ps_y[:, p % 2], K["swap"], raw[:, p % 2], start=True, stop=True).then_inc(g_perm.sem, 1)
                elif step == "v":
                    pe.wait_ge(g_raw.sem, g_raw.after(n, 3))
                    for a in range(NP):
                        dst = ps_x[:, a // 2, (a % 2) * D:(a % 2 + 1) * D]
                        for k in range(KT):
                            last = nc.tensor.matmul(dst, h_in[:, w, k, a * P:(a + 1) * P], w_qkv[:, k, 2 * D:3 * D], start=(k == 0), stop=(k == KT - 1))
                    last.then_inc(g_vm.sem, 1)
                elif kind == "s":
                    pe.wait_ge(g_kb.sem, g_kb.after(n, p))
                    if p == 0:
                        pe.wait_ge(g_kbv.sem, g_kbv.after(n))
                        pe.wait_ge(g_vb.sem, g_vb.after(n))
                    else:
                        g_sub.wait(pe, n, p - 1)
                    for b in range(2):
                        at = (2 * p + b) * S
                        for t in range(KT):
                            last = nc.tensor.matmul(ps_x[b * S:(b + 1) * S, t], qk[:, t, at:at + S], key_blocks[:, p % 2, b, t], start=True, stop=True)
                    last.then_inc(g_s.sem, 1)
                elif kind == "t":
                    pe.wait_ge(g_exp.sem, g_exp.after(n, p))
                    if p == 0:
                        pe.wait_ge(g_rs.sem, g_rs.after(n, 3))
                    else:
                        g_o.wait(pe, n, p - 1)
                    for i in range(HP):
                        last = nc.tensor.transpose(ps_y[:, i // 4, (i % 4) * P:(i % 4 + 1) * P], sc[:, p % 2, 2 * i:2 * i + 2].rearrange("p h m -> p (h m)"), K["ident"])
                    last.then_inc(g_t.sem, 1)
                elif kind == "pv":
                    pe.wait_ge(g_pt.sem, g_pt.after(n, p))
                    for b in range(2):
                        for i in range(HP):
                            c = slice(i * 2 * DH, (i + 1) * 2 * DH)
                            last = nc.tensor.matmul(ps_y[b * S:(b + 1) * S, 0, c], pt[:, i, b * S:(b + 1) * S], vb[:, b, p, c], start=True, stop=True)
                    last.then_inc(g_pv.sem, 1)
                elif kind == "ot":
                    pe.wait_ge(g_on.sem, g_on.after(n, p))
                    for t in range(KT):
                        last = nc.tensor.transpose(ps_y[:, 1, t * P:(t + 1) * P], on[:, p % 2, t * P:(t + 1) * P], K["ident"])
                    last.then_inc(g_ot.sem, 1)
                elif step == "proj":
                    pe.wait_ge(g_o.sem, g_o.after(n))
                    if isinstance(n, int) and n == NG - 1:
                        pe.wait_ge(g_sub.sem, g_sub.after(n))
                    else:
                        n1.normed.wait(pe, n + 1)
                    for t in range(KT):
                        for k in range(KT):
                            last = nc.tensor.matmul(ps_x[:, t], K["l3_ao"][:, k, t * P:(t + 1) * P], h_in[:, w, k], start=(k == 0), stop=(k == KT - 1))
                    last.then_inc(g_pm.sem, 1)

            def down(n, j):
                pe.wait_ge(f_h.sem, f_h.after(n, j))
                if j == 0:
                    s_ffo.wait(pe, n, -1)
                for t in range(KT):
                    last = nc.tensor.matmul(ps_o[:, t], w_fo[:, j, t * P:(t + 1) * P], hidden[:, j % 2], start=(j == 0), stop=(j == HJ - 1))
                last.then_inc(f_down.sem, 1)

            def ff_part(n, u, j, part):
                if part == 2:
                    if j >= 1:
                        down(n, j - 1)
                    return
                if j == 0 and part == 0:
                    pe.wait_ge(n2.done.sem, n2.done.after(n))
                (f_h if part else f_sig).wait(pe, n, j - 1)
                for k in range(KT):
                    c = ((1 - part) * HJ + j) * P
                    last = nc.tensor.matmul(ps_ag[:, part], w_fc[:, k, c:c + P], min_[:, u, k], start=(k == 0), stop=(k == KT - 1))
                last.then_inc((f_a if part else f_g).sem, 1)

            def norm1_variance(engine, n, w):
                g_sub.wait(pe, n, -1)
                n1.tensor_variance(pe, n, w)

            norms = {**n1.steps("pe", "norm1"), **n2.steps("pe", "norm2"), "norm1.variance": norm1_variance}
            three_stage(pe, "pe", L3_TABLE, by_name(front_step, "pe", norms),
                        lambda n, u, g: ff_part(n, u, g // 3, g % 3), 3 * HJ, lambda n, u: down(n, HJ - 1))

        @block.scalar
        def _(act):
            def front_step(n, w, step):
                kind, p = step[:-1], int(step[-1]) if step[-1].isdigit() else None
                if kind == "qk":
                    act.wait_ge(g_qk.sem, g_qk.after(n, p))
                    g_rc.wait(act, n, p - 2)
                    g_perm.wait(act, n, p - 2)
                    b0 = V["L3_cond_b_qkv"] + p
                    nc.scalar.activation(raw[:, p % 2], ps_x[:, p % 2], ACT.Identity, bias=bias[:, b0:b0 + 1]).then_inc(g_raw.sem, 1)
                elif kind == "exp":
                    act.wait_ge(g_sub.sem, g_sub.after(n, p))
                    nc.scalar.activation(sc[:, p % 2], sc[:, p % 2], ACT.Exp, scale=1.0 / np.sqrt(DH)).then_inc(g_exp.sem, 1)
                elif kind == "t":
                    act.wait_ge(g_t.sem, g_t.after(n, p))
                    nc.scalar.copy(pt[:].rearrange("p a n -> p (a n)"), ps_y[:].rearrange("p a n -> p (a n)")).then_inc(g_pt.sem, 1)
                elif kind == "ot":
                    act.wait_ge(g_ot.sem, g_ot.after(n, p))
                    b0 = V["L3_cond_b_qkv"] + 2 * KT
                    for t in range(KT):
                        last = nc.scalar.activation(h_in[:, w, t, p * P:(p + 1) * P], ps_y[:, 1, t * P:(t + 1) * P], ACT.Identity, bias=bias[:, b0 + t:b0 + t + 1])
                    last.then_inc(g_o.sem, 1)

            def ff_part(n, u, j, part):
                if part == 0:
                    act.wait_ge(f_g.sem, f_g.after(n, j))
                    f_h.wait(act, n, j - 1)
                    b0 = V["L3_cond_b_fc"] + HJ + j
                    nc.scalar.activation(sig[:], ps_ag[:, 0], ACT.Silu, bias=bias[:, b0:b0 + 1]).then_inc(f_sig.sem, 1)

            three_stage(act, "act", L3_TABLE, by_name(front_step, "act", {**n1.steps("act", "norm1"), **n2.steps("act", "norm2")}),
                        lambda n, u, g: ff_part(n, u, g // 3, g % 3), 3 * HJ)

        @block.gpsimd
        def _(pool):
            def front_step(n, w, step):
                kind, p = step[:-1], int(step[-1]) if step[-1].isdigit() else None
                if kind == "perm":
                    pool.wait_ge(g_raw.sem, g_raw.after(n, p))
                    g_rope.wait(pool, n, p - 2)
                    cos = K["rope_cos"].unsqueeze(1).broadcast_to([P, GB, S])
                    b3 = lambda a: a.rearrange("p (b s) -> p b s", s=S)
                    nc.gpsimd.tensor_tensor(b3(rc[:, p % 2]), b3(raw[:, p % 2]), cos, ALU.mult).then_inc(g_rc.sem, 1)
                elif kind == "kb":
                    pool.wait_ge(g_rope.sem, g_rope.after(n))
                    g_s.wait(pool, n, p - 2)
                    batches = (1,) if p == 0 else (0, 1)
                    mask = K["head_mask"].unsqueeze(2).broadcast_to([P, HT, S])
                    for b in batches:
                        at = (2 * p + b) * S
                        for t in range(KT):
                            a = qk[:, KT + t, at:at + S].unsqueeze(1).broadcast_to([P, HT, S])
                            last = nc.gpsimd.tensor_tensor(key_blocks[:, p % 2, b, t].rearrange("p (h s) -> p h s", s=S), a, mask, ALU.mult)
                    last.then_inc(g_kb.sem, 1)

            three_stage(pool, "pool", L3_TABLE, by_name(front_step, "pool", {**n1.steps("pool", "norm1"), **n2.steps("pool", "norm2")}),
                        lambda n, u, g: None, 3 * HJ)

        @block.vector
        def _(v):
            nc.vector.memset(vb[:], 0.0).then_inc(g_vz.sem, 1)
            g_vz.wait(v, 0)

            def sums(n, p):
                v.wait_ge(g_exp.sem, g_exp.after(n, p))
                nc.vector.reduce_sum(rs[:, p % 2], sc[:, p % 2], AX.X).then_inc(g_sum.sem, 1)
                v.wait_ge(g_sum.sem, g_sum.after(n, p))
                nc.vector.reciprocal(rs[:, p % 2], rs[:, p % 2]).then_inc(g_rr.sem, 1)

            def front_step(n, w, step):
                kind, p = step[:-1], int(step[-1]) if step[-1].isdigit() else None
                if kind == "kb":
                    v.wait_ge(g_rope.sem, g_rope.after(n))
                    g_s.wait(v, n, -2)
                    mask = K["head_mask"].unsqueeze(2).broadcast_to([P, HT, S])
                    for t in range(KT):
                        a = qk[:, KT + t, 0:S].unsqueeze(1).broadcast_to([P, HT, S])
                        last = nc.vector.tensor_tensor(key_blocks[:, 0, 0, t].rearrange("p (h s) -> p h s", s=S), a, mask, ALU.mult)
                    last.then_inc(g_kbv.sem, 1)
                elif kind == "perm":
                    v.wait_ge(g_perm.sem, g_perm.after(n, p))
                    g_rope.wait(v, n, p - 2)
                    sin = K["rope_sin"].unsqueeze(1).broadcast_to([P, GB, S])
                    b3 = lambda a: a.rearrange("p (b s) -> p b s", s=S)
                    nc.vector.tensor_tensor(b3(rsn[:, p % 2]), b3(ps_y[:, p % 2]), sin, ALU.mult).then_inc(g_rs.sem, 1)
                    v.wait_ge(g_rs.sem, g_rs.after(n, p))
                    v.wait_ge(g_rc.sem, g_rc.after(n, p))
                    nc.vector.tensor_tensor(qk[:, p], rc[:, p % 2], rsn[:, p % 2], ALU.add).then_inc(g_rope.sem, 1)
                elif step == "v":
                    v.wait_ge(g_vm.sem, g_vm.after(n))
                    src = ps_x[:].rearrange("p k (a h e d) -> p (k a) h e d", a=2, e=2, d=DH)
                    dst = vb[:].rearrange("p b a (h e d) -> p b a h e d", e=2, d=DH)
                    for b in range(2):
                        for e in range(2):
                            last = nc.vector.tensor_copy(dst[e * S:(e + 1) * S, b, :, :, e], src[b * S:(b + 1) * S, :, :, e])
                    last.then_inc(g_vb.sem, 1)
                elif kind == "s":
                    v.wait_ge(g_s.sem, g_s.after(n, p))
                    ps = ps_x[:].rearrange("p t (h s) -> p (t h) s", s=S)
                    nc.vector.reduce_max(mx[:, p % 2], ps, AX.X).then_inc(g_mx.sem, 1)
                    v.wait_ge(g_mx.sem, g_mx.after(n, p))
                    nc.vector.tensor_tensor(sc[:, p % 2], ps, mx[:, p % 2].unsqueeze(2).broadcast_to([P, H, S]), ALU.subtract).then_inc(g_sub.sem, 1)
                elif kind == "sum":
                    sums(n, p)
                elif kind == "pv":
                    v.wait_ge(g_pv.sem, g_pv.after(n, p))
                    v.wait_ge(g_rr.sem, g_rr.after(n, p))
                    r = rs[:, p % 2].unsqueeze(2).broadcast_to([P, H, DH])
                    nc.vector.tensor_tensor(on[:, p % 2].rearrange("p (h d) -> p h d", d=DH), ps_y[:, 0, 0:D].rearrange("p (h d) -> p h d", d=DH), r,
                                            ALU.mult).then_inc(g_on.sem, 1)
                elif step == "proj":
                    v.wait_ge(g_pm.sem, g_pm.after(n))
                    b0 = V["L3_cond_b_ao"]
                    for t in range(KT):
                        last = nc.vector.scalar_tensor_tensor(x1[:, w, t], ps_x[:, t], bias[:, b0 + t:b0 + t + 1], x_all[:, n, t], ALU.add, ALU.add)
                    last.then_inc(s_x1.sem, 1)

            def ff_part(n, u, j, part):
                if part == 1:
                    v.wait_ge(f_a.sem, f_a.after(n, j))
                    v.wait_ge(f_sig.sem, f_sig.after(n, j))
                    f_down.wait(v, n, j - 2)
                    b0 = V["L3_cond_b_fc"] + j
                    nc.vector.scalar_tensor_tensor(hidden[:, j % 2], ps_ag[:, 1], bias[:, b0:b0 + 1], sig[:], ALU.add, ALU.mult).then_inc(f_h.sem, 1)

            def back_end(n, u):
                v.wait_ge(f_down.sem, f_down.after(n))
                b0 = V["L3_cond_b_fo"]
                for t in range(KT):
                    last = nc.vector.scalar_tensor_tensor(x_all[:, n, t], ps_o[:, t], bias[:, b0 + t:b0 + t + 1], x1[:, u, t], ALU.add, ALU.add)
                last.then_inc(s_ffo.sem, 1)

            three_stage(v, "dve", L3_TABLE, by_name(front_step, "dve", {**n1.steps("dve", "norm1"), **n2.steps("dve", "norm2")}),
                        lambda n, u, g: ff_part(n, u, g // 3, g % 3), 3 * HJ, back_end)
    sg.close_layer(NG)



VECTORS = ["L0_cond_bm", "L0_cond_bc", "L0_cond_D_diag", "L0_cond_b1", "L0_cond_b2",
           "L1_cond_norm1_w", "L1_cond_film1_b", "L1_cond_q_b", "L1_cond_k_b", "L1_cond_v_b", "L1_cond_proj_b",
           "L1_cond_norm2_w", "L1_cond_film2_b", "L1_cond_mlp_b1", "L1_cond_mlp_b2",
           "L2_cond_b_self", "L2_cond_bq", "L2_cond_bk", "L2_cond_bout",
           "L3_cond_g1", "L3_cond_g2", "L3_cond_b_qkv", "L3_cond_b_ao", "L3_cond_b_fc", "L3_cond_b_fo",
           "L3_cond_b_t1", "L3_cond_b_t2"]


def program(nc, T, vec_at):
    ctx = ExitStack()
    with ctx:
        mem = Mem(nc, ctx)
        sg = Signals(mem)
        K = {"vec_at": vec_at}
        K["x"] = mem.sb("x_all", [P, NG, KT, GT])
        K["bias"] = mem.sb("bias_columns", [P, T["vectors"].shape[1]])
        K["consts"] = mem.sb("constants", [P, T["consts"].shape[1]])
        K["sign"] = K["consts"][:, 0:1]
        K["minus_half"] = mem.sb("minus_half", [P, 4])
        K["ones"] = mem.sb("ones", [P, P])
        K["mean"] = mem.sb("mean_weights", [P, P])
        for name in ("l3a_scale", "l3a_shift", "l3b_scale", "l3b_shift"):
            K[name] = mem.sb(name, [P, KT, B])
        K["x_loaded"], K["w_loaded"] = mem.sem("x_loaded"), mem.sem("weights_loaded")
        arena, arena_at = mem.sb_and_place("weights_a", [P, 2 * KT * FF + 2 * HJ * D])
        c2 = KT * FF
        K["l0_w1"] = arena[:, 0:c2].rearrange("p (k n) -> p k n", k=KT)
        K["l0_w2"] = arena[:, c2:c2 + HJ * D].rearrange("p (k n) -> p k n", k=HJ)
        for name, at, tiles in (("l0_w1_low", 0, KT), ("l0_w2_low", c2, HJ), ("l0_w1_high", c2 + HJ * D + 1024, KT),
                                ("l1_w1_high", 0, KT), ("l1_w2_high", c2, HJ)):
            K[name] = mem.rounded_at(name, [P, tiles, c2 // tiles], arena_at + 4 * at)
        K["l1_wv_high"] = mem.rounded_at("l1_wv_high", [P, KT, D], arena_at + 4 * (2 * c2 + 7 * KT * D))
        K["s5_b"] = arena[:, c2 + HJ * D:c2 + HJ * D + 512].rearrange("p (c k n) -> p c k n", c=2, k=KT)
        K["s5_c"] = arena[:, c2 + HJ * D + 512:c2 + HJ * D + 1024].rearrange("p (c n) -> p c n", c=2)
        K["weights_first"] = [
            (K["l0_w1"], T["L0_cond_W1"].rearrange("(k p) n -> p k n", p=P)),
            (K["l0_w2"], T["L0_cond_W2"].rearrange("(k p) n -> p k n", p=P)),
            (K["s5_b"][:], T["s5_b"][:]), (K["s5_c"][:], T["s5_c"][:])]
        def weight(m, name, src, tiles, cols):
            K[name] = m.sb(name, [P, tiles, cols])
            return K[name][:], T[src].rearrange("(k p) n -> p k n", p=P)

        c = K["consts"]
        K["ident"], K["block_mask"] = (c[:, 32 + i * P:32 + (i + 1) * P] for i in range(2))
        K["head_mask"], K["label_w"], K["label_b"] = c[:, 1:9], c[:, 9:20], c[:, 20:21]
        K["swap"] = c[:, 32 + 2 * P:32 + 3 * P]
        K["rope_cos"], K["rope_sin"] = (c[:, 32 + 3 * P + i * S:32 + 3 * P + (i + 1) * S] for i in range(2))
        K["x_stored"] = mem.sem("x_stored")

        def arena_weight(at, name, src, tiles, cols):
            K[name] = arena[:, at:at + tiles * cols].rearrange("p (k n) -> p k n", k=tiles)
            return K[name], T[src].rearrange("(k p) n -> p k n", p=P)

        K["weights_l2"], at = [], 2 * c2
        for name, src, tiles in (("l2_ws", "WselfT_v", KT), ("l2_wq", "l2_WqT", 2 * KT), ("l2_wk", "l2_WkT", 2 * KT), ("l2_wv", "l2_WoutT", 2 * KT)):
            K["weights_l2"].append(arena_weight(at, name, src, tiles, D))
            at += tiles * D
        K["arena_rest"] = arena[:, 2 * c2:]
        K["weights_l3"] = [arena_weight(0, "l3_fc", "L3_cond_w_fc", KT, 2 * FF)]
        with ExitStack() as l2:
            m2 = Mem(nc, l2)
            K["l2_q"] = m2.sb("l2_q", [P, KT, B])
            with ExitStack() as l1:
                m1 = Mem(nc, l1)
                for name in ("l1a_scale", "l1a_shift", "l1b_scale", "l1b_shift"):
                    K[name] = m1.sb(name, [P, KT, B])
                for c, w in zip("qkvo", ("q", "k", "v", "proj")):
                    K["weights_first"].append(weight(m1, "l1_w" + c, f"L1_cond_{w}_w", KT, D))
                    if c != "o":
                        K[f"l1_w{c}_low"] = m1.rounded_at(f"l1_w{c}_low", [P, KT, D], nc.sbuf_base - 4 * KT * D)
                with ExitStack() as l0:
                    m0 = Mem(nc, l0)
                    for name in ("l0_shift", "l0_scale", "l0_gate", "l0_gate_ff", "l0_scale_ff", "l0_shift_ff"):
                        K[name] = m0.sb(name, [P, KT, B])
                    K["turn_in"], K["turn_out"], K["decay"] = m0.sb("turn_in", [P, 2, S]), m0.sb("turn_out", [P, 2, S]), m0.sb("decay", [P, GT])
                    conditioning(nc, mem, sg, T, K)
                    layer0(nc, mem, sg, T, K)
                layer1(nc, mem, sg, T, K)
            K["weights_l3"] += [weight(m2, "l3_qkv", "L3_cond_w_qkv", KT, 3 * D), weight(m2, "l3_ao", "L3_cond_w_ao", KT, D),
                                weight(m2, "l3_fo", "L3_cond_w_fo", HJ, D)]
            layer2(nc, mem, sg, T, K)
            layer3(nc, mem, sg, T, K)


def kernel(**inputs):
    import concourse.bacc as bacc
    from concourse.bass_utils import run_bass_kernel_spmd

    a = {k: np.asarray(v) for k, v in inputs.items()}
    lay = {}
    lay["x"] = a["x"].reshape(NG, GT, KT, P).transpose(3, 0, 2, 1)
    lay["condT"] = a["cond_1024"].T.reshape(KT, P, B).transpose(1, 0, 2)
    cols, vec_at, at = [], {}, 0
    for name in VECTORS:
        c = a[name].reshape(-1, P).T
        vec_at[name] = at
        at += c.shape[1]
        cols.append(c)
    lay["vectors"] = np.concatenate(cols, 1)
    lam = np.stack([a["L0_cond_Lam_re"], a["L0_cond_Lam_im"], a["L0_cond_log_step"]], 1)
    lay["lam"] = np.concatenate([lam, lam], 0)
    b_re, b_im = a["L0_cond_B_re"].T, a["L0_cond_B_im"].T
    pair = np.stack([np.concatenate([b_re, b_im], 1), np.concatenate([b_im, b_re], 1)])
    lay["s5_b"] = pair.reshape(2, KT, P, P).transpose(2, 0, 1, 3)
    c_re, c_im = a["L0_cond_C_re"].T, a["L0_cond_C_im"].T
    lay["s5_c"] = np.stack([np.concatenate([c_re, c_im], 0), np.concatenate([c_im, c_re], 0)]).transpose(1, 0, 2)
    lay["WselfT_q"] = a["L2_cond_W_self"].T[D:]
    lanes = np.arange(P)
    consts = np.zeros((P, 32 + 3 * P + 2 * S), np.float32)
    consts[:NS, 0], consts[NS:, 0] = -1.0, 1.0
    consts[:, 1:9] = lanes[:, None] // 16 == np.arange(8)
    consts[:, 9:20] = a["L2_cond_w_bias"]
    consts[:, 20] = a["L2_cond_b_bias"]
    consts[:, 32:32 + P] = np.eye(P)
    consts[:, 32 + P:32 + 2 * P] = np.where(lanes[:, None] // S == lanes // S, 0.0, -1e30)
    consts[:, 32 + 2 * P:32 + 3 * P] = np.eye(P)[lanes ^ 1]
    inv_freq = (np.float32(1.0) / np.power(np.float32(10000.0), np.arange(0, 16, 2, dtype=np.float32) / np.float32(16))).astype(np.float32)
    angle = np.arange(S, dtype=np.float32)[None] * inv_freq[lanes % 16 // 2][:, None]
    consts[:, 32 + 3 * P:32 + 3 * P + S] = np.cos(angle)
    consts[:, 32 + 3 * P + S:] = np.sin(angle) * np.where(lanes % 2, 1.0, -1.0)[:, None]
    adj = a["mask_BxSxSx11_ik0"]
    both = np.stack([adj[:, :, :20], adj[:, :20].transpose(0, 2, 1, 3)], 2)
    lay["adj"] = both.reshape(NG, NP, P, -1).transpose(0, 2, 1, 3).reshape(NG, P, -1)
    lay["WselfT_v"] = a["L2_cond_W_self"].T[:D]
    lay["l2_WqT"] = a["L2_cond_Wq"].transpose(0, 2, 1).reshape(2 * D, D)
    lay["l2_WkT"] = a["L2_cond_Wk"].transpose(0, 2, 1).reshape(2 * D, D)
    lay["l2_WoutT"] = a["L2_cond_Wout"].reshape(2, D, D).transpose(0, 2, 1).reshape(2 * D, D)
    lay["consts"] = consts
    for name in ("L0_cond_Wm", "L0_cond_Wc", "L1_cond_film1_w", "L1_cond_film2_w", "L3_cond_w_t1", "L3_cond_w_t2", "L0_cond_W1", "L0_cond_W2",
                 "L1_cond_mlp_w1", "L1_cond_mlp_w2", "L1_cond_q_w", "L1_cond_k_w", "L1_cond_v_w", "L1_cond_proj_w",
                 "L3_cond_w_qkv", "L3_cond_w_ao", "L3_cond_w_fc", "L3_cond_w_fo"):
        lay[name] = a[name]

    nc = bacc.Bacc("TRN2", target_bir_lowering=False, num_devices=1)
    arrays, T = {}, {}
    for name, v in lay.items():
        v = np.ascontiguousarray(v)
        arrays[f"in_{name}"] = v
        T[name] = nc.dram_tensor(f"in_{name}", v.shape, mybir.dt.from_np(v.dtype), kind="ExternalInput").ap()
    T["out"] = nc.dram_tensor("out_x", (P, NG, KT, GT), F32, kind="ExternalOutput").ap()
    program(nc, T, vec_at)
    r = run_bass_kernel_spmd(nc, [arrays], core_ids=[0])
    out = np.asarray(r.results[0]["out_x"])
    return out.transpose(1, 3, 2, 0).reshape(B, S, D)
```
